# Optimizing a Trainium2 kernel written in Bass

```python
import numpy as np
import jax
import jax.numpy as jnp

def _softmax(x, axis=-1):
    return jax.nn.softmax(x, axis=axis)

def _gelu(x):
    return jax.nn.gelu(x, approximate=True)

def _silu(x):
    return jax.nn.silu(x)

def _sigmoid(x):
    return jax.nn.sigmoid(x)

def _layernorm(x, axis=-1, eps=1e-05):
    m = jnp.mean(x, axis=axis, keepdims=True)
    v = jnp.var(x, axis=axis, keepdims=True)
    return (x - m) / jnp.sqrt(v + eps)

def _scatter_add(tgt, idx, src, axis=0):
    return tgt.at[idx].add(src)

def _segment_sum(src, seg, n):
    return jax.ops.segment_sum(src, seg, n)
kernel_name = 'mk_gnn_ffn_d4_gnn_r8_09bcca'

def setup_inputs(seed: int=0):
    np.random.seed(seed)
    _w = jnp.asarray

    def _rec_inputs():
        import jax
        import jax.numpy as jnp
        _gk = jax.random.key(seed)
        x = -6.415e-05 + 1 * jax.random.normal(jax.random.fold_in(_gk, 1), (1250, 1024), jnp.float32)
        src = jax.random.randint(jax.random.fold_in(_gk, 2), (40000,), 0, 1250, jnp.int32)
        dst = jax.random.randint(jax.random.fold_in(_gk, 3), (40000,), 0, 1250, jnp.int32)
        _o = jnp.argsort(dst, stable=True)
        src = src[_o]
        dst = dst[_o]
        return (x, src, dst)
    x, src, dst = _rec_inputs()

    def _L0_gnn_setup():
        import jax, jax.numpy as jnp
        import numpy as np
        N_NODES = 1250
        N_EDGES = 20000
        DIM = 1024
        key = jax.random.key(seed)
        k1, k2, k3 = jax.random.split(key, 3)
        x = jax.random.normal(k1, (N_NODES, DIM), dtype=jnp.float32)
        edge_index = jax.random.randint(k2, (2, N_EDGES), 0, N_NODES, dtype=jnp.int64)
        W = jax.random.normal(k3, (DIM, DIM), dtype=jnp.float32) * (1.0 / np.sqrt(DIM))
        b = jnp.zeros((DIM,), dtype=jnp.float32)
        return {'x': x, 'edge_index': edge_index, 'W': W, 'b': b}
    _L0_gnn_all = _L0_gnn_setup()
    _L0_gnn_in = {k: v for k, v in _L0_gnn_all.items() if k in ('W', 'b')}
    del _L0_gnn_all

    def _L0_ffn_setup():
        import jax, jax.numpy as jnp
        import numpy as np
        BS, L, D = (4, 256, 1024)
        H, E, K = (8, 16, 2)
        HD = D // H
        I = 512 // H
        key = jax.random.key(seed)
        ks = jax.random.split(key, 10)
        s = lambda k, shp, fan: jax.random.normal(k, shp, jnp.float32) / np.sqrt(fan)
        return {'x': jax.random.normal(ks[0], (BS, L, D), jnp.float32), 'Wm': s(ks[1], (D, D), D), 'bm': jnp.zeros((D,), jnp.float32), 'expert_emb': jax.random.normal(ks[2], (HD, E), jnp.float32), 'W1': s(ks[3], (E, HD, I), HD), 'b1': jnp.zeros((E, I), jnp.float32), 'W2': s(ks[4], (E, I, HD), I), 'b2': jnp.zeros((E, HD), jnp.float32), 'Wo': s(ks[5], (D, D), D), 'bo': jnp.zeros((D,), jnp.float32)}
    _L0_ffn_all = _L0_ffn_setup()
    _L0_ffn_in = {k: v for k, v in _L0_ffn_all.items() if k in ('Wm', 'bm', 'expert_emb', 'W1', 'b1', 'W2', 'b2', 'Wo', 'bo')}
    del _L0_ffn_all

    def _L1_gnn_setup():
        import jax, jax.numpy as jnp
        import numpy as np
        NEG_SLOPE = 0.1
        EPS = 1e-05
        key = jax.random.key(seed)
        k1, k2, k3, k4, k5 = jax.random.split(key, 5)
        N, E, DIN, DOUT = (1250, 20000, 1024, 1024)
        x = jax.random.normal(k1, (N, DIN), dtype=jnp.float32)
        W = jax.random.normal(k2, (DIN, DOUT), dtype=jnp.float32) * 0.02
        a = jax.random.normal(k3, (1, 2 * DOUT), dtype=jnp.float32) * 0.02
        src = jax.random.randint(k4, (E,), 0, N, dtype=jnp.int64)
        dst = jax.random.randint(k5, (E,), 0, N, dtype=jnp.int64)
        return {'x': x, 'W': W, 'a': a, 'src': src, 'dst': dst}
    _L1_gnn_all = _L1_gnn_setup()
    _L1_gnn_in = {k: v for k, v in _L1_gnn_all.items() if k in ('W', 'a')}
    del _L1_gnn_all

    def _L1_ffn_setup():
        import jax, jax.numpy as jnp
        import numpy as np
        NUM_EXPERTS = 8
        TOP_K = 2
        key = jax.random.key(seed)
        ks = jax.random.split(key, 4)
        B, S, H, F = (4, 512, 1024, 512)
        x = jax.random.normal(ks[0], (B, S, H), dtype=jnp.float32)
        router_w = jax.random.normal(ks[1], (H, NUM_EXPERTS), dtype=jnp.float32) * 0.02
        w1 = jax.random.normal(ks[2], (H, F), dtype=jnp.float32) * 0.02
        b1 = jnp.zeros((F,), dtype=jnp.float32)
        w2 = jax.random.normal(ks[3], (F, H), dtype=jnp.float32) * 0.02
        b2 = jnp.zeros((H,), dtype=jnp.float32)
        return {'x': x, 'router_w': router_w, 'w1': w1, 'b1': b1, 'w2': w2, 'b2': b2}
    _L1_ffn_all = _L1_ffn_setup()
    _L1_ffn_in = {k: v for k, v in _L1_ffn_all.items() if k in ('router_w', 'w1', 'b1', 'w2', 'b2')}
    del _L1_ffn_all

    def _L2_gnn_setup():
        import jax, jax.numpy as jnp
        import numpy as np
        N = 2500
        E = 40000
        D_IN = 1024
        D_OUT = 1024
        key = jax.random.key(seed)
        k1, k2, k3, k4 = jax.random.split(key, 4)
        x = jax.random.normal(k1, (N, D_IN), dtype=jnp.float32)
        edge_index = jax.random.randint(k2, (2, E), 0, N, dtype=jnp.int64)
        W = jax.random.normal(k3, (D_OUT, D_IN), dtype=jnp.float32) * (1.0 / np.sqrt(D_IN))
        b = jax.random.normal(k4, (D_OUT,), dtype=jnp.float32) * 0.01
        return {'x': x, 'edge_index': edge_index, 'W': W, 'b': b}
    _L2_gnn_all = _L2_gnn_setup()
    _L2_gnn_in = {k: v for k, v in _L2_gnn_all.items() if k in ('W', 'b')}
    del _L2_gnn_all

    def _L2_ffn_setup():
        import jax, jax.numpy as jnp
        import numpy as np

        def _ste(w, w_q):
            return w + jax.lax.stop_gradient(w_q - w)

        def quantize_w8_per(w, axis):
            amax = jnp.clip(jnp.max(jnp.abs(w), axis=axis, keepdims=True), 1e-08, None)
            scale = 127.0 / amax
            w_q = jnp.clip(jnp.round(w * scale), -128.0, 127.0) / scale
            return _ste(w, w_q)

        def quantize_a16(x):
            amax = jnp.clip(jnp.max(jnp.abs(x)), 1e-08, None)
            scale = 32767.0 / amax
            x_q = jnp.clip(jnp.round(x * scale), -32768.0, 32767.0) / scale
            return _ste(x, x_q)
        key = jax.random.key(seed)
        k1, k2, k3 = jax.random.split(key, 3)
        d_model, d_ff = (1024, 512)
        x = jax.random.normal(k1, (4, 256, d_model), dtype=jnp.float32)
        W_in = jax.random.normal(k2, (d_model, d_ff), dtype=jnp.float32) / np.sqrt(d_model)
        b_in = jnp.zeros((d_ff,), dtype=jnp.float32)
        W_out = jax.random.normal(k3, (d_ff, d_model), dtype=jnp.float32) / np.sqrt(d_ff)
        b_out = jnp.zeros((d_model,), dtype=jnp.float32)
        return {'x': x, 'W_in': W_in, 'b_in': b_in, 'W_out': W_out, 'b_out': b_out}
    _L2_ffn_all = _L2_ffn_setup()
    _L2_ffn_in = {k: v for k, v in _L2_ffn_all.items() if k in ('W_in', 'b_in', 'W_out', 'b_out')}
    del _L2_ffn_all

    def _L3_gnn_setup():
        import jax, jax.numpy as jnp
        import numpy as np
        N = 2500
        E = 40000
        IN = 1024
        HID = 256
        H = 4
        D = HID // H
        OUT = 1024
        EPS = 1e-06
        NEG_SLOPE = 0.2
        key = jax.random.key(seed)
        ks = jax.random.split(key, 8)
        x = jax.random.normal(ks[0], (N, IN), dtype=jnp.float32)
        edge_index = jax.random.randint(ks[1], (2, E), 0, N, dtype=jnp.int64)
        s = 0.02
        return {'x': x, 'edge_index': edge_index, 'rms_w': jnp.ones((IN,), dtype=jnp.float32), 'W_down': jax.random.normal(ks[2], (IN, HID), dtype=jnp.float32) * s, 'Wl': jax.random.normal(ks[3], (HID, HID), dtype=jnp.float32) * s, 'Wr': jax.random.normal(ks[4], (HID, HID), dtype=jnp.float32) * s, 'att': jax.random.normal(ks[5], (H, D), dtype=jnp.float32) * s, 'W_up': jax.random.normal(ks[6], (HID, OUT), dtype=jnp.float32) * s}
    _L3_gnn_all = _L3_gnn_setup()
    _L3_gnn_in = {k: v for k, v in _L3_gnn_all.items() if k in ('rms_w', 'W_down', 'Wl', 'Wr', 'att', 'W_up')}
    del _L3_gnn_all

    def _L3_ffn_setup():
        import jax, jax.numpy as jnp
        import numpy as np
        H = 1024
        I = 256
        E = 8
        TOP_K = 2
        NUM_SHARED = 1
        key = jax.random.key(seed)
        ks = jax.random.split(key, 9)
        s = 0.02
        x = jax.random.normal(ks[0], (2, 256, H), dtype=jnp.float32)
        sg_w = jax.random.normal(ks[1], (I, H), dtype=jnp.float32) * s
        su_w = jax.random.normal(ks[2], (I, H), dtype=jnp.float32) * s
        sd_w = jax.random.normal(ks[3], (H, I), dtype=jnp.float32) * s
        router_w = jax.random.normal(ks[4], (E, H), dtype=jnp.float32) * s
        routing_bias = jnp.zeros((E,), dtype=jnp.float32)
        wg = jax.random.normal(ks[5], (E, I, H), dtype=jnp.float32) * s
        wu = jax.random.normal(ks[6], (E, I, H), dtype=jnp.float32) * s
        wd = jax.random.normal(ks[7], (E, H, I), dtype=jnp.float32) * s
        return {'x': x, 'sg_w': sg_w, 'su_w': su_w, 'sd_w': sd_w, 'router_w': router_w, 'routing_bias': routing_bias, 'wg': wg, 'wu': wu, 'wd': wd}
    _L3_ffn_all = _L3_ffn_setup()
    _L3_ffn_in = {k: v for k, v in _L3_ffn_all.items() if k in ('sg_w', 'su_w', 'sd_w', 'router_w', 'routing_bias', 'wg', 'wu', 'wd')}
    del _L3_ffn_all
    return {'x': x, 'src': src, 'dst': dst, 'L0_gnn_W': _L0_gnn_in['W'], 'L0_gnn_b': _L0_gnn_in['b'], 'L0_ffn_Wm': _L0_ffn_in['Wm'], 'L0_ffn_bm': _L0_ffn_in['bm'], 'L0_ffn_expert_emb': _L0_ffn_in['expert_emb'], 'L0_ffn_W1': _L0_ffn_in['W1'], 'L0_ffn_b1': _L0_ffn_in['b1'], 'L0_ffn_W2': _L0_ffn_in['W2'], 'L0_ffn_b2': _L0_ffn_in['b2'], 'L0_ffn_Wo': _L0_ffn_in['Wo'], 'L0_ffn_bo': _L0_ffn_in['bo'], 'L1_gnn_W': _L1_gnn_in['W'], 'L1_gnn_a': _L1_gnn_in['a'], 'L1_ffn_router_w': _L1_ffn_in['router_w'], 'L1_ffn_w1': _L1_ffn_in['w1'], 'L1_ffn_b1': _L1_ffn_in['b1'], 'L1_ffn_w2': _L1_ffn_in['w2'], 'L1_ffn_b2': _L1_ffn_in['b2'], 'L2_gnn_W': _L2_gnn_in['W'], 'L2_gnn_b': _L2_gnn_in['b'], 'L2_ffn_W_in': _L2_ffn_in['W_in'], 'L2_ffn_b_in': _L2_ffn_in['b_in'], 'L2_ffn_W_out': _L2_ffn_in['W_out'], 'L2_ffn_b_out': _L2_ffn_in['b_out'], 'L3_gnn_rms_w': _L3_gnn_in['rms_w'], 'L3_gnn_W_down': _L3_gnn_in['W_down'], 'L3_gnn_Wl': _L3_gnn_in['Wl'], 'L3_gnn_Wr': _L3_gnn_in['Wr'], 'L3_gnn_att': _L3_gnn_in['att'], 'L3_gnn_W_up': _L3_gnn_in['W_up'], 'L3_ffn_sg_w': _L3_ffn_in['sg_w'], 'L3_ffn_su_w': _L3_ffn_in['su_w'], 'L3_ffn_sd_w': _L3_ffn_in['sd_w'], 'L3_ffn_router_w': _L3_ffn_in['router_w'], 'L3_ffn_routing_bias': _L3_ffn_in['routing_bias'], 'L3_ffn_wg': _L3_ffn_in['wg'], 'L3_ffn_wu': _L3_ffn_in['wu'], 'L3_ffn_wd': _L3_ffn_in['wd']}

def reference(x, src, dst, L0_gnn_W, L0_gnn_b, L0_ffn_Wm, L0_ffn_bm, L0_ffn_expert_emb, L0_ffn_W1, L0_ffn_b1, L0_ffn_W2, L0_ffn_b2, L0_ffn_Wo, L0_ffn_bo, L1_gnn_W, L1_gnn_a, L1_ffn_router_w, L1_ffn_w1, L1_ffn_b1, L1_ffn_w2, L1_ffn_b2, L2_gnn_W, L2_gnn_b, L2_ffn_W_in, L2_ffn_b_in, L2_ffn_W_out, L2_ffn_b_out, L3_gnn_rms_w, L3_gnn_W_down, L3_gnn_Wl, L3_gnn_Wr, L3_gnn_att, L3_gnn_W_up, L3_ffn_sg_w, L3_ffn_su_w, L3_ffn_sd_w, L3_ffn_router_w, L3_ffn_routing_bias, L3_ffn_wg, L3_ffn_wu, L3_ffn_wd):
    import jax
    import jax.numpy as jnp

    def _L0_gnn_ref(x, edge_index, W, b):
        import jax, jax.numpy as jnp
        import numpy as np
        N_NODES = 1250
        N_EDGES = 20000
        DIM = 1024
        'GCNConv (add_self_loops=True, symmetric norm) -> Dropout(eval=identity) -> ReLU.'
        n = x.shape[0]
        loops = jnp.arange(n, dtype=edge_index.dtype)
        src = jnp.concatenate([edge_index[0], loops])
        dst = jnp.concatenate([edge_index[1], loops])
        deg = jax.ops.segment_sum(jnp.ones_like(dst, dtype=x.dtype), dst, num_segments=n)
        dinv = jnp.where(deg > 0, jax.lax.rsqrt(deg), jnp.zeros_like(deg))
        norm = dinv[src] * dinv[dst]
        h = x @ W
        msg = h[src] * norm[:, None]
        out = jax.ops.segment_sum(msg, dst, num_segments=n) + b
        return jax.nn.relu(out)

    def _L0_ffn_ref(x, Wm, bm, expert_emb, W1, b1, W2, b2, Wo, bo):
        import jax, jax.numpy as jnp
        import numpy as np
        BS, L, D = (4, 256, 1024)
        H, E, K = (8, 16, 2)
        HD = D // H
        I = 512 // H
        bs, L_, d = x.shape
        h = x @ Wm + bm
        t = h.reshape(bs * L_ * H, HD)
        logits = t @ expert_emb
        w = jax.nn.softmax(logits, axis=-1)
        topw, topi = jax.lax.top_k(w, K)
        hmid = jax.nn.gelu(jnp.einsum('td,edi->tei', t, W1) + b1, approximate=False)
        eo = jnp.einsum('tei,eio->teo', hmid, W2) + b2
        sel = jnp.take_along_axis(eo, topi[:, :, None], axis=1)
        comb = (sel * topw[:, :, None]).sum(axis=1)
        out = comb.reshape(bs, L_, d)
        return out @ Wo + bo

    def _L1_gnn_ref(x, W, a, src, dst):
        import jax, jax.numpy as jnp
        import numpy as np
        NEG_SLOPE = 0.1
        EPS = 1e-05
        N = x.shape[0]
        d = W.shape[1]
        h = x @ W
        a_l, a_r = (a[0, :d], a[0, d:])
        al = h @ a_l
        ar = h @ a_r
        e = jnp.exp(-jax.nn.leaky_relu(al[src] + ar[dst], negative_slope=NEG_SLOPE))
        rowsum = jax.ops.segment_sum(e, src, num_segments=N)
        h_prime = jax.ops.segment_sum(e[:, None] * h[dst], src, num_segments=N)
        h_prime = h_prime / (rowsum[:, None] + EPS)
        return jax.nn.elu(h_prime)

    def _L1_ffn_ref(x, router_w, w1, b1, w2, b2):
        import jax, jax.numpy as jnp
        import numpy as np
        NUM_EXPERTS = 8
        TOP_K = 2
        B, S, H = x.shape
        xt = x.reshape(-1, H)
        router_logits = jnp.matmul(xt, router_w)
        router_probs = jax.nn.softmax(router_logits, axis=-1)
        top_k_probs, top_k_indices = jax.lax.top_k(router_probs, TOP_K)
        top_k_probs = top_k_probs / jnp.sum(top_k_probs, axis=-1, keepdims=True)
        one_hot = jax.nn.one_hot(top_k_indices, NUM_EXPERTS, dtype=xt.dtype)
        combine = jnp.einsum('tk,tke->te', top_k_probs, one_hot)
        expert_out = jnp.matmul(jax.nn.gelu(jnp.matmul(xt, w1) + b1), w2) + b2
        out = expert_out * jnp.sum(combine, axis=-1, keepdims=True)
        return out.reshape(B, S, H)

    def _L2_gnn_ref(x, edge_index, W, b):
        import jax, jax.numpy as jnp
        import numpy as np
        N = 2500
        E = 40000
        D_IN = 1024
        D_OUT = 1024
        num_nodes = x.shape[0]
        self_idx = jnp.arange(num_nodes, dtype=edge_index.dtype)
        ei = jnp.concatenate([edge_index, jnp.stack([self_idx, self_idx], axis=0)], axis=1)
        row, col = (ei[0], ei[1])
        h = jnp.einsum('nd,od->no', x, W) + b
        deg = jnp.zeros((num_nodes,), dtype=h.dtype).at[row].add(1.0)
        deg_inv_sqrt = deg ** (-0.5)
        norm = deg_inv_sqrt[row] * deg_inv_sqrt[col]
        msg = norm[:, None] * h[col]
        out = jax.ops.segment_sum(msg, row, num_segments=num_nodes)
        return out

    def _L2_ffn_ref(x, W_in, b_in, W_out, b_out):
        import jax, jax.numpy as jnp
        import numpy as np

        def _ste(w, w_q):
            return w + jax.lax.stop_gradient(w_q - w)

        def quantize_w8_per(w, axis):
            amax = jnp.clip(jnp.max(jnp.abs(w), axis=axis, keepdims=True), 1e-08, None)
            scale = 127.0 / amax
            w_q = jnp.clip(jnp.round(w * scale), -128.0, 127.0) / scale
            return _ste(w, w_q)

        def quantize_a16(x):
            amax = jnp.clip(jnp.max(jnp.abs(x)), 1e-08, None)
            scale = 32767.0 / amax
            x_q = jnp.clip(jnp.round(x * scale), -32768.0, 32767.0) / scale
            return _ste(x, x_q)
        W_in_sim = quantize_w8_per(W_in, axis=0)
        W_out_sim = quantize_w8_per(W_out, axis=1)
        x_sim = quantize_a16(x)
        hidden = jax.nn.gelu(x_sim @ W_in_sim + b_in, approximate=False)
        hidden_sim = quantize_a16(hidden)
        out = hidden_sim @ W_out_sim + b_out
        return out

    def _L3_gnn_ref(x, edge_index, rms_w, W_down, Wl, Wr, att, W_up):
        import jax, jax.numpy as jnp
        import numpy as np
        N = 2500
        E = 40000
        IN = 1024
        HID = 256
        H = 4
        D = HID // H
        OUT = 1024
        EPS = 1e-06
        NEG_SLOPE = 0.2
        n = x.shape[0]
        ms = jnp.mean(jnp.square(x), axis=-1, keepdims=True)
        x = x * jax.lax.rsqrt(ms + EPS) * rms_w
        x = x @ W_down
        loop = jnp.arange(n, dtype=edge_index.dtype)
        src = jnp.concatenate([edge_index[0], loop])
        dst = jnp.concatenate([edge_index[1], loop])
        xl = (x @ Wl).reshape(n, H, D)
        xr = (x @ Wr).reshape(n, H, D)
        msg = xl[src] + xr[dst]
        act = jnp.where(msg > 0, msg, NEG_SLOPE * msg)
        e = jnp.einsum('ehd,hd->eh', act, att)
        m = jax.ops.segment_max(e, dst, num_segments=n)
        p = jnp.exp(e - m[dst])
        denom = jax.ops.segment_sum(p, dst, num_segments=n)
        alpha = p / (denom[dst] + 1e-16)
        out = jax.ops.segment_sum(alpha[..., None] * xl[src], dst, num_segments=n)
        out = out.reshape(n, HID)
        return out @ W_up

    def _L3_ffn_ref(x, sg_w, su_w, sd_w, router_w, routing_bias, wg, wu, wd):
        import jax, jax.numpy as jnp
        import numpy as np
        H = 1024
        I = 256
        E = 8
        TOP_K = 2
        NUM_SHARED = 1
        orig_shape = x.shape
        xt = x.reshape(-1, H)
        T = xt.shape[0]
        shared = jax.nn.silu(xt @ sg_w.T) * (xt @ su_w.T) @ sd_w.T
        shared = shared / NUM_SHARED
        logits = xt @ router_w.T + routing_bias
        probs = jax.nn.sigmoid(logits)
        topk_p, topk_idx = jax.lax.top_k(probs, TOP_K)
        topk_p = topk_p / jnp.sum(topk_p, axis=-1, keepdims=True)
        w = jnp.zeros((T, E), dtype=xt.dtype)
        w = w.at[jnp.arange(T)[:, None], topk_idx].add(topk_p)
        g = jnp.einsum('th,eih->tei', xt, wg)
        u = jnp.einsum('th,eih->tei', xt, wu)
        h = jax.nn.silu(g) * u
        y = jnp.einsum('tei,ehi->teh', h, wd)
        routed = jnp.einsum('te,teh->th', w, y)
        return (shared + routed).reshape(orig_shape)
    edge_index = jnp.stack([src, dst])
    x = x + _L0_gnn_ref(_layernorm(x, axis=-1), edge_index, L0_gnn_W, L0_gnn_b)
    x = x + _L0_ffn_ref(_layernorm(x, axis=-1)[None], L0_ffn_Wm, L0_ffn_bm, L0_ffn_expert_emb, L0_ffn_W1, L0_ffn_b1, L0_ffn_W2, L0_ffn_b2, L0_ffn_Wo, L0_ffn_bo)[0]
    x = x + _L1_gnn_ref(_layernorm(x, axis=-1), L1_gnn_W, L1_gnn_a, src, dst)
    x = x + _L1_ffn_ref(_layernorm(x, axis=-1)[None], L1_ffn_router_w, L1_ffn_w1, L1_ffn_b1, L1_ffn_w2, L1_ffn_b2)[0]
    x = x + _L2_gnn_ref(_layernorm(x, axis=-1), edge_index, L2_gnn_W, L2_gnn_b)
    x = x + _L2_ffn_ref(_layernorm(x, axis=-1)[None], L2_ffn_W_in, L2_ffn_b_in, L2_ffn_W_out, L2_ffn_b_out)[0]
    x = x + _L3_gnn_ref(_layernorm(x, axis=-1), edge_index, L3_gnn_rms_w, L3_gnn_W_down, L3_gnn_Wl, L3_gnn_Wr, L3_gnn_att, L3_gnn_W_up)
    x = x + _L3_ffn_ref(_layernorm(x, axis=-1)[None], L3_ffn_sg_w, L3_ffn_su_w, L3_ffn_sd_w, L3_ffn_router_w, L3_ffn_routing_bias, L3_ffn_wg, L3_ffn_wu, L3_ffn_wd)[0]
    return x

_drawn_inputs = setup_inputs


def setup_inputs(seed=0):
    import zlib

    import numpy as np

    out = dict(_drawn_inputs(seed))
    spreads = {'L0_gnn_b': (0.0, 0.1),
     'L0_ffn_bm': (0.0, 0.1),
     'L0_ffn_b1': (0.0, 0.1),
     'L0_ffn_b2': (0.0, 0.1),
     'L0_ffn_bo': (0.0, 0.1),
     'L1_ffn_b1': (0.0, 0.281),
     'L1_ffn_b2': (0.0, 0.1),
     'L2_ffn_b_in': (0.0, 0.1),
     'L2_ffn_b_out': (0.0, 0.1),
     'L3_gnn_rms_w': (1.0, 0.6),
     'L3_ffn_routing_bias': (0.0, 0.54)}
    factors = {'L1_ffn_router_w': 8.0,
     'L2_gnn_b': 6.755,
     'L3_gnn_W_down': 3.347,
     'L3_gnn_Wl': 3.176,
     'L3_gnn_Wr': 8.0,
     'L3_gnn_att': 8.0,
     'L3_gnn_W_up': 3.301}
    for name, (base, spread) in spreads.items():
        noise = np.random.default_rng([zlib.crc32(name.encode()), seed]).standard_normal(out[name].shape)
        drawn = base * np.exp(spread * noise) if base else spread * noise
        out[name] = jnp.asarray(drawn.astype(out[name].dtype))
    for name, factor in factors.items():
        out[name] = (out[name] * factor).astype(out[name].dtype)
    return out
```

```python
from contextlib import ExitStack

import concourse.bass as bass
from concourse import mybir

F32 = mybir.dt.float32
F16 = mybir.dt.float16
BF16 = mybir.dt.bfloat16
U16 = mybir.dt.uint16
I32 = mybir.dt.int32
ALU = mybir.AluOpType
ACT = mybir.ActivationFunctionType
AX_X = mybir.AxisListType.X
RMAX = bass.bass_isa.ReduceOp.max

P = 128
SIZE = {F32: 4, I32: 4, F16: 2, BF16: 2, U16: 2}

NODES = 1250
F = 512
DIM = 1024
E3 = 8
HID = 256
EDGES = 40000
T = -(-NODES // P)
NP = T * P
K = DIM // P
LAST = NODES - (T - 1) * P
EP = 125
ET = EDGES // EP
CHUNK = 4
NC = ET // CHUNK
HALF = 512
THIRD = [(0, 427), (427, 427), (854, 426)]
LN_EPS = 1e-5
RMS_EPS = 1e-6
BIG = 3.0e38
ROUND = 1.5 * 2.0 ** 23


def ds(i, n=1):
    return bass.ds(i, n)


def wait(e, sem, value):
    if isinstance(value, int) and value <= 0:
        return
    e.wait_ge(sem, value)


def pairs(e, n, body, first=2, last=0):
    for i in range(first):
        body(i, i % 2)
    if n - last > first:
        with e.Fori(first // 2, (n - last) // 2) as h:
            for j in range(2):
                body(h * 2 + j, j)
    for i in range(n - last, n):
        body(i, i % 2)


def singles(e, n, body, first=1, last=0):
    for i in range(first):
        body(i)
    if n - last > first:
        with e.Fori(first, n - last) as i:
            body(i)
    for i in range(n - last, n):
        body(i)


def program(nc, A, out):
    xl_table = nc.dram_tensor("xl_table", (NP, HID), F32).ap()
    ctx = ExitStack()
    with ctx:
        def sb(name, shape, dt):
            return ctx.enter_context(nc.sbuf_tensor(name, shape, dt))

        def sem(name):
            return ctx.enter_context(nc.semaphore(name))

        def view(region, start, shape, dt):
            n = 1
            for s in shape:
                n *= s
            words = -(-n * SIZE[dt] // 4)
            ap = region[:, start // 4:start // 4 + words]
            if dt is not F32:
                ap = ap.bitcast(dt)[:, 0:n]
            if len(shape) == 2:
                ap = ap.rearrange("p (a b) -> p a b", a=shape[0])
            return ap

        x = sb("x", [P, T, DIM], F32)
        adj = sb("adj", [P, T, NP], U16)
        turned = sb("turned", [P, K * NP], F32)
        hidden = sb("hidden", [P, T * DIM], F32)
        weights = sb("weights", [P, K * DIM], F32)
        stage = sb("stage", [P, 2, HALF], F32)
        coef = sb("coef", [P, 2 * NP], F32)
        xhat = sb("xhat", [P, DIM], F32)
        work = sb("work", [P, NP], F32)
        bias = sb("bias", [P, NP], F32)
        cols = sb("cols", [P, 3 * K + 4], F32)

        xT_h = view(turned, 0, [K, NP], F16)
        xT_l = view(turned, K * NP * 2, [K, NP], BF16)
        h_h = view(hidden, 0, [T, DIM], F16)
        h_l = view(hidden, T * DIM * 2, [T, DIM], BF16)
        w_h = view(weights, 0, [K, DIM], F16)
        w_l = view(weights, K * DIM * 2, [K, DIM], BF16)
        coef_h = [view(coef, b * NP * 4, [T, P], F16) for b in range(2)]
        coef_l = [view(coef, b * NP * 4 + NP * 2, [T, P], BF16) for b in range(2)]
        row_h = view(work, 0, [NP], F16)
        row_l = view(work, NP * 2, [NP], BF16)
        z = view(work, 0, [T, P], F32)
        hT_h = view(hidden, 0, [K, NP], F16)
        hT_l = view(hidden, K * NP * 2, [K, NP], BF16)
        fT = (view(hidden, 0, [F // P, NP], F16), view(hidden, F // P * NP * 2, [F // P, NP], BF16))
        half_a = (view(weights, 0, [K, F], F16), view(weights, K * DIM * 2, [K, F], BF16))
        half_b = (view(weights, K * F * 2, [F // P, DIM], F16), view(weights, K * DIM * 2 + K * F * 2, [F // P, DIM], BF16))
        w1 = (view(coef, 0, [DIM], F16), view(coef, 2048, [DIM], BF16))
        w2 = (view(coef, 4096, [K, P], F16), view(coef, 6144, [K, P], BF16))
        b2_f = view(coef, 8192, [P], F32)
        b2 = (view(coef, 8704, [P], F16), view(coef, 8960, [P], BF16))
        emb_f = view(coef, 9216, [16], F32)
        emb = (view(coef, 9280, [16], F16), view(coef, 9312, [16], BF16))
        pick = view(xhat, 0, [K, P], F16)
        N3 = THIRD[0][1]
        hid = [(view(turned, b * K * N3 * 4, [K, N3], F16), view(turned, b * K * N3 * 4 + K * N3 * 2, [K, N3], BF16))
               for b in range(2)]
        at = 2 * K * N3 * 4
        gm = [(view(turned, at + b * 1712, [N3], F16), view(turned, at + b * 1712 + 856, [N3], BF16)) for b in range(3)]
        gT = (view(turned, 7 * NP * 4, [NP], F16), view(turned, 7 * NP * 4 + NP * 2, [NP], BF16))
        up_buf = [view(work, a * 4, [n], F32) for a, n in THIRD]
        unit = [view(work, b * 1712, [N3], F32) for b in range(2)]
        GROUPS = T * K
        lg = view(work, 0, [GROUPS, 16], F32)
        gates_g = view(turned, 0, [GROUPS, 16], F32)
        gates = view(turned, 0, [T, P], F32)
        t_c = view(turned, 5120, [GROUPS, 16], F32)
        t_o = view(turned, 10240, [GROUPS, 16], F32)
        t_m = view(turned, 15360, [GROUPS, 16], F32)
        g_m = view(turned, 20480, [GROUPS], F32)
        g_z = view(turned, 20800, [GROUPS], F32)
        g_c = view(turned, 21120, [GROUPS], F32)
        spare = view(coef, 0, [DIM], F32)
        router_f = view(coef, 0, [K, 8], F32)
        router = (view(coef, 256, [K, 8], F16), view(coef, 384, [K, 8], BF16))
        r_l = view(coef, 512, [T, 8], F32)
        r_e = view(coef, 832, [T, 8], F32)
        r_o = view(coef, 1152, [T, 8], F32)

        edge_i = view(hidden, 0, [2, ET], I32)
        edge_f = view(hidden, 2560, [2, ET], F32)
        span_i = view(hidden, 5120, [EDGES // NC], I32)
        span_f = view(hidden, 7120, [EDGES // NC], F32)
        src_row = view(hidden, 9120, [NP], F16)
        dst_row = view(hidden, 11680, [P], F16)
        src_hot = [view(hidden, 12288 + b * 5120, [2, NP], F16) for b in range(2)]
        dst_hot = [view(hidden, 22528 + b * 512, [2, P], F16) for b in range(2)]
        nothing = view(hidden, 23552, [HALF], F16)

        ident = sb("ident", [P, P], F32)
        ident16 = sb("ident16", [P, P], F16)
        identb = sb("identb", [P, P], BF16)
        ones = sb("ones", [P, P], F32)
        tiny = sb("tiny", [P, 312], F32)
        used = [0]

        def small(shape, dt):
            n = 1
            for s in shape:
                n *= s
            begin = used[0]
            used[0] += -(-n * SIZE[dt] // 4)
            assert used[0] <= 312
            return view(tiny, begin * 4, shape, dt)

        one16 = small([2], F16)
        win_lo = small([T], F32)
        win_neg = small([T], F32)
        chunk_no = small([1], F32)
        span = small([2], F32)
        hit = small([2 * T], F32)
        hit_all = small([2 * T], F32)
        bounds = small([2 * T], I32)
        deg3 = small([T, 3], F32)
        deg_in = small([T], F32)
        deg_out = small([T], F32)
        deg_part = small([2, T], F32)
        dinv_in = small([T], F32)
        dinv_out = small([T], F32)
        bn = small([2, 6], F32)
        mv = small([2], F32)
        std = small([1], F32)
        rstd = small([1], F32)
        rank = small([16], F32)
        part_i = small([3], I32)
        part_f = small([2], F32)
        eight = small([K], F32)
        head_mask = small([K], F32)
        al = small([T], F32)
        ar = small([T], F32)
        low2 = small([2], F32)
        low2_all = small([2], F32)
        shift = small([3], F32)
        r_s = small([3, T], F32)
        spacer = small([3], F32)
        eps = small([2], F32)

        used_late = [0]

        def late(shape, dt):
            n = 1
            for s in shape:
                n *= s
            begin = used_late[0]
            used_late[0] += -(-n * SIZE[dt] // 4)
            assert used_late[0] <= NP - DIM
            return view(bias, (DIM + begin) * 4, shape, dt)

        w_max = late([16], F32)
        w_amax = late([8], F32)
        w_quant = late([8], F32)
        w_step = late([8], F32)
        magic = late([1], F32)
        x_max = late([2], F32)
        x_max_all = late([1], F32)
        x_quant = late([1], F32)
        x_step = late([1], F32)
        up_scale = late([F // P], F32)
        h_max = late([3 * F // P], F32)
        h_max1 = late([1], F32)
        h_max_all = late([1], F32)
        h_quant = late([1], F32)
        h_scale = late([F // P], F32)
        w_row = view(work, F * 4, [F], F32)
        w_diag = view(work, 0, [F // P, P], F32)
        xT_f = view(turned, 0, [K, NP], F32)
        hid_f = view(turned, 0, [F // P, NP], F32)

        down = (view(weights, 16384, [K, HID], F16), view(weights, 20480, [K, HID], BF16))
        wlr = (view(weights, 24576, [2, 2 * HID], F16), view(weights, 26624, [2, 2 * HID], BF16))
        w_upp = (view(weights, 0, [2, DIM], F16), view(weights, 4096, [2, DIM], BF16))
        xdT = (view(hidden, 0, [2, NP], F16), view(hidden, 5120, [2, NP], BF16))
        lr = view(hidden, 10240, [T, 2 * HID], F32)
        xr_h = view(hidden, 30720, [T, HID], F16)
        xr_l = view(hidden, 35840, [T, HID], BF16)
        aggT = xdT
        adj_words = adj[:, :, :].rearrange("p a b -> p (a b)").bitcast(F32)
        region = {"turned": (turned, 0, K * NP * 4), "adj": (adj, 0, T * NP * 2)}

        def area(which, shape, dt):
            base, begin, end = region[which]
            n = 1
            for s in shape:
                n *= s
            region[which] = (base, begin + -(-n * SIZE[dt] // 4) * 4, end)
            assert region[which][1] <= end
            if which == "adj":
                base = adj_words
            return view(base, begin, shape, dt)
        xl_got = [area("turned", [2, HID], F32) for b in range(2)]
        z3 = [area("turned", [2, HID + 4], F32) for b in range(2)]
        run_max = area("turned", [4, 4 * P], F32)
        away = [area("turned", [2, P], F32) for b in range(2)]
        to_dst = [area("turned", [2, P], F16) for b in range(2)]
        by_dst = [area("turned", [2 * EP], F16) for b in range(2)]
        dst_in = [area("turned", [2 * EP], I32) for b in range(2)]
        wx_h = [area("turned", [2, HID + 4], F16) for b in range(2)]
        wx_l = [area("turned", [2, HID + 4], BF16) for b in range(2)]
        self_z = view(turned, 0, [T, HID], F32)
        dst_no = area("adj", [P], F32)
        none16 = area("adj", [HID + 4], F16)
        e_all = area("adj", [ET, 4], F32)
        src_i = area("adj", [ET], I32)
        dst_i = area("adj", [ET], I32)
        dst_f = area("adj", [ET], F32)
        sums = area("adj", [T, HID], F32)
        e_now = [area("adj", [2, 4], F32) for b in range(2)]
        s_now = [area("adj", [2, 4], F32) for b in range(2)]
        idx_now = [area("adj", [2], I32) for b in range(2)]
        e_self = area("adj", [T, 4], F32)
        part_no = area("adj", [1], F32)
        m_now = area("adj", [4], F32)
        m_h = area("adj", [5], F16)
        m_l = area("adj", [5], BF16)
        p_self = area("adj", [4], F32)
        den = area("adj", [4], F32)
        own = area("adj", [HID], F32)
        att = bias[:, 0:HID]

        gu = [(view(r, 0, [K, 2 * HID], F16), view(r, 8192, [K, 2 * HID], BF16)) for r in (weights, adj_words)]
        dn = [(view(r, 16384, [2, DIM], F16), view(r, 20480, [2, DIM], BF16)) for r in (weights, adj_words)]
        h3 = [(view(hidden, 10240 * (b + 1), [2, NP], F16), view(hidden, 10240 * (b + 1) + 5120, [2, NP], BF16)) for b in range(2)]
        route_bias = late([8], F32)
        gates3 = late([T, E3 + 1], F32)

        bank = ctx.enter_context(nc.psum_tensor("bank", [P, 8, HALF], F32))
        ps_out = [bank[:, 2 * b:2 * b + 2, :].rearrange("p a b -> p (a b)") for b in range(2)]
        ps_turn = bank[:, 4:6, :].rearrange("p a (b c) -> p (a b) c", c=P)

        s_x = sem("x_loaded")
        s_pad = sem("pad_cleared")
        s_edges = sem("edges_loaded")
        s_const = sem("constants_made")
        s_pool = sem("pool_step")
        s_v = sem("vector_step")
        s_span = sem("hits_known")
        s_hits = sem("hits_spread")
        s_bounds = sem("bounds_known")
        s_hot = sem("onehots_made")
        s_hot_free = sem("onehots_free")
        s_adj = sem("adj_window_summed")
        s_adj_free = sem("adj_window_stored")
        s_deg = sem("degrees_known")
        s_sq = sem("degree_roots")
        s_dinv = sem("degree_factors")
        s_out = sem("product_ready")
        s_out_free = sem("product_free")
        s_hh = sem("high_part_kept")
        s_h = sem("values_split")
        s_upd = sem("residual_updated")
        s_bn = sem("stats_done")
        s_mv = sem("moments_done")
        s_std = sem("std_done")
        s_rstd = sem("rstd_done")
        s_xhat = sem("xhat_done")
        s_turned = sem("tile_turned")
        s_turn_h = sem("turned_high_kept")
        s_turn = sem("turned_split")
        s_stage = [sem(f"stage{b}_loaded") for b in range(2)]
        s_wh = sem("weight_high_kept")
        s_w = sem("weight_split")
        s_row_h = sem("row_high_kept")
        s_row_l = sem("row_low_made")
        s_row = sem("row_split")
        s_cnt = sem("outs_counted")
        s_sum = sem("sum_scaled")
        s_rowt = sem("row_turned")
        s_coef_h = sem("coef_high_kept")
        s_coef = sem("coef_ready")
        s_bias = sem("bias_loaded")
        s_cols = sem("columns_loaded")
        s_small = sem("small_weights_loaded")
        s_up = sem("up_unit_ready")
        s_up_free = sem("up_unit_free")
        s_up_h = sem("up_high_kept")
        s_emb = sem("embedding_split")
        s_b2 = sem("b2_split")
        s_logit = sem("logits_ready")
        s_lg = sem("logits_shifted")
        s_ex = sem("logits_exponentiated")
        s_gate = sem("gates_ready")
        s_gate_t = sem("gates_turned")
        s_gth = sem("turned_gates_high_kept")
        s_gt = sem("turned_gates_split")
        s_gm = sem("head_gates_masked")
        s_unit = sem("expert_unit_ready")
        s_gelu = sem("expert_gelu_done")
        s_spread = sem("gate_spread_ready")
        s_gated = sem("expert_gated")
        s_hid_h = sem("expert_high_kept")
        s_hid = sem("expert_hidden_split")
        s_comb_mm = sem("expert_sum_ready")
        s_comb_h = sem("expert_sum_high_kept")
        s_comb = sem("expert_sum_split")
        s_diag = sem("al_on_diagonals")
        s_al_row = sem("al_row_ready")
        s_al = sem("al_row_kept")
        s_mins = sem("score_minima")
        s_mins_all = sem("score_minima_spread")
        s_shift = sem("shift_known")
        s_epsr = sem("eps_scaled")
        s_z = sem("scores_leaky")
        s_ez = sem("scores_exponentiated")
        s_cz = sem("scores_counted")
        s_zs = sem("scores_added")
        s_step1 = sem("layer1_update_step")
        s_neg = sem("negative_part_ready")
        s_eneg = sem("negative_part_exponentiated")
        s_g1 = sem("gelu_done")
        s_hid_l = sem("hidden_split")
        s_router1 = sem("router_split")
        s_wmax = sem("weight_maxima")
        s_wscale = sem("weight_scales")
        s_wq = sem("weight_quantise_step")
        s_row2 = sem("scale_row_ready")
        s_row2k = sem("scale_row_kept")
        s_low2 = sem("count_low_made")
        s_xm = sem("x_maximum_step")
        s_max1 = sem("x_maximum")
        s_max1_all = sem("x_maximum_spread")
        s_q = sem("x_scaled")
        s_q_h = sem("x_high_kept")
        s_q_l = sem("x_quantised")
        s_g2 = sem("gelu2_done")
        s_max2 = sem("hidden_maximum")
        s_max2_all = sem("hidden_maximum_spread")
        s_hq = sem("hidden_scaled")
        s_hq_h = sem("hidden_high_kept")
        s_hq_l = sem("hidden_quantised")
        s_rms = sem("rms_weight_multiplied")
        s_idx = sem("edges_reloaded")
        s_aux = sem("layer3_constants")
        s_lr = sem("xl_xr_kept")
        s_xrh = sem("xr_high_kept")
        s_xr = sem("xr_split")
        s_table = sem("xl_table_stored")
        s_row_in = [sem(f"dst_row{b}_loaded") for b in range(2)]
        s_dt = sem("dst_onehots_made")
        s_pick = sem("dst_values_picked")
        s_idx_now = sem("indices_copied")
        s_got = [sem(f"xl_rows{b}_gathered") for b in range(2)]
        s_got_free = sem("xl_rows_free")
        s_score = sem("score_step")
        s_win = sem("window_step")
        s_acct = sem("maxima_turned")
        s_mk = sem("window_maxima_split")
        s_selfp = sem("self_weight_ready")
        s_sub = sem("score_masked")
        s_s = sem("score_shifted")
        s_p = sem("weight_exponentiated")
        s_ph = sem("weighted_high_kept")
        s_pl = sem("weighted_split")
        s_scat = sem("half_scattered")
        s_agg = sem("window_summed")
        s_aggt = sem("sums_turned")
        s_aggh = sem("sums_high_kept")
        s_aggl = sem("sums_split")
        s_gates3 = sem("gates3_ready")
        s_gu = sem("gate_up_ready")
        s_silu = sem("silu_done")
        s_h3 = sem("hidden3_made")
        s_h3h = sem("hidden3_high_kept")
        s_h3l = sem("hidden3_split")
        s_met = sem("waits_met")
        s_store = sem("x_stored")

        LOADS = [
            ("L0_gnn_W", A["L0_gnn_W"], w_h, w_l, K, DIM, []),
            ("L0_ffn_Wm", A["L0_ffn_Wm"], w_h, w_l, K, DIM, [(s_out, T)]),
            ("L0_ffn_W1", A["L0_ffn_W1"], w1[0].rearrange("p (a n) -> p a n", a=1), w1[1].rearrange("p (a n) -> p a n", a=1),
             1, DIM, [(s_out, 2 * T), (s_cnt, 3 * T)]),
            ("L0_ffn_W2", A["L0_ffn_W2"], w2[0], w2[1], K, P, []),
            ("L0_ffn_Wo", A["L0_ffn_Wo"], w_h, w_l, K, DIM, [(s_up, 3 * K)]),
            ("L1_gnn_W", A["L1_gnn_W"], w_h, w_l, K, DIM, [(s_out, 3 * T)]),
            ("L1_ffn_w1", A["L1_ffn_w1"], half_a[0], half_a[1], K, F, [(s_out, 4 * T)]),
            ("L1_ffn_w2", A["L1_ffn_w2"], half_b[0], half_b[1], F // P, DIM, []),
            ("maxima_in", A["L2_ffn_W_inT"], w_max[:, 0:8], "max", F // P, DIM, [(s_upd, 3 * T)]),
            ("maxima_out", A["L2_ffn_W_out"], w_max[:, 8:16], "max", F // P, DIM, []),
            ("L2_gnn_W_a", A["L2_gnn_WT"][0:HALF, :], w_h[:, 0:K // 2, :], w_l[:, 0:K // 2, :], K // 2, DIM, [(s_up, 3 * K + 3 * F // P)]),
            ("L2_gnn_W_b", A["L2_gnn_WT"][HALF:DIM, :], w_h[:, K // 2:K, :], w_l[:, K // 2:K, :], K // 2, DIM, [(s_out, 6 * T)]),
            ("L2_ffn_W_in", A["L2_ffn_W_in"], half_a[0], "row", K, F, [(s_out, 7 * T), (s_row2k, 1)]),
            ("L2_ffn_W_out", A["L2_ffn_W_out"], half_b[0], "col", F // P, DIM, []),
            ("L3_gnn_W_down", A["L3_gnn_W_down"], down[0], down[1], K, HID, [(s_cols, 80)]),
            ("L3_gnn_Wl", A["L3_gnn_Wl"], wlr[0][:, :, 0:HID], wlr[1][:, :, 0:HID], 2, HID, []),
            ("L3_gnn_Wr", A["L3_gnn_Wr"], wlr[0][:, :, HID:2 * HID], wlr[1][:, :, HID:2 * HID], 2, HID, []),
            ("L3_gnn_W_up", A["L3_gnn_W_up"], w_upp[0], w_upp[1], 2, DIM, [(s_up, 3 * K + 6 * F // P)]),
        ]
        PARTS = {}
        n = 0
        for name, _, _, _, blocks, columns, _ in LOADS:
            n += blocks * max(1, columns // HALF)
            PARTS[name] = n

        SPLIT = n - sum(l[4] * max(1, l[5] // HALF) for l in LOADS if isinstance(l[3], str))

        def load_weights(e, store, first, end):
            names = [load[0] for load in LOADS]
            begin = names.index(first)
            n = PARTS[names[begin - 1]] if begin else 0
            if store:
                wait(e, s_w, n)
            for name, dram, high, low, blocks, columns, free in LOADS[begin:names.index(end) if end else None]:
                if store:
                    for what, value in free:
                        e.wait_ge(what, value)
                src = dram.rearrange("(k p) n -> p k n", p=P)
                width = min(columns, HALF)
                per = columns // width

                skipped = n - sum(l[4] * max(1, l[5] // HALF) for l in LOADS[:names.index(name)] if isinstance(l[3], str))

                def body(h, name=name, n=n, skipped=skipped, high=high, low=low, src=src, width=width, per=per):
                    for b in range(2):
                        k, c = (h, b * width) if per == 2 else (h * 2 + b, 0)
                        m = n + h * 2 + b
                        part = (slice(None), ds(k, 1), slice(c, c + width))
                        flat = stage[:, b, 0:width]
                        if store:
                            e.wait_ge(s_stage[b], (h + n // 2 + 1) * 16)
                        if store and isinstance(low, str) and low == "max":
                            e.tensor_reduce(high[:, h * 2 + b:h * 2 + b + 1], flat, AX_X, ALU.max,
                                            apply_absolute_value=True).then_inc(s_w, 1)
                        elif store and isinstance(low, str):
                            q = h * 6 + b * 3 + (0 if low == "row" else 3 * K)
                            scale = w_row if low == "row" else w_quant[:, ds(F // P + k)].broadcast_to([P, width])
                            e.tensor_tensor(flat, flat, scale, ALU.mult).then_inc(s_wq, 1)
                            e.wait_ge(s_wq, q + 1)
                            e.tensor_tensor(flat, flat, magic[:, 0:1].broadcast_to([P, width]), ALU.add).then_inc(s_wq, 1)
                            e.wait_ge(s_wq, q + 2)
                            e.tensor_tensor(high[part], flat, magic[:, 0:1].broadcast_to([P, width]), ALU.subtract).then_inc(s_wq, 1)
                            e.wait_ge(s_wq, q + 3)
                            e.sem_inc(s_w, 1)
                        elif store:
                            if name == "L3_gnn_W_down":
                                e.tensor_tensor(flat, flat, cols[:, k:k + 1].broadcast_to([P, width]), ALU.mult).then_inc(s_rms, 1)
                                e.wait_ge(s_rms, k + 1)
                            e.tensor_copy(high[part], flat).then_inc(s_wh, 1)
                            e.wait_ge(s_wh, h * 2 + (b + 1 + skipped))
                            e.tensor_tensor(low[part], flat, high[part], ALU.subtract).then_inc(s_w, 1)
                        else:
                            wait(e, s_w, m - 1)
                            e.dma_start(flat, src[part]).then_inc(s_stage[b], 16)

                steps = blocks * per // 2
                singles(e, steps, body, first=steps if name in ("maxima_in", "maxima_out", "L2_ffn_W_out", "L3_gnn_W_down") else 1)
                n += blocks * per

        def wait_own(e, what, value):
            e.wait_ge(what, value)
            if not isinstance(value, int):
                e.wait_ge(s_const, 1)

        def window_bounds(e, w):
            return (e.value_load(bounds[0:1, ds(w)], min_val=0, max_val=NC - 1),
                    e.value_load(bounds[0:1, ds(w + T)], min_val=1, max_val=NC))

        U3 = 6

        def load_experts(e, store):
            n = PARTS["L3_gnn_W_up"]

            def expert(x3, j):
                for name, (high, low), blocks in (("L3_gu", gu[j], K), ("L3_down", dn[j], 2)):
                    src = A[name].rearrange("(k p) n -> p k n", p=P)
                    if store:
                        if name == "L3_gu":
                            if isinstance(x3, int) and x3 < 2:
                                e.wait_ge(s_aggl if j else s_out, 1 if j else 11 * T)
                            else:
                                e.wait_ge(s_gu, x3 * U3 - U3)
                        else:
                            if isinstance(x3, int) and x3 < 2:
                                pass
                            else:
                                e.wait_ge(s_out, x3 * T + 10 * T)
                    for part in range(blocks if name == "L3_gu" else 2 * blocks):
                        at = part + (0 if name == "L3_gu" else K)
                        k, c = (part, 0) if name == "L3_gu" else (part // 2, part % 2 * HALF)
                        b = at % 2
                        flat = stage[:, b, :]
                        if store:
                            e.wait_ge(s_stage[b], (x3 * 6 + (at // 2 + n // 2 + 1)) * 16)
                            e.sem_inc(s_met, 1)
                            e.tensor_copy(high[:, k, c:c + HALF], flat).then_inc(s_wh, 1)
                            e.wait_ge(s_wh, x3 * 12 + (at + 1 + SPLIT))
                            e.tensor_tensor(low[:, k, c:c + HALF], flat, high[:, k, c:c + HALF], ALU.subtract).then_inc(s_w, 1)
                        else:
                            e.wait_ge(s_w, x3 * 12 + (n + at - 1))
                            e.dma_start(flat, src[:, ds(x3 * blocks + k), c:c + HALF]).then_inc(s_stage[b], 16)
            pairs(e, E3 + 1, expert, 2, 1)

        def over_windows(e, begin, chunk_max, between, chunk_sum, end):
            ch, cm, cs = (e.alloc_register(f"layer3_{n}_chunks") for n in ("all", "max", "sum"))
            for r in (ch, cm, cs):
                e.reg_mov(r, 0)
            with e.Fori(0, T) as w:
                first, last = window_bounds(e, w)
                begin(w, e.snap(ch), e.snap(cm), e.snap(cs))
                with e.Fori(first, last) as c:
                    chunk_max(w, c, e.snap(ch), e.snap(cm))
                    e.reg_add(ch, ch, 1)
                    e.reg_add(cm, cm, 1)
                between(w, e.snap(ch), e.snap(cm), e.snap(cs))
                with e.Fori(first, last) as c:
                    chunk_sum(w, c, e.snap(ch), e.snap(cs))
                    e.reg_add(ch, ch, 1)
                    e.reg_add(cs, cs, 1)
                end(w, e.snap(ch), e.snap(cm), e.snap(cs))

        block = ctx.enter_context(nc.Block())

        @block.sync
        def _(sp):
            sp.dma_start(edge_i[0:EP, 0, :], A["src"]).then_inc(s_edges, 16)
            sp.dma_start(edge_i[0:EP, 1, :], A["dst"]).then_inc(s_edges, 16)
            sp.dma_start(span_i[0:NC, :], A["dst_chunks"]).then_inc(s_edges, 16)
            sp.wait_ge(s_pad, 1)
            sp.dma_start(x[:, 0:T - 1, :], A["x"][0:(T - 1) * P, :].rearrange("(t p) n -> p t n", p=P)).then_inc(s_x, 16)
            sp.dma_start(x[0:LAST, T - 1, :], A["x"][(T - 1) * P:NODES, :]).then_inc(s_x, 16)
            load_weights(sp, False, "L0_gnn_W", None)
            sp.wait_ge(s_coef, 3 * T)
            sp.dma_start(src_i[0:EP, :], A["src"]).then_inc(s_idx, 16)
            sp.dma_start(dst_i[0:EP, :], A["dst"]).then_inc(s_idx, 16)
            sp.wait_ge(s_lr, T)
            sp.dma_start(xl_table.rearrange("(t p) n -> p t n", p=P), lr[:, :, 0:HID]).then_inc(s_table, 16)

            def nothing_more(*_):
                pass

            def load_dst(w, c, ch, _):
                for b in range(2):
                    sp.wait_ge(s_dt, ch * 2 + (b + 1))
                    sp.dma_start(dst_in[b], A["dst_row"][:, ds(c * (CHUNK * EP) + b * 2 * EP, 2 * EP)].partition_broadcast(P)).then_inc(s_row_in[b], 16)
            over_windows(sp, nothing_more, load_dst, nothing_more, load_dst, nothing_more)
            load_experts(sp, False)
            sp.wait_ge(s_upd, (7 + E3 + 1) * T)
            sp.dma_start(out[0:(T - 1) * P, :].rearrange("(t p) n -> p t n", p=P), x[:, 0:T - 1, :]).then_inc(s_store, 16)
            sp.dma_start(out[(T - 1) * P:NODES, :], x[0:LAST, T - 1, :]).then_inc(s_store, 16)
            sp.wait_ge(s_store, 32)

        @block.gpsimd
        def _(pool):
            pool.memset(x[:, T - 1, :], 0.0).then_inc(s_pad, 1)
            pool.memset(ident[:, :], 0.0)
            pool.memset(ones[:, :], 1.0)
            pool.memset(one16[:, :], 1.0)
            pool.memset(eps[:, 0:1], LN_EPS)
            pool.memset(eps[:, 1:2], LN_EPS * RMS_EPS)
            pool.memset(nothing, 0.0)

            def count(to, pattern, base=0, channel_multiplier=0):
                return pool.iota(to, pattern, base=base, channel_multiplier=channel_multiplier,
                                 allow_small_or_imprecise_dtypes=True)
            count(win_lo[:, :], [[P, T]])
            count(win_neg[:, :], [[-P, T]])
            count(chunk_no[:, :], [[0, 1]], channel_multiplier=1)
            count(rank[:, :], [[-1, 16]], base=16)
            count(eight[:, :], [[1, K]])
            count(part_i[:, 0:1], [[0, 1]], channel_multiplier=1)
            count(src_row, [[1, NP]])
            count(dst_row, [[1, P]]).then_inc(s_pool, 1)
            pool.wait_ge(s_pool, 1)
            pool.affine_select(out=ident[:, :], in_=ident[:, :], compare_op=ALU.not_equal, fill=1.0, base=0,
                               pattern=[[-1, P]], channel_multiplier=1).then_inc(s_pool, 1)
            pool.wait_ge(s_pool, 2)
            pool.tensor_copy(identb[:, :], ident[:, :])
            pool.tensor_copy(ident16[:, :], ident[:, :]).then_inc(s_const, 1)
            pool.wait_ge(s_span, 1)
            pool.partition_all_reduce(hit_all[0:NC, :], hit[0:NC, :], NC, RMAX).then_inc(s_hits, 1)
            load_weights(pool, True, "L0_gnn_W", "L1_ffn_w1")
            pool.wait_ge(s_mins, 1)
            pool.partition_all_reduce(low2_all[:, :], low2[:, :], P, RMAX).then_inc(s_mins_all, 1)
            load_weights(pool, True, "L1_ffn_w1", "maxima_in")
            load_weights(pool, True, "L2_gnn_W_a", "L2_ffn_W_in")
            pool.memset(magic[:, :], ROUND).then_inc(s_pool, 1)
            pool.wait_ge(s_pool, 3)
            load_weights(pool, True, "L2_ffn_W_in", "L3_gnn_W_up")
            pool.wait_ge(s_max1, 1)
            pool.partition_all_reduce(x_max_all[:, :], x_max[:, 0:1], P, RMAX).then_inc(s_max1_all, 1)
            load_weights(pool, True, "L3_gnn_W_up", None)
            pool.wait_ge(s_max2, 1)
            pool.partition_all_reduce(h_max_all[:, :], h_max1[:, :], P, RMAX).then_inc(s_max2_all, 1)

            pool.wait_ge(s_coef, 3 * T)
            pool.memset(none16, 0.0)
            count(dst_no, [[1, P]])
            count(part_no, [[0, 1]], channel_multiplier=1)
            pool.memset(m_h, 1.0)
            pool.memset(m_l, 0.0).then_inc(s_aux, 1)
            pool.wait_ge(s_idx, 32)
            pool.wait_ge(s_table, 16)

            def nothing_more(*_):
                pass

            def gather(w, c, ch, _):
                for b in range(2):
                    pool.wait_ge(s_got_free, ch * 2 + (b + 1))
                    pool.sem_inc(s_idx_now, 1)
                    pool.tensor_copy(idx_now[b][0:EP, :], src_i[0:EP, ds(c * CHUNK + 2 * b, 2)]).then_inc(s_idx_now, 1)
                    pool.wait_ge(s_idx_now, ch * 6 + (3 * b + 2))
                    pool.sem_inc(s_idx_now, 1)
                    for q in range(2):
                        pool.indirect_dma_start(xl_got[b][0:EP, q, :], None, xl_table[:, :],
                                                bass.IndirectOffsetOnAxis(ap=idx_now[b][0:EP, q:q + 1], axis=0),
                                                bounds_check=NP - 1).then_inc(s_got[b], 16)
            over_windows(pool, nothing_more, gather, nothing_more, gather, nothing_more)
            load_experts(pool, True)
        @block.scalar
        def _(act):
            def store_window(w):
                wait_own(act, s_adj, w + 1)
                for c, (a, n) in enumerate(THIRD):
                    last = act.activation(adj[:, ds(w, 1), a:a + n], bank[:, c, 0:n], ACT.Copy,
                                          accum_out=deg3[:, ds(w, 1), c])
                last.then_inc(s_adj_free, 1)

            def std_of(i, base):
                wait_own(act, s_mv, base + i + 1)
                act.activation(std[:, :], mv[:, 1:2], ACT.Sqrt, bias=eps[:, 0:1]).then_inc(s_std, 1)

            def std3_of(i, base):
                wait_own(act, s_mv, base + i + 1)
                act.activation(std[:, :], mv[:, 1:2], ACT.Sqrt, scale=1.0 + RMS_EPS, bias=eps[:, 1:2]).then_inc(s_std, 1)

            def keep_turned_high(i, base):
                wait_own(act, s_turned, base + i + 1)
                act.activation(xT_h[:, :, ds(i * P, P)], ps_turn, ACT.Copy).then_inc(s_turn_h, 1)

            def project_scaled(i, j, idx, scale):
                wait_own(act, s_out, idx * T + i + 1)
                act.activation(h_h[:, ds(i), :], ps_out[j], ACT.Copy, scale=scale[:, ds(i)]).then_inc(s_hh, 1)

            for name, at, n in (("L0_ffn_bm", 0, K), ("L0_ffn_b1", K, K), ("L1_ffn_b1", 2 * K, F // P),
                                ("L2_ffn_b_in", 2 * K + F // P, F // P)):
                act.dma_start(cols[:, at:at + n], A[name]).then_inc(s_cols, 16)
            wait_own(act, s_const, 1)
            act.sem_inc(s_adj_free, 1)
            singles(act, T, store_window, first=0)
            wait_own(act, s_deg, 1)
            act.activation(dinv_in[:, :], deg_in[:, :], ACT.Sqrt, bias=ones[:, 0:1]).then_inc(s_sq, 1)

            std_of(0, 0)
            keep_turned_high(0, 0)

            def norm_project(i, j, more=True):
                if more:
                    std_of(i + 1, 0)
                    keep_turned_high(i + 1, 0)
                project_scaled(i, j, 0, dinv_in)
            pairs(act, T - 2, norm_project, first=0)
            norm_project(T - 2, 0)
            norm_project(T - 1, 1, False)

            def row_high(w):
                if not (isinstance(w, int) and w == 0):
                    wait_own(act, s_rowt, 2 * w)
                act.activation(row_h, adj[:, ds(w), :], ACT.Copy).then_inc(s_row_h, 1)

            def coef_high(w, j):
                wait_own(act, s_rowt, 2 * w + 1)
                if not isinstance(w, int) or w >= 2:
                    wait_own(act, s_cnt, 3 * w - 3)
                act.activation(coef_h[j], bank[:, 6:8, :].bitcast(F16)[:, :, 0:5 * P], ACT.Copy).then_inc(s_coef_h, 1)

            def keep_before(i, base):
                if not (isinstance(i, int) and i == 0):
                    keep_turned_high(i - 1, base)

            row_high(0)
            coef_high(0, 0)
            act.dma_start(bias[:, 0:DIM], A["L0_gnn_b"].partition_broadcast(P)).then_inc(s_bias, 16)

            def gather0(i, j, more=True):
                if more:
                    row_high(i + 1)
                    coef_high(i + 1, 1 - j)
                keep_before(i, T)
                std_of(i, T)
            pairs(act, T - 2, gather0)
            gather0(T - 2, 0)
            gather0(T - 1, 1, False)
            keep_turned_high(T - 1, T)

            wait_own(act, s_upd, T)
            act.dma_start(bias[:, 0:DIM], A["L0_ffn_bo"].partition_broadcast(P)).then_inc(s_bias, 16)
            wait_own(act, s_cnt, 3 * T)
            wait_own(act, s_out, 2 * T)
            act.dma_start(emb_f, A["L0_ffn_expert_emb"]).then_inc(s_small, 16)
            for head in range(K):
                act.dma_start(b2_f[head * 16:(head + 1) * 16, :], A["L0_ffn_b2"]).then_inc(s_small, 16)
            wait_own(act, s_cols, 64)

            def up0(f):
                for c, (a, n) in enumerate(THIRD):
                    wait_own(act, s_up, f * 3 + (c + 1))
                    act.activation(hT_h[:, ds(f), a:a + n], bank[:, c, 0:n], ACT.Identity, bias=cols[:, ds(f)]).then_inc(s_up_h, 1)
            singles(act, K, up0)

            wait_own(act, s_lg, 1)
            act.activation(gates_g, lg, ACT.Exp).then_inc(s_ex, 1)
            wait_own(act, s_gate_t, 1)
            act.activation(gT[0], bank[:, 0:3, :].rearrange("p a b -> p (a b)")[:, 0:NP], ACT.Copy).then_inc(s_gth, 1)

            def experts(hp, first=False):
                for jj in range(6):
                    s, b, c = hp * 6 + jj, jj % 2, jj % 3
                    head = hp * 2 + jj // 3
                    a, n = THIRD[c]

                    def gelu(j):
                        u = s * K + j
                        wait_own(act, s_unit, u + 1)
                        if not (first and jj == 0 and j < 2):
                            wait_own(act, s_hid, u - 1)
                        act.activation(unit[j % 2][:, 0:n], bank[:, j % 2, 0:n], ACT.Gelu, bias=cols[:, K + j:K + j + 1]).then_inc(s_gelu, 1)

                    def high(j):
                        wait_own(act, s_gated, s * K + (j + 1))
                        if j == 0 and not (first and jj < 2):
                            wait_own(act, s_comb_mm, s - 1)
                        act.activation(hid[b][0][:, j, 0:n], unit[j % 2][:, 0:n], ACT.Copy).then_inc(s_hid_h, 1)

                    gelu(0)
                    for j in range(1, K):
                        gelu(j)
                        high(j - 1)
                    high(K - 1)
                    if not (first and jj == 0):
                        comb_high(s - 1, 1 - b, (jj - 1) % 3, hp * 2 + (jj - 1) // 3)

            def comb_high(s, b, c, head):
                a, n = THIRD[c]
                wait_own(act, s_comb_mm, s + 1)
                act.activation(hT_h[:, ds(head), a:a + n], bank[:, 6 + b, 0:n], ACT.Copy).then_inc(s_comb_h, 1)
            experts(0, True)
            with act.Fori(1, K // 2) as hp:
                experts(hp)
            comb_high(3 * K - 1, 1, 2, K - 1)

            def out0(i, j):
                keep_before(i, 2 * T)
                std_of(i, 2 * T)
            pairs(act, T, out0)
            keep_turned_high(T - 1, 2 * T)

            wait_own(act, s_upd, 2 * T)
            act.dma_start(cols[:, 0:K], A["L3_gnn_rms_w"]).then_inc(s_cols, 16)
            act.dma_start(bias[:, 0:DIM], A["L1_gnn_a"][:, 0:DIM].partition_broadcast(P)).then_inc(s_bias, 16)
            act.dma_start(work[:, 0:DIM], A["L1_gnn_a"][:, DIM:2 * DIM].partition_broadcast(P)).then_inc(s_bias, 16)

            def project1(i, j):
                wait_own(act, s_out, i + (3 * T + 1))
                act.activation(h_h[:, ds(i), :], ps_out[j], ACT.Copy).then_inc(s_hh, 1)
            pairs(act, T, project1)
            wait_own(act, s_al_row, 1)
            for c, (a, n) in enumerate(THIRD):
                last = act.activation(bias[:, a:a + n], bank[:, 4 + c, 0:n], ACT.Copy)
            last.then_inc(s_al, 1)
            wait_own(act, s_shift, 1)
            act.activation(shift[:, 1:2], shift[:, 0:1], ACT.Exp).then_inc(s_epsr, 1)

            def coef1(i):
                wait_own(act, s_z, i + 1)
                act.activation(work[:, :], work[:, :], ACT.Exp, scale=-1.0, bias=shift[:, 0:1]).then_inc(s_ez, 1)

            def coef1_high(i, j):
                wait_own(act, s_cz, i + 1)
                if not isinstance(i, int) or i >= 2:
                    wait_own(act, s_out, i + (4 * T - 1))
                act.activation(coef_h[j], z, ACT.Copy).then_inc(s_coef_h, 1)
            coef1(0)
            coef1_high(0, 0)

            def gather1(i, j, more=True):
                if more:
                    coef1(i + 1)
                    coef1_high(i + 1, 1 - j)
                keep_before(i, 3 * T)
                wait_own(act, s_neg, i + 1)
                act.activation(xhat[:, :], xhat[:, :], ACT.Exp).then_inc(s_eneg, 1)
                std_of(i, 3 * T)
            pairs(act, T - 2, gather1)
            gather1(T - 2, 0)
            gather1(T - 1, 1, False)
            keep_turned_high(T - 1, 3 * T)

            wait_own(act, s_upd, 3 * T)
            act.dma_start(bias[:, 0:DIM], A["L1_ffn_b2"].partition_broadcast(P)).then_inc(s_bias, 16)
            act.dma_start(router_f, A["L1_ffn_router_w"].rearrange("(k p) n -> p k n", p=P)).then_inc(s_small, 16)

            def up1(f):
                for c, (a, n) in enumerate(THIRD):
                    u = f * 3 + c
                    act.wait_ge(s_up, u + (3 * K + 1))
                    act.activation(spacer[:, 2:3], one16[:, 0:1], ACT.Copy)
                    act.activation(up_buf[c][:, 0:n], bank[:, c, 0:n], ACT.Gelu_apprx_tanh, bias=cols[:, ds(f + 2 * K)]).then_inc(s_up_free, 1)
                    wait_own(act, s_up_free, u + (3 * K + 1))
                    act.activation(fT[0][:, ds(f), a:a + n], up_buf[c][:, 0:n], ACT.Copy).then_inc(s_up_h, 1)
            singles(act, F // P, up1)
            wait_own(act, s_lg, 2)
            act.activation(r_e, r_l, ACT.Exp).then_inc(s_ex, 1)

            def out1(i, j):
                keep_before(i, 4 * T)
                std_of(i, 4 * T)
            pairs(act, T, out1)
            keep_turned_high(T - 1, 4 * T)


            wait_own(act, s_upd, 4 * T)
            act.dma_start(bias[:, 0:DIM], A["L2_gnn_b"].partition_broadcast(P)).then_inc(s_bias, 16)
            wait_own(act, s_cnt, 3 * T)
            act.activation(dinv_out[:, :], deg_out[:, :], ACT.Sqrt).then_inc(s_sq, 1)
            wait_own(act, s_row2, 1)
            act.activation(w_row, bank[:, 7, 0:F], ACT.Copy).then_inc(s_row2k, 1)

            def project2(i, j):
                wait_own(act, s_sum, i + (3 * T + 1))
                act.activation(h_h[:, ds(i), :], ps_out[j], ACT.Copy, scale=dinv_out[:, ds(i)]).then_inc(s_hh, 1)
            wait_own(act, s_dinv, 2)
            pairs(act, T, project2)

            def coef2_high(i, j):
                if not isinstance(i, int) or i >= 2:
                    wait_own(act, s_out, i + (7 * T - 1))
                act.activation(coef_h[j], adj[:, :, ds(i * P, P)], ACT.Copy).then_inc(s_coef_h, 1)
            coef2_high(0, 0)

            def keep_turned(i, base):
                wait_own(act, s_turned, base + i + 1)
                act.activation(xT_f[:, :, ds(i * P, P)], ps_turn, ACT.Copy).then_inc(s_turn, 1)

            def gather2(i, j, more=True):
                if more:
                    coef2_high(i + 1, 1 - j)
                if not (isinstance(i, int) and i == 0):
                    keep_turned(i - 1, 5 * T)
                std_of(i, 5 * T)
            pairs(act, T - 2, gather2)
            gather2(T - 2, 0)
            gather2(T - 1, 1, False)
            keep_turned(T - 1, 5 * T)
            act.sem_inc(s_turn_h, T)

            act.dma_start(bias[:, 0:DIM], A["L2_ffn_b_out"].partition_broadcast(P)).then_inc(s_bias, 16)
            for k in range(K):
                wait_own(act, s_q, k + 1)
                act.activation(hT_h[:, k, :], xT_f[:, k, :], ACT.Copy).then_inc(s_q_h, 1)
            wait_own(act, s_q_l, K)

            def up2(f):
                for c, (a, n) in enumerate(THIRD):
                    act.wait_ge(s_up, f * 3 + (c + 3 * K + 3 * F // P + 1))
                    act.wait_ge(s_up_free, f * 3 + (c + 3 * K + 3 * F // P))
                    act.activation(spacer[:, 2:3], one16[:, 0:1], ACT.Copy)
                    act.activation(hid_f[:, ds(f), a:a + n], bank[:, c, 0:n], ACT.Gelu, bias=cols[:, ds(f + 2 * K + F // P)],
                                   scale=up_scale[:, ds(f)]).then_inc(s_up_free, 1)
            singles(act, F // P, up2)
            for f in range(F // P):
                wait_own(act, s_hq, f + 1)
                act.activation(fT[0][:, f, :], hid_f[:, f, :], ACT.Copy).then_inc(s_hq_h, 1)

            def out2(i, j):
                keep_before(i, 6 * T)
                std3_of(i, 6 * T)
            pairs(act, T, out2)
            keep_turned_high(T - 1, 6 * T)

            wait_own(act, s_upd, 6 * T)
            act.dma_start(att, A["L3_gnn_att"].partition_broadcast(P)).then_inc(s_bias, 16)

            def up3(f):
                for c, (a, n) in enumerate(THIRD):
                    wait_own(act, s_up, f * 3 + (c + 1 + 3 * K + 6 * F // P))
                    act.activation(xdT[0][:, f, a:a + n], bank[:, c, 0:n], ACT.Copy).then_inc(s_up_h, 1)
            for f in range(2):
                up3(f)

            def project3(i, j):
                wait_own(act, s_out, i + (9 * T + 1))
                act.activation(lr[:, ds(i), :], ps_out[j][:, 0:HALF], ACT.Copy).then_inc(s_lr, 1)
            pairs(act, T, project3)
            wait_own(act, s_lr, T)
            act.activation(xr_h, lr[:, :, HID:2 * HID], ACT.Copy).then_inc(s_xrh, 1)

            def nothing_more(*_):
                pass

            def self_weight(w, ch, cm, cs):
                act.wait_ge(s_win, w * 8 + 7)
                act.activation(p_self, p_self, ACT.Exp).then_inc(s_selfp, 1)

            def edge_weights(w, c, ch, cs):
                for b in range(2):
                    act.wait_ge(s_s, cs * 2 + (b + 1))
                    act.activation(z3[b][0:EP, :, HID:HID + 4], s_now[b][0:EP], ACT.Exp).then_inc(s_p, 1)
                for b in range(2):
                    act.wait_ge(s_got_free, ch * 2 + (b + 3))
                    act.wait_ge(s_scat, cs * 2 + (b + 1))
                    act.activation(wx_h[b][0:EP], z3[b][0:EP], ACT.Copy).then_inc(s_ph, 1)
            over_windows(act, nothing_more, nothing_more, self_weight, edge_weights, nothing_more)

            wait_own(act, s_aggt, 1)
            act.activation(aggT[0], bank[:, 0:5, :].rearrange("p a b -> p (a b)").rearrange("p (a b) -> p a b", a=2), ACT.Copy).then_inc(s_aggh, 1)

            def out3(i, j):
                keep_before(i, 7 * T)
                std_of(i, 7 * T)
            pairs(act, T, out3)
            keep_turned_high(T - 1, 7 * T)

            wait_own(act, s_upd, 7 * T)
            act.dma_start(router_f, A["L3_ffn_router_wT"].rearrange("(k p) n -> p k n", p=P)).then_inc(s_small, 16)
            act.dma_start(route_bias, A["L3_ffn_routing_bias"].partition_broadcast(P)).then_inc(s_small, 16)
            wait_own(act, s_lg, 3)
            act.activation(r_e, r_l, ACT.Sigmoid).then_inc(s_ex, 1)

            def expert3(x3, j):
                for unit3 in range(U3):
                    f, c = unit3 // 3, unit3 % 3
                    a, n = THIRD[c]
                    act.wait_ge(s_gu, x3 * U3 + (unit3 + 1))
                    act.activation(up_buf[c][:, 0:n], bank[:, 4 + unit3 % 2, 0:n], ACT.Silu).then_inc(s_silu, 1)
                    act.wait_ge(s_h3, x3 * U3 + (unit3 + 1))
                    if unit3 == 0:
                        act.wait_ge(s_out, x3 * T + 10 * T)
                    act.activation(h3[j][0][:, f, a:a + n], up_buf[c][:, 0:n], ACT.Copy).then_inc(s_h3h, 1)
            pairs(act, E3 + 1, expert3, 0, 1)
        @block.vector
        def _(dve):
            step = [0]

            def link(ins):
                step[0] += 1
                ins.then_inc(s_v, 1)
                dve.wait_ge(s_v, step[0])

            dve.wait_ge(s_edges, 48)
            dve.tensor_copy(edge_f[0:EP], edge_i[0:EP])
            link(dve.tensor_copy(span_f[0:NC, :], span_i[0:NC, :]))
            dve.tensor_reduce(span[0:NC, 0:1], span_f[0:NC, :], AX_X, ALU.min)
            link(dve.tensor_reduce(span[0:NC, 1:2], span_f[0:NC, :], AX_X, ALU.max))
            dve.wait_ge(s_const, 1)
            dve.tensor_scalar(hit[0:NC, 0:T], win_lo[0:NC, :], span[0:NC, 1:2], None, ALU.is_le)
            link(dve.tensor_scalar(hit[0:NC, T:2 * T], win_lo[0:NC, :], float(P - 1), span[0:NC, 0:1], ALU.add, ALU.is_ge))
            link(dve.tensor_tensor(hit[0:NC, 0:T], hit[0:NC, 0:T], hit[0:NC, T:2 * T], ALU.mult))
            dve.tensor_scalar(span[0:NC, 0:1], chunk_no[0:NC, :], 1.0, None, ALU.add)
            link(dve.tensor_scalar(span[0:NC, 1:2], chunk_no[0:NC, :], -1.0, float(NC), ALU.mult, ALU.add))
            dve.tensor_scalar(hit[0:NC, T:2 * T], hit[0:NC, 0:T], span[0:NC, 0:1], None, ALU.mult)
            link(dve.tensor_scalar(hit_all[0:NC, 0:T], hit[0:NC, 0:T], span[0:NC, 1:2], None, ALU.mult))
            dve.tensor_copy(hit[0:NC, 0:T], hit_all[0:NC, 0:T]).then_inc(s_span, 1)
            dve.wait_ge(s_hits, 1)
            link(dve.tensor_scalar(hit[0:1, 0:T], hit_all[0:1, 0:T], -1.0, float(NC), ALU.mult, ALU.add))
            link(dve.tensor_scalar(hit[0:1, 0:T], hit[0:1, 0:T], float(NC - 1), None, ALU.min))
            link(dve.tensor_scalar(hit[0:1, T:2 * T], hit[0:1, 0:T], 1.0, None, ALU.add))
            link(dve.tensor_tensor(hit[0:1, T:2 * T], hit[0:1, T:2 * T], hit_all[0:1, T:2 * T], ALU.max))
            link(dve.tensor_copy(bounds[0:1, :], hit[0:1, :]))
            dve.sem_inc(s_bounds, 1)

            done = dve.alloc_register("onehot_halves")
            dve.reg_mov(done, 0)
            with dve.Fori(0, T) as w:
                first, end = window_bounds(dve, w)
                with dve.Fori(first, end) as c:
                    m = dve.snap(done)
                    for b in range(2):
                        dve.wait_ge(s_hot_free, m + (b + 1))
                        for q in range(2):
                            t = c * CHUNK + (2 * b + q)
                            dve.tensor_scalar(src_hot[b][0:EP, q, :], src_row[0:EP, :], edge_f[0:EP, 0, ds(t)], None, ALU.is_equal)
                            last = dve.tensor_scalar(dst_hot[b][0:EP, q, :], dst_row[0:EP, :], edge_f[0:EP, 1, ds(t)],
                                                     win_neg[0:EP, ds(w)], ALU.subtract, ALU.is_equal)
                        last.then_inc(s_hot, 1)
                    dve.reg_add(done, done, 2)
            dve.wait_ge(s_adj_free, T + 1)
            dve.tensor_reduce(deg_in[:, :], deg3[:, :, :], AX_X, ALU.add).then_inc(s_deg, 1)
            link(dve.memset(deg_out[:, :], 0.0))
            dve.wait_ge(s_sq, 1)
            dve.reciprocal(dinv_in[:, :], dinv_in[:, :]).then_inc(s_dinv, 1)

            def stats(i, base, updated):
                if updated is not None:
                    dve.wait_ge(s_upd, updated)
                    dve.memset(spacer[:, 0:1], 0.0)
                dve.bn_stats(bn[:, 0, :], x[:, ds(i), 0:HALF].rearrange("p a n -> p (a n)"))
                dve.bn_stats(bn[:, 1, :], x[:, ds(i), HALF:DIM].rearrange("p a n -> p (a n)")).then_inc(s_bn, 1)
                dve.wait_ge(s_bn, base + i + 1)
                dve.memset(spacer[:, 1:2], 0.0)
                dve.bn_aggr(mv[:, :], bn[:, :, :]).then_inc(s_mv, 1)

            def normalise(i, base):
                dve.wait_ge(s_std, base + i + 1)
                dve.reciprocal(rstd[:, :], std[:, :]).then_inc(s_rstd, 1)
                dve.wait_ge(s_rstd, base + i + 1)
                wait(dve, s_turned, base + i)
                dve.tensor_scalar(xhat[:, :], x[:, ds(i), :], mv[:, 0:1], rstd[:, :], ALU.subtract, ALU.mult).then_inc(s_xhat, 1)

            def keep_turned_low(i, base):
                dve.wait_ge(s_turn_h, base + i + 1)
                dve.tensor_tensor(xT_l[:, :, ds(i * P, P)], ps_turn, xT_h[:, :, ds(i * P, P)], ALU.subtract).then_inc(s_turn, 1)

            dve.wait_ge(s_x, 32)
            dve.wait_ge(s_dinv, 1)
            stats(0, 0, None)
            normalise(0, 0)
            keep_turned_low(0, 0)

            def norm_project(i, j, more=True):
                if more:
                    stats(i + 1, 0, None)
                    normalise(i + 1, 0)
                    keep_turned_low(i + 1, 0)
                dve.wait_ge(s_hh, i + 1)
                dve.scalar_tensor_tensor(h_l[:, ds(i), :], ps_out[j], dinv_in[:, ds(i)], h_h[:, ds(i), :],
                                         ALU.mult, ALU.subtract).then_inc(s_out_free, 1)
            pairs(dve, T - 2, norm_project, first=0)
            norm_project(T - 2, 0)
            norm_project(T - 1, 1, False)

            def row_low(w):
                dve.wait_ge(s_row_h, w + 1)
                dve.tensor_tensor(row_l, adj[:, ds(w), :], row_h, ALU.subtract).then_inc(s_row_l, 1)
                dve.wait_ge(s_row_l, w + 1)
                dve.tensor_tensor(row_l[:, ds(w * P, P)], row_l[:, ds(w * P, P)], ident[:, :], ALU.add).then_inc(s_row, 1)

            def coef_low(w, j):
                dve.wait_ge(s_rowt, 2 * w + 2)
                dve.tensor_copy(coef_l[j], bank[:, 6:8, :].bitcast(BF16)[:, :, 0:5 * P]).then_inc(s_coef, 1)

            def count_out(w, j):
                dve.wait_ge(s_coef, w + 1)
                dve.wait_ge(s_coef_h, w + 1)
                dve.tensor_reduce(deg_part[:, 0, :], coef_h[j], AX_X, ALU.add)
                dve.tensor_reduce(deg_part[:, 1, :], coef_l[j], AX_X, ALU.add).then_inc(s_cnt, 1)
                dve.wait_ge(s_cnt, 3 * w + 1)
                dve.tensor_tensor(deg_out[:, :], deg_out[:, :], deg_part[:, 0, :], ALU.add).then_inc(s_cnt, 1)
                dve.wait_ge(s_cnt, 3 * w + 2)
                dve.tensor_tensor(deg_out[:, :], deg_out[:, :], deg_part[:, 1, :], ALU.add).then_inc(s_cnt, 1)

            def keep_before(i, base):
                if not (isinstance(i, int) and i == 0):
                    keep_turned_low(i - 1, base)

            def next_norm(i, tail):
                stats(i, (tail + 1) * T, i + (tail * T + 1))
                normalise(i, (tail + 1) * T)

            row_low(0)
            coef_low(0, 0)
            dve.wait_ge(s_bias, 16)

            def gather0(i, j, more=True):
                if more:
                    row_low(i + 1)
                    coef_low(i + 1, 1 - j)
                keep_before(i, T)
                count_out(i, j)
                dve.wait_ge(s_out, i + (T + 1))
                dve.scalar_tensor_tensor(ps_out[j], ps_out[j], dinv_in[:, ds(i)], bias[:, 0:DIM], ALU.mult, ALU.add).then_inc(s_sum, 1)
                dve.wait_ge(s_sum, i + 1)
                dve.scalar_tensor_tensor(x[:, ds(i), :], ps_out[j], 0.0, x[:, ds(i), :], ALU.max, ALU.add).then_inc(s_upd, 1)
                next_norm(i, 0)
            pairs(dve, T - 2, gather0)
            gather0(T - 2, 0)
            gather0(T - 1, 1, False)
            keep_turned_low(T - 1, T)

            dve.wait_ge(s_cols, 64)

            def up0(f):
                for c, (a, n) in enumerate(THIRD):
                    dve.wait_ge(s_up_h, f * 3 + (c + 1))
                    dve.scalar_tensor_tensor(hT_l[:, ds(f), a:a + n], bank[:, c, 0:n], cols[:, ds(f)], hT_h[:, ds(f), a:a + n],
                                             ALU.add, ALU.subtract).then_inc(s_up_free, 1)
            singles(dve, K, up0)

            dve.wait_ge(s_small, 16 * (K + 1))
            dve.tensor_copy(emb[0], emb_f)
            link(dve.tensor_copy(b2[0], b2_f))
            dve.tensor_tensor(emb[1], emb_f, emb[0], ALU.subtract).then_inc(s_emb, 1)
            dve.tensor_tensor(b2[1], b2_f, b2[0], ALU.subtract).then_inc(s_b2, 1)
            dve.tensor_scalar(part_i[:, 1:2], part_i[:, 0:1], 15, None, ALU.bitwise_and)
            link(dve.tensor_scalar(part_i[:, 2:3], part_i[:, 0:1], 4, None, ALU.logical_shift_right))
            link(dve.tensor_copy(part_f[:, :], part_i[:, 1:3]))
            dve.tensor_scalar(head_mask[:, :], eight[:, :], part_f[:, 1:2], None, ALU.is_equal)
            for half in range(2):
                for j in range(K):
                    last = dve.tensor_scalar(pick[:, j, half * 64:(half + 1) * 64], ones[:, 0:64], float(2 * j + half), part_f[:, 0:1],
                                             ALU.mult, ALU.is_equal)
            link(last)

            def spread(v, like):
                return v.unsqueeze(2).broadcast_to([P, like.shape[1], like.shape[2]])

            def along(row, like):
                return row[:, 0:like.shape[2]].unsqueeze(1).broadcast_to([P, like.shape[1], like.shape[2]])

            def first_largest(v, top, found, best, scratch):
                link(dve.tensor_tensor(scratch, v, spread(top, v), ALU.is_equal))
                link(dve.tensor_tensor(scratch, scratch, along(rank, v), ALU.mult))
                link(dve.tensor_reduce(best, scratch, AX_X, ALU.max))
                link(dve.tensor_tensor(found, scratch, spread(best, v), ALU.is_equal))

            dve.wait_ge(s_logit, T)
            raw = bank[:, 4:7, :].rearrange("p a b -> p (a b)")[:, 0:GROUPS * 16].rearrange("p (g e) -> p g e", e=16)
            link(dve.tensor_reduce(g_m, raw, AX_X, ALU.max))
            dve.tensor_tensor(lg, raw, spread(g_m, lg), ALU.subtract).then_inc(s_lg, 1)
            dve.wait_ge(s_lg, 1)
            link(dve.memset(g_m, 0.0))
            first_largest(lg, g_m, t_m, g_c, t_c)
            dve.wait_ge(s_ex, 1)
            link(dve.scalar_tensor_tensor(lg, t_m, -BIG, lg, ALU.mult, ALU.add))
            link(dve.tensor_reduce(g_m, lg, AX_X, ALU.max))
            first_largest(lg, g_m, t_o, g_c, t_c)
            link(dve.tensor_tensor(t_m, t_m, t_o, ALU.add))
            link(dve.tensor_reduce(g_z, gates_g, AX_X, ALU.add))
            dve.reciprocal(g_z, g_z)
            link(dve.tensor_tensor(gates_g, gates_g, t_m, ALU.mult))
            dve.tensor_tensor(gates_g, gates_g, spread(g_z, lg), ALU.mult).then_inc(s_gate, 1)
            dve.wait_ge(s_gth, 1)
            dve.tensor_tensor(gT[1], bank[:, 0:3, :].rearrange("p a b -> p (a b)")[:, 0:NP], gT[0], ALU.subtract).then_inc(s_gt, 1)
            dve.wait_ge(s_gt, 1)

            def mask_gates(s, c, head):
                a, n = THIRD[c]
                dve.tensor_scalar(gm[c][0][:, 0:n], gT[0][:, a:a + n], head_mask[:, ds(head)], None, ALU.mult)
                dve.tensor_scalar(gm[c][1][:, 0:n], gT[1][:, a:a + n], head_mask[:, ds(head)], None, ALU.mult).then_inc(s_gm, 1)

            def comb_low(s, b, c, head):
                a, n = THIRD[c]
                dve.wait_ge(s_comb_h, s + 1)
                dve.tensor_tensor(hT_l[:, ds(head), a:a + n], bank[:, 6 + b, 0:n], hT_h[:, ds(head), a:a + n], ALU.subtract).then_inc(s_comb, 1)

            def experts(hp, first=False, last=False):
                for jj in range(6):
                    s, b, c = hp * 6 + jj, jj % 2, jj % 3
                    a, n = THIRD[c]
                    for j in range(K + 1):
                        u = s * K + j
                        if j < K:
                            dve.wait_ge(s_spread, u + 1)
                            dve.wait_ge(s_gelu, u + 1)
                            dve.tensor_tensor(unit[j % 2][:, 0:n], unit[j % 2][:, 0:n], bank[:, 2 + j % 2, 0:n], ALU.mult).then_inc(s_gated, 1)
                        if j > 0:
                            dve.wait_ge(s_hid_h, u)
                            dve.tensor_tensor(hid[b][1][:, j - 1, 0:n], unit[(j - 1) % 2][:, 0:n], hid[b][0][:, j - 1, 0:n],
                                              ALU.subtract).then_inc(s_hid, 1)
                        if j == 4 and not (last and jj == 5):
                            if not (first and jj < 2):
                                dve.wait_ge(s_comb_mm, s - 1)
                            mask_gates(s + 1, (jj + 1) % 3, hp * 2 + (jj + 1) // 3)
                    if not (first and jj == 0):
                        comb_low(s - 1, 1 - b, (jj - 1) % 3, hp * 2 + (jj - 1) // 3)
            mask_gates(0, 0, 0)
            experts(0, True)
            with dve.Fori(1, K // 2 - 1) as hp:
                experts(hp)
            experts(K // 2 - 1, False, True)
            comb_low(3 * K - 1, 1, 2, K - 1)

            dve.wait_ge(s_bias, 32)

            def out0(i, j):
                keep_before(i, 2 * T)
                dve.wait_ge(s_out, i + (2 * T + 1))
                dve.tensor_tensor(ps_out[j], ps_out[j], bias[:, 0:DIM], ALU.add).then_inc(s_sum, 1)
                dve.wait_ge(s_sum, i + (T + 1))
                dve.tensor_tensor(x[:, ds(i), :], ps_out[j], x[:, ds(i), :], ALU.add).then_inc(s_upd, 1)
                next_norm(i, 1)
            pairs(dve, T, out0)
            keep_turned_low(T - 1, 2 * T)

            dve.wait_ge(s_bias, 64)

            def project1(i, j):
                dve.wait_ge(s_hh, i + (T + 1))
                if not isinstance(i, int) or i >= 1:
                    dve.wait_ge(s_out_free, i + T)
                dve.scalar_tensor_tensor(xhat[:, :], ps_out[j], 1.0, bias[:, 0:DIM], ALU.mult, ALU.mult, accum_out=al[:, ds(i)])
                dve.scalar_tensor_tensor(spare, ps_out[j], 1.0, work[:, 0:DIM], ALU.mult, ALU.mult, accum_out=ar[:, ds(i)])
                dve.tensor_tensor(h_l[:, ds(i), :], ps_out[j], h_h[:, ds(i), :], ALU.subtract).then_inc(s_out_free, 1)
            pairs(dve, T, project1)
            dve.wait_ge(s_out_free, 2 * T)
            dve.tensor_tensor(z, ident[:, :].unsqueeze(1).broadcast_to([P, T, P]), al[:, :].unsqueeze(2).broadcast_to([P, T, P]),
                              ALU.mult).then_inc(s_diag, 1)
            dve.tensor_reduce(low2[:, 0:1], al[:, :], AX_X, ALU.min)
            link(dve.tensor_reduce(low2[:, 1:2], ar[:, :], AX_X, ALU.min))
            dve.tensor_scalar(low2[:, :], low2[:, :], -1.0, None, ALU.mult).then_inc(s_mins, 1)
            dve.wait_ge(s_mins_all, 1)
            link(dve.tensor_tensor(shift[:, 0:1], low2_all[:, 0:1], low2_all[:, 1:2], ALU.add))
            link(dve.tensor_scalar(shift[:, 0:1], shift[:, 0:1], -1.0, None, ALU.mult))
            link(dve.scalar_tensor_tensor(shift[:, 0:1], shift[:, 0:1], 0.1, shift[:, 0:1], ALU.mult, ALU.max))
            dve.tensor_scalar(shift[:, 0:1], shift[:, 0:1], 0.4, 0.0, ALU.add, ALU.min).then_inc(s_shift, 1)
            dve.wait_ge(s_epsr, 1)
            link(dve.tensor_scalar(shift[:, 2:3], shift[:, 1:2], 1e-5, None, ALU.mult))
            dve.wait_ge(s_al, 1)

            def coef1(i, j):
                dve.tensor_tensor(z, bias[:, ds(i * P, P)].unsqueeze(1).broadcast_to([P, T, P]),
                                  ar[:, :].unsqueeze(2).broadcast_to([P, T, P]), ALU.add).then_inc(s_zs, 1)
                dve.wait_ge(s_zs, i + 1)
                dve.scalar_tensor_tensor(z, z, 0.1, z, ALU.mult, ALU.max).then_inc(s_z, 1)
                dve.wait_ge(s_ez, i + 1)
                dve.tensor_tensor(z, z, adj[:, :, ds(i * P, P)], ALU.mult).then_inc(s_cz, 1)

            def coef1_low(i, j):
                dve.wait_ge(s_coef_h, i + (T + 1))
                dve.tensor_tensor(coef_l[j], z, coef_h[j], ALU.subtract).then_inc(s_coef, 1)
            coef1(0, 0)
            coef1_low(0, 0)

            def gather1(i, j, more=True):
                if more:
                    dve.wait_ge(s_coef, i + (T + 1))
                    coef1(i + 1, 1 - j)
                    coef1_low(i + 1, 1 - j)
                keep_before(i, 3 * T)
                dve.wait_ge(s_out, i + (4 * T + 1))
                dve.tensor_scalar(rstd[:, :], bank[:, 6 + j, 0:1], shift[:, 2:3], None, ALU.add).then_inc(s_step1, 1)
                dve.wait_ge(s_step1, 4 * i + 1)
                dve.reciprocal(rstd[:, :], rstd[:, :]).then_inc(s_step1, 1)
                dve.wait_ge(s_step1, 4 * i + 2)
                dve.tensor_scalar(ps_out[j], ps_out[j], rstd[:, :], None, ALU.mult).then_inc(s_step1, 1)
                dve.wait_ge(s_step1, 4 * i + 3)
                dve.tensor_scalar(xhat[:, :], ps_out[j], 0.0, None, ALU.min).then_inc(s_neg, 1)
                dve.wait_ge(s_eneg, i + 1)
                dve.scalar_tensor_tensor(ps_out[j], ps_out[j], 0.0, xhat[:, :], ALU.max, ALU.add).then_inc(s_step1, 1)
                dve.wait_ge(s_step1, 4 * i + 4)
                dve.scalar_tensor_tensor(x[:, ds(i), :], ps_out[j], -1.0, x[:, ds(i), :], ALU.add, ALU.add).then_inc(s_upd, 1)
                next_norm(i, 2)
            pairs(dve, T - 2, gather1)
            gather1(T - 2, 0)
            gather1(T - 1, 1, False)
            keep_turned_low(T - 1, 3 * T)

            def up1(f):
                for c, (a, n) in enumerate(THIRD):
                    dve.wait_ge(s_up_h, f * 3 + (3 * K + c + 1))
                    dve.tensor_tensor(fT[1][:, ds(f), a:a + n], up_buf[c][:, 0:n], fT[0][:, ds(f), a:a + n],
                                      ALU.subtract).then_inc(s_hid_l, 1)
            dve.wait_ge(s_small, 16 * (K + 2))
            link(dve.tensor_copy(router[0], router_f))
            dve.tensor_tensor(router[1], router_f, router[0], ALU.subtract).then_inc(s_router1, 1)
            singles(dve, F // P, up1)
            load_weights(dve, True, "maxima_in", "L2_gnn_W_a")
            dve.wait_ge(s_logit, 2 * T)
            raw1 = bank[:, 7, 0:T * 8].rearrange("p (t e) -> p t e", e=8)
            a_, b_, c_ = r_s[:, 0, :], r_s[:, 1, :], r_s[:, 2, :]
            link(dve.tensor_reduce(a_, raw1, AX_X, ALU.max))
            dve.tensor_tensor(r_l, raw1, spread(a_, r_l), ALU.subtract).then_inc(s_lg, 1)
            dve.wait_ge(s_ex, 2)
            link(dve.tensor_reduce(a_, r_e, AX_X, ALU.add))
            link(dve.reciprocal(a_, a_))
            link(dve.tensor_tensor(r_e, r_e, spread(a_, r_e), ALU.mult))
            link(dve.tensor_reduce(a_, r_e, AX_X, ALU.max))
            first_largest(r_e, a_, r_o, b_, r_l)
            link(dve.tensor_scalar(r_o, r_o, -1.0, 1.0, ALU.mult, ALU.add))
            link(dve.tensor_tensor(r_e, r_e, r_o, ALU.mult))
            link(dve.tensor_reduce(b_, r_e, AX_X, ALU.max))
            link(dve.tensor_tensor(c_, a_, b_, ALU.add))
            link(dve.reciprocal(c_, c_))
            dve.tensor_tensor(a_, a_, c_, ALU.mult)
            link(dve.tensor_tensor(b_, b_, c_, ALU.mult))
            link(dve.tensor_tensor(a_, a_, b_, ALU.add))
            dve.wait_ge(s_bias, 80)

            def out1(i, j):
                keep_before(i, 4 * T)
                dve.wait_ge(s_out, i + (5 * T + 1))
                dve.tensor_tensor(ps_out[j], ps_out[j], bias[:, 0:DIM], ALU.add).then_inc(s_sum, 1)
                dve.wait_ge(s_sum, i + (2 * T + 1))
                dve.scalar_tensor_tensor(x[:, ds(i), :], ps_out[j], r_s[:, 0, ds(i)], x[:, ds(i), :], ALU.mult, ALU.add).then_inc(s_upd, 1)
                next_norm(i, 3)
            pairs(dve, T, out1)
            keep_turned_low(T - 1, 4 * T)

            dve.wait_ge(s_w, PARTS["maxima_out"])
            link(dve.tensor_reduce(w_amax[:, :], w_max.rearrange("p (a b) -> p a b", b=2), AX_X, ALU.max))
            link(dve.tensor_scalar(w_amax[:, :], w_amax[:, :], 1e-8, None, ALU.max))
            dve.tensor_scalar(w_step[:, :], w_amax[:, :], 1.0 / 127.0, None, ALU.mult)
            link(dve.reciprocal(w_quant[:, :], w_amax[:, :]))
            link(dve.tensor_scalar(w_quant[:, :], w_quant[:, :], 127.0, None, ALU.mult))
            dve.tensor_tensor(w_diag, ident[:, :].unsqueeze(1).broadcast_to([P, F // P, P]),
                              w_quant[:, 0:F // P].unsqueeze(2).broadcast_to([P, F // P, P]), ALU.mult).then_inc(s_wscale, 1)
            dve.wait_ge(s_sq, 2)
            dve.reciprocal(dinv_out[:, :], dinv_out[:, :]).then_inc(s_dinv, 1)
            dve.wait_ge(s_dinv, 2)
            dve.wait_ge(s_bias, 96)

            def project2(i, j):
                dve.wait_ge(s_out, i + (6 * T + 1))
                dve.tensor_tensor(ps_out[j], ps_out[j], bias[:, 0:DIM], ALU.add).then_inc(s_sum, 1)
                dve.wait_ge(s_hh, i + (2 * T + 1))
                dve.scalar_tensor_tensor(h_l[:, ds(i), :], ps_out[j], dinv_out[:, ds(i)], h_h[:, ds(i), :],
                                         ALU.mult, ALU.subtract).then_inc(s_out_free, 1)
            pairs(dve, T, project2)

            def coef2_low(i, j):
                dve.wait_ge(s_coef_h, i + (2 * T + 1))
                dve.tensor_tensor(coef_l[j], adj[:, :, ds(i * P, P)], coef_h[j], ALU.subtract).then_inc(s_low2, 1)
                dve.wait_ge(s_low2, i + 1)
                dve.tensor_tensor(coef_l[j][:, ds(i), :], coef_l[j][:, ds(i), :], ident[:, :].unsqueeze(1), ALU.add).then_inc(s_coef, 1)

            def largest(i, rows=P):
                dve.wait_ge(s_xhat, i + (5 * T + 1))
                dve.tensor_reduce(x_max[0:rows, 1:2], xhat[0:rows, :], AX_X, ALU.max, apply_absolute_value=True).then_inc(s_xm, 1)
                dve.wait_ge(s_xm, i + 2)
                dve.tensor_tensor(x_max[0:rows, 0:1], x_max[0:rows, 0:1], x_max[0:rows, 1:2], ALU.max)

            coef2_low(0, 0)
            dve.memset(x_max[:, :], 0.0).then_inc(s_xm, 1)

            def gather2(i, j, more=True):
                if more:
                    coef2_low(i + 1, 1 - j)
                dve.wait_ge(s_out, i + (7 * T + 1))
                dve.scalar_tensor_tensor(x[:, ds(i), :], ps_out[j], dinv_out[:, ds(i)], x[:, ds(i), :], ALU.mult, ALU.add).then_inc(s_upd, 1)
                next_norm(i, 4)
                if more:
                    largest(i)
            pairs(dve, T - 2, gather2)
            gather2(T - 2, 0)
            gather2(T - 1, 1, False)
            largest(T - 1, LAST)
            dve.memset(spacer[:, 0:1], 0.0).then_inc(s_max1, 1)

            dve.wait_ge(s_max1_all, 1)
            link(dve.tensor_scalar(x_max_all[:, :], x_max_all[:, :], 1e-8, None, ALU.max))
            dve.tensor_scalar(x_step[:, :], x_max_all[:, :], 1.0 / 32767.0, None, ALU.mult)
            link(dve.reciprocal(x_quant[:, :], x_max_all[:, :]))
            link(dve.tensor_scalar(x_quant[:, :], x_quant[:, :], 32767.0, None, ALU.mult))
            dve.tensor_scalar(up_scale[:, :], w_step[:, 0:F // P], x_step[:, :], None, ALU.mult)
            dve.wait_ge(s_turn, 6 * T)
            for k in range(K):
                link(dve.tensor_scalar(xT_f[:, k, :], xT_f[:, k, :], x_quant[:, :], ROUND, ALU.mult, ALU.add))
                dve.tensor_scalar(xT_f[:, k, :], xT_f[:, k, :], -ROUND, None, ALU.add).then_inc(s_q, 1)
                if k:
                    dve.wait_ge(s_q_h, k)
                    dve.tensor_tensor(hT_l[:, k - 1, :], xT_f[:, k - 1, :], hT_h[:, k - 1, :], ALU.subtract).then_inc(s_q_l, 1)
            dve.wait_ge(s_q_h, K)
            dve.tensor_tensor(hT_l[:, K - 1, :], xT_f[:, K - 1, :], hT_h[:, K - 1, :], ALU.subtract).then_inc(s_q_l, 1)

            for f in range(F // P):
                for c, (a, n) in enumerate(THIRD):
                    u = f * 3 + c
                    dve.wait_ge(s_up_free, 3 * K + 3 * F // P + u + 1)
                    last = dve.tensor_reduce(h_max[:, u:u + 1], hid_f[:, f, a:min(a + n, NODES)], AX_X, ALU.max, apply_absolute_value=True)
            link(last)
            dve.tensor_reduce(h_max1[:, :], h_max[:, :], AX_X, ALU.max).then_inc(s_max2, 1)
            dve.wait_ge(s_max2_all, 1)
            link(dve.tensor_scalar(h_max_all[:, :], h_max_all[:, :], 1e-8, None, ALU.max))
            link(dve.reciprocal(h_quant[:, :], h_max_all[:, :]))
            dve.tensor_scalar(h_max_all[:, :], h_max_all[:, :], 1.0 / 32767.0, None, ALU.mult)
            link(dve.tensor_scalar(h_quant[:, :], h_quant[:, :], 32767.0, None, ALU.mult))
            link(dve.tensor_scalar(h_scale[:, :], w_step[:, F // P:], h_max_all[:, :], None, ALU.mult))
            for f in range(F // P):
                link(dve.tensor_scalar(hid_f[:, f, :], hid_f[:, f, :], h_quant[:, :], ROUND, ALU.mult, ALU.add))
                dve.tensor_scalar(hid_f[:, f, :], hid_f[:, f, :], -ROUND, h_scale[:, f:f + 1], ALU.add, ALU.mult).then_inc(s_hq, 1)
                if f:
                    dve.wait_ge(s_hq_h, f)
                    dve.tensor_tensor(fT[1][:, f - 1, :], hid_f[:, f - 1, :], fT[0][:, f - 1, :], ALU.subtract).then_inc(s_hq_l, 1)
            dve.wait_ge(s_hq_h, F // P)
            dve.tensor_tensor(fT[1][:, F // P - 1, :], hid_f[:, F // P - 1, :], fT[0][:, F // P - 1, :], ALU.subtract).then_inc(s_hq_l, 1)
            dve.wait_ge(s_bias, 112)

            def out2(i, j):
                keep_before(i, 6 * T)
                dve.wait_ge(s_out, i + (8 * T + 1))
                dve.tensor_tensor(ps_out[j], ps_out[j], bias[:, 0:DIM], ALU.add).then_inc(s_sum, 1)
                dve.wait_ge(s_sum, i + (4 * T + 1))
                dve.tensor_tensor(x[:, ds(i), :], ps_out[j], x[:, ds(i), :], ALU.add).then_inc(s_upd, 1)
                next_norm(i, 5)
            pairs(dve, T, out2)
            keep_turned_low(T - 1, 6 * T)

            for f in range(2):
                for c, (a, n) in enumerate(THIRD):
                    dve.wait_ge(s_up_h, 3 * K + 3 * F // P + f * 3 + c + 1)
                    dve.tensor_tensor(xdT[1][:, f, a:a + n], bank[:, c, 0:n], xdT[0][:, f, a:a + n], ALU.subtract).then_inc(s_up_free, 1)
            dve.wait_ge(s_idx, 32)
            dve.tensor_copy(dst_f[0:EP, :], dst_i[0:EP, :])
            dve.wait_ge(s_xrh, 1)
            dve.tensor_tensor(xr_l, lr[:, :, HID:2 * HID], xr_h, ALU.subtract).then_inc(s_xr, 1)
            dve.wait_ge(s_bias, 128)
            link(dve.tensor_tensor(self_z, lr[:, :, 0:HID], lr[:, :, HID:2 * HID], ALU.add))
            link(dve.scalar_tensor_tensor(self_z, self_z, 0.2, self_z, ALU.mult, ALU.max))
            link(dve.tensor_tensor(self_z, self_z, att.unsqueeze(1).broadcast_to([P, T, HID]), ALU.mult))
            link(dve.tensor_reduce(e_self.rearrange("p a b -> p (a b)"), self_z.rearrange("p t (h d) -> p (t h) d", d=64), AX_X, ALU.add))
            dve.sem_inc(s_got_free, 2)
            dve.sem_inc(s_score, 1)
            dve.sem_inc(s_win, 1)
            dve.wait_ge(s_aux, 1)

            att_half = att[0:EP, :].unsqueeze(1).broadcast_to([EP, 2, HID])

            def dst_onehots(w, ch):
                for b in range(2):
                    dve.wait_ge(s_row_in[b], ch * 16 + 16)
                    dve.wait_ge(s_pick, ch * 2 + (b + 1))
                    dve.tensor_scalar(by_dst[b], dst_in[b], win_neg[:, ds(w)], part_no[:, :], ALU.add, ALU.is_equal).then_inc(s_dt, 1)

            def clear_max(w, ch, cm, cs):
                dve.wait_ge(s_win, w * 8 + 1)
                dve.memset(run_max, -BIG).then_inc(s_win, 1)
                dve.wait_ge(s_win, w * 8 + 2)
                dve.memset(spacer[:, 0:1], 0.0)

            def chunk_max(w, c, ch, cm):
                n = cm * 12 + 1
                dve.wait_ge(s_score, n)
                dst_onehots(w, ch)
                for b in range(2):
                    for q in range(2):
                        last = dve.tensor_scalar(away[b][0:EP, q, :], dst_no[0:EP, :], dst_f[0:EP, ds(c * CHUNK + 2 * b + q)],
                                                 win_neg[0:EP, ds(w)], ALU.subtract, ALU.is_equal)
                    last.then_inc(s_score, 1)
                for b in range(2):
                    dve.wait_ge(s_score, n + (b + 1))
                    dve.tensor_scalar(away[b][0:EP], away[b][0:EP], -1.0, BIG, ALU.add, ALU.mult).then_inc(s_score, 1)
                for b in range(2):
                    dve.wait_ge(s_got[b], ch * 32 + 32)
                    dve.wait_ge(s_pick, ch * 2 + (b + 3))
                    dve.tensor_tensor(z3[b][0:EP, :, 0:HID], bank[0:EP, 4 + b, :].rearrange("p (a b) -> p a b", a=2), xl_got[b][0:EP], ALU.add).then_inc(s_got_free, 1)
                for b in range(2):
                    dve.wait_ge(s_got_free, ch * 2 + (b + 3))
                    dve.scalar_tensor_tensor(z3[b][0:EP, :, 0:HID], z3[b][0:EP, :, 0:HID], 0.2, z3[b][0:EP, :, 0:HID], ALU.mult, ALU.max).then_inc(s_score, 1)
                for b in range(2):
                    dve.wait_ge(s_score, n + (b + 5))
                    dve.tensor_tensor(z3[b][0:EP, :, 0:HID], z3[b][0:EP, :, 0:HID], att_half, ALU.mult).then_inc(s_score, 1)
                for b in range(2):
                    dve.wait_ge(s_score, n + (b + 7))
                    dve.tensor_reduce(e_now[b][0:EP], z3[b][0:EP, :, 0:HID].rearrange("p q (h d) -> p q h d", d=64), AX_X, ALU.add).then_inc(s_score, 1)
                for b in range(2):
                    dve.wait_ge(s_score, n + (b + 9))
                    dve.tensor_scalar(e_all[0:EP, ds(c * CHUNK + 2 * b, 2), :], e_now[b][0:EP], 0.0, None, ALU.add)
                    for q in range(2):
                        for h in range(4):
                            acc = run_max[0:EP, 2 * b + q, h * P:(h + 1) * P]
                            last = dve.scalar_tensor_tensor(acc, away[b][0:EP, q, :], e_now[b][0:EP, q, h:h + 1], acc, ALU.add, ALU.max)
                    last.then_inc(s_score, 1)

            def window_max(w, ch, cm, cs):
                n = w * 8 + 1
                dve.wait_ge(s_score, cm * 12 + 1)
                dve.tensor_tensor(run_max[0:EP, 0:2, :], run_max[0:EP, 0:2, :], run_max[0:EP, 2:4, :], ALU.max).then_inc(s_win, 1)
                dve.wait_ge(s_win, n + 2)
                dve.tensor_tensor(run_max[0:EP, 0, :], run_max[0:EP, 0, :], run_max[0:EP, 1, :], ALU.max).then_inc(s_win, 1)
                dve.wait_ge(s_acct, w + 1)
                dve.tensor_reduce(m_now, bank[:, 6, 0:4 * EP].rearrange("p (h e) -> p h e", h=4), AX_X, ALU.max).then_inc(s_win, 1)
                dve.wait_ge(s_win, n + 4)
                dve.tensor_tensor(m_now.unsqueeze(1), m_now.unsqueeze(1), e_self[:, ds(w), :], ALU.max).then_inc(s_win, 1)
                dve.wait_ge(s_win, n + 5)
                dve.tensor_copy(m_h[:, 0:4], m_now).then_inc(s_mk, 1)
                dve.tensor_tensor(p_self.unsqueeze(1), e_self[:, ds(w), :], m_now.unsqueeze(1), ALU.subtract).then_inc(s_win, 1)
                dve.wait_ge(s_mk, w * 2 + 1)
                dve.tensor_tensor(m_l[:, 0:4], m_now, m_h[:, 0:4], ALU.subtract).then_inc(s_mk, 1)

            def chunk_sum(w, c, ch, cs):
                dst_onehots(w, ch)
                for b in range(2):
                    dve.wait_ge(s_scat, cs * 2 + (b + 1))
                    for q in range(2):
                        dve.tensor_scalar(to_dst[b][0:EP, q, :], dst_no[0:EP, :], dst_f[0:EP, ds(c * CHUNK + 2 * b + q)],
                                          win_neg[0:EP, ds(w)], ALU.subtract, ALU.is_equal)
                picked = [bank[0:EP, 4 + b, 0:10].rearrange("p (a b) -> p a b", a=2) for b in range(2)]
                for b in range(2):
                    dve.wait_ge(s_pick, ch * 2 + (b + 3))
                    dve.tensor_tensor(s_now[b][0:EP], e_all[0:EP, ds(c * CHUNK + 2 * b, 2), :], picked[b][:, :, 4:5].broadcast_to([EP, 2, 4]),
                                      ALU.mult).then_inc(s_sub, 1)
                for b in range(2):
                    dve.wait_ge(s_sub, cs * 2 + (b + 1))
                    dve.tensor_tensor(s_now[b][0:EP], s_now[b][0:EP], picked[b][:, :, 0:4], ALU.subtract).then_inc(s_s, 1)
                for b in range(2):
                    dve.wait_ge(s_got[b], ch * 32 + 32)
                    dve.wait_ge(s_p, cs * 2 + (b + 1))
                    dve.tensor_tensor(z3[b][0:EP, :, 0:HID].rearrange("p q (h d) -> p q h d", d=64),
                                      xl_got[b][0:EP].rearrange("p q (h d) -> p q h d", d=64),
                                      z3[b][0:EP, :, HID:HID + 4].unsqueeze(3).broadcast_to([EP, 2, 4, 64]), ALU.mult).then_inc(s_got_free, 1)
                for b in range(2):
                    dve.wait_ge(s_ph, cs * 2 + (b + 1))
                    dve.tensor_tensor(wx_l[b][0:EP], z3[b][0:EP], wx_h[b][0:EP], ALU.subtract).then_inc(s_pl, 1)

            def window_sum(w, ch, cm, cs):
                n = w * 8 + 1
                dve.wait_ge(s_selfp, w + 1)
                dve.tensor_tensor(own.rearrange("p (h d) -> p h d", d=64), lr[:, ds(w), 0:HID].rearrange("p a (h d) -> p (a h) d", d=64),
                                  p_self.unsqueeze(2).broadcast_to([P, 4, 64]), ALU.mult)
                dve.wait_ge(s_agg, w + 1)
                dve.scalar_tensor_tensor(den, bank[:, 0, HID:HID + 4], 1e-16, p_self, ALU.add, ALU.add).then_inc(s_win, 1)
                dve.wait_ge(s_win, n + 7)
                dve.reciprocal(den, den)
                dve.tensor_tensor(own, own, bank[:, 0, 0:HID], ALU.add).then_inc(s_win, 1)
                dve.wait_ge(s_win, n + 8)
                dve.tensor_tensor(sums[:, ds(w), :].rearrange("p a (h d) -> p (a h) d", d=64), own.rearrange("p (h d) -> p h d", d=64),
                                  den.unsqueeze(2).broadcast_to([P, 4, 64]), ALU.mult)
            over_windows(dve, clear_max, chunk_max, window_max, chunk_sum, window_sum)
            dve.memset(spacer[:, 0:1], 0.0).then_inc(s_win, 1)

            dve.wait_ge(s_aggh, 1)
            dve.tensor_tensor(aggT[1], bank[:, 0:5, :].rearrange("p a b -> p (a b)").rearrange("p (a b) -> p a b", a=2), aggT[0], ALU.subtract).then_inc(s_aggl, 1)

            def out3(i, j):
                keep_before(i, 7 * T)
                dve.wait_ge(s_out, i + (10 * T + 1))
                dve.tensor_tensor(x[:, ds(i), :], ps_out[j], x[:, ds(i), :], ALU.add).then_inc(s_upd, 1)
                next_norm(i, 6)
            pairs(dve, T, out3)
            keep_turned_low(T - 1, 7 * T)

            dve.wait_ge(s_small, 16 * (K + 4))
            link(dve.tensor_copy(router[0], router_f))
            dve.tensor_tensor(router[1], router_f, router[0], ALU.subtract).then_inc(s_router1, 1)
            dve.wait_ge(s_logit, 3 * T)
            raw3 = bank[:, 3, 0:T * 8].rearrange("p (t e) -> p t e", e=8)
            dve.tensor_tensor(r_l, raw3, route_bias.unsqueeze(1).broadcast_to([P, T, 8]), ALU.add).then_inc(s_lg, 1)
            dve.wait_ge(s_ex, 3)
            link(dve.tensor_reduce(a_, r_e, AX_X, ALU.max))
            first_largest(r_e, a_, r_o, b_, r_l)
            link(dve.scalar_tensor_tensor(r_l, r_o, -2.0, r_e, ALU.mult, ALU.add))
            link(dve.tensor_reduce(b_, r_l, AX_X, ALU.max))
            link(dve.tensor_tensor(c_, a_, b_, ALU.add))
            dve.reciprocal(c_, c_)
            r_2 = gates3[:, :, 0:8]
            link(dve.tensor_copy(gates3[:, :, 0:8], r_o))
            first_largest(r_l, b_, r_o, a_, r_l)
            link(dve.tensor_tensor(r_o, r_o, r_2, ALU.add))
            link(dve.tensor_tensor(r_o, r_o, r_e, ALU.mult))
            dve.tensor_tensor(gates3[:, :, 0:8], r_o, spread(c_, r_o), ALU.mult)
            link(dve.memset(gates3[:, :, 8:9], 1.0))
            dve.sem_inc(s_gates3, 1)

            def hidden3(x3, j):
                for unit3 in range(U3):
                    f, c = unit3 // 3, unit3 % 3
                    a, n = THIRD[c]
                    dve.wait_ge(s_silu, x3 * U3 + (unit3 + 1))
                    dve.tensor_tensor(up_buf[c][:, 0:n], up_buf[c][:, 0:n], bank[:, 6 + unit3 % 2, 0:n], ALU.mult).then_inc(s_h3, 1)
                    dve.wait_ge(s_h3h, x3 * U3 + (unit3 + 1))
                    dve.tensor_tensor(h3[j][1][:, f, a:a + n], up_buf[c][:, 0:n], h3[j][0][:, f, a:a + n], ALU.subtract).then_inc(s_h3l, 1)

            def add3(x3):
                def tile(i, j):
                    dve.wait_ge(s_out, x3 * T + i + (11 * T + 1))
                    dve.wait_ge(s_upd, x3 * T + i + (6 * T + 1))
                    dve.scalar_tensor_tensor(x[:, ds(i), :], ps_out[j], gates3[:, ds(i), ds(x3)], x[:, ds(i), :], ALU.mult, ALU.add).then_inc(s_upd, 1)
                pairs(dve, T, tile, 0)

            def expert3(x3, j):
                hidden3(x3, j)
                add3(x3 - 1)
            hidden3(0, 0)
            expert3(1, 1)
            with dve.Fori(1, E3 // 2) as h:
                for j in range(2):
                    expert3(h * 2 + j, j)
            expert3(E3, 0)
            add3(E3)
        @block.tensor
        def _(pe):
            pe.wait_ge(s_const, 1)
            pe.sem_inc(s_hot_free, 2)

            done = pe.alloc_register("onehot_halves")
            pe.reg_mov(done, 0)
            pe.wait_ge(s_bounds, 1)
            with pe.Fori(0, T) as w:
                first, end = window_bounds(pe, w)
                pe.wait_ge(s_adj_free, w + 1)
                for c, (a, n) in enumerate(THIRD):
                    pe.matmul(bank[:, c, 0:n], nothing[0:EP, 0:P], nothing[0:EP, 0:n], start=True, stop=False)
                with pe.Fori(first, end):
                    m = pe.snap(done)
                    for b in range(2):
                        pe.wait_ge(s_hot, m + (b + 1))
                        for q in range(2):
                            for c, (a, n) in enumerate(THIRD):
                                last = pe.matmul(bank[:, c, 0:n], dst_hot[b][0:EP, q, :], src_hot[b][0:EP, q, a:a + n],
                                                 start=False, stop=False)
                        last.then_inc(s_hot_free, 1)
                    pe.reg_add(done, done, 2)
                for c, (a, n) in enumerate(THIRD):
                    last = pe.matmul(bank[:, c, 0:n], nothing[0:EP, 0:P], nothing[0:EP, 0:n], start=False, stop=True)
                last.then_inc(s_adj, 1)

            def turn(i, base):
                pe.wait_ge(s_xhat, base + i + 1)
                wait(pe, s_turn, base + i)
                for k in range(K):
                    last = pe.transpose(ps_turn[:, k, :], xhat[:, k * P:(k + 1) * P], ident[:, :])
                last.then_inc(s_turned, 1)

            def product(to, lhs, rhs, first, last, blocks, terms=((0, 0), (1, 0), (0, 1))):
                mm = None
                for k in range(first, last):
                    for n, (a, b) in enumerate(terms):
                        mm = pe.matmul(to, lhs(k, a), rhs(k, b), start=(k == 0 and n == 0),
                                       stop=(k == blocks - 1 and n == len(terms) - 1))
                return mm

            def tile_row(j, lhs, rhs, blocks, between=None, late=None, terms=((0, 0), (1, 0), (0, 1))):
                product(bank[:, 2 * j, :], lhs, lambda k, b: rhs(k, b)[:, 0:HALF], 0, blocks, blocks, terms)
                if between:
                    between()
                right = (bank[:, 2 * j + 1, :], lhs, lambda k, b: rhs(k, b)[:, HALF:DIM])
                product(*right, 0, blocks // 2, blocks, terms)
                if late:
                    late()
                product(*right, blocks // 2, blocks, blocks, terms).then_inc(s_out, 1)

            xT = (xT_h, xT_l)
            hT = (hT_h, hT_l)
            wt = (w_h, w_l)
            hv = (h_h, h_l)

            def project(i, j, between=None):
                tile_row(j, lambda k, a: xT[a][:, k, ds(i * P, P)], lambda k, b: wt[b][:, k, :], K, between)

            turn(0, 0)

            def norm_project(i, j, more=True):
                if isinstance(i, int) and i == 0:
                    pe.wait_ge(s_w, PARTS["L0_gnn_W"])
                    pe.wait_ge(s_adj_free, T + 1)
                if not isinstance(i, int) or i >= 2:
                    pe.wait_ge(s_out_free, i - 1)
                pe.wait_ge(s_turn, i + 1)
                project(i, j, (lambda: turn(i + 1, 0)) if more else None)
            pairs(pe, T - 2, norm_project)
            norm_project(T - 2, 0)
            norm_project(T - 1, 1, False)

            def turn_row(w, low):
                if low:
                    pe.wait_ge(s_row, w + 1)
                    pe.wait_ge(s_coef_h, w + 1)
                else:
                    pe.wait_ge(s_row_h, w + 1)
                    wait(pe, s_coef, w)
                row, dt, idt = (row_l, BF16, identb) if low else (row_h, F16, ident16)
                for s in range(T):
                    to = bank[:, 6 + s // 5, :].bitcast(dt)[:, (s % 5) * P:(s % 5 + 1) * P]
                    last = pe.transpose(to, row[:, s * P:(s + 1) * P], idt[:, :])
                last.then_inc(s_rowt, 1)

            def gathered(i, j, between, late):
                cf = (coef_h[j], coef_l[j])
                tile_row(j, lambda k, a: cf[a][:, k, :], lambda k, b: hv[b][:, k, :], T, between, late)

            def turn_before(i, base):
                if not (isinstance(i, int) and i == 0):
                    turn(i - 1, base)

            turn_row(0, False)
            turn_row(0, True)

            def gather0(i, j, more=True):
                if isinstance(i, int) and i < 2:
                    pe.wait_ge(s_out_free, T)
                else:
                    pe.wait_ge(s_upd, i - 1)
                pe.wait_ge(s_coef, i + 1)

                def late():
                    if more:
                        turn_row(i + 1, True)
                    turn_before(i, T)
                gathered(i, j, (lambda: turn_row(i + 1, False)) if more else None, late)
            pairs(pe, T - 2, gather0)
            gather0(T - 2, 0)
            gather0(T - 1, 1, False)
            turn(T - 1, T)

            def up_unit(f, c, base, lhs, rhs, blocks, terms=((0, 0), (1, 0), (0, 1))):
                a, n = THIRD[c]
                if isinstance(f, int) and f == 0:
                    if base:
                        pe.wait_ge(s_up_free, base)
                else:
                    pe.wait_ge(s_up_free, f * 3 + (base + c - 2))
                product(bank[:, c, 0:n], lhs, lambda k, b: rhs(k, b, slice(a, a + n)), 0, blocks, blocks, terms).then_inc(s_up, 1)

            pe.wait_ge(s_turn, 2 * T)
            pe.wait_ge(s_upd, T)
            pe.wait_ge(s_w, PARTS["L0_ffn_Wm"])
            singles(pe, K, lambda f: [up_unit(f, c, 0, lambda k, a: wt[a][:, k, ds(f * P, P)],
                                              lambda k, b, cols: xT[b][:, k, cols], K) for c in range(3)])

            pe.wait_ge(s_up_free, 3 * K)
            pe.wait_ge(s_emb, 1)
            logits = bank[:, 4:7, :].rearrange("p a b -> p (a b)")

            def route(t):
                for head in range(K):
                    mm = product(logits[:, ds(t * P + head * 16, 16)], lambda k, a: hT[a][:, head, ds(t * P, P)],
                                 lambda k, b: emb[b][:, :], 0, 1, 1)
                mm.then_inc(s_logit, 1)
            singles(pe, T, route)

            pe.wait_ge(s_gate, 1)
            for t in range(T):
                mm = pe.transpose(bank[:, t // 4, (t % 4) * P:(t % 4 + 1) * P], gates[:, t, :], ident[:, :])
            mm.then_inc(s_gate_t, 1)

            def expert_out(s, b, j, third):
                n = THIRD[third][1]
                if j == 0:
                    wait(pe, s_comb, s - 1)
                pe.wait_ge(s_hid, s * K + (j + 1))
                product(bank[:, 6 + b, 0:n], lambda k, a: w2[a][:, k, :], lambda k, c: hid[b][c][:, k, 0:n], j, j + 1, K + 1)
                if j == K - 1:
                    product(bank[:, 6 + b, 0:n], lambda k, a: b2[a][:, :], lambda k, c: gm[third][c][:, 0:n], K, K + 1, K + 1).then_inc(s_comb_mm, 1)

            pe.wait_ge(s_w, PARTS["L0_ffn_W2"])
            pe.wait_ge(s_b2, 1)
            pe.wait_ge(s_gt, 1)

            def experts(hp, first=False):
                for jj in range(6):
                    s, b, c = hp * 6 + jj, jj % 2, jj % 3
                    head = hp * 2 + jj // 3
                    a, n = THIRD[c]
                    for j in range(K):
                        u = s * K + j
                        if not (first and jj == 0 and j < 2):
                            pe.wait_ge(s_gelu, u - 1)
                        product(bank[:, j % 2, 0:n], lambda k, p: w1[p][:, j * P:(j + 1) * P],
                                lambda k, p: hT[p][:, ds(head), a:a + n].rearrange("p a n -> p (a n)"), 0, 1, 1).then_inc(s_unit, 1)
                        if j == 0:
                            pe.wait_ge(s_gm, s + 1)
                        if not (first and jj == 0 and j < 2):
                            pe.wait_ge(s_gated, u - 1)
                        product(bank[:, 2 + j % 2, 0:n], lambda k, p: pick[:, j, :], lambda k, p: gm[c][p][:, 0:n],
                                0, 1, 1, ((0, 0), (0, 1))).then_inc(s_spread, 1)
                        if not (first and jj == 0):
                            expert_out(s - 1, 1 - b, j, (jj - 1) % 3)
            experts(0, True)
            with pe.Fori(1, K // 2) as hp:
                experts(hp)
            for j in range(K):
                expert_out(3 * K - 1, 1, j, 2)

            pe.wait_ge(s_w, PARTS["L0_ffn_Wo"])
            pe.wait_ge(s_comb, 3 * K)
            pe.wait_ge(s_gelu, 3 * K * K)
            pe.wait_ge(s_gated, 3 * K * K)

            def out0(i, j):
                if not isinstance(i, int) or i >= 2:
                    pe.wait_ge(s_upd, i + (T - 1))
                tile_row(j, lambda k, a: hT[a][:, k, ds(i * P, P)], lambda k, b: wt[b][:, k, :], K, None,
                         lambda: turn_before(i, 2 * T))
            pairs(pe, T, out0)
            turn(T - 1, 2 * T)

            pe.wait_ge(s_w, PARTS["L1_gnn_W"])
            pe.wait_ge(s_turn, 3 * T)

            def project1(i, j):
                if isinstance(i, int) and i < 2:
                    pe.wait_ge(s_upd, 2 * T)
                else:
                    pe.wait_ge(s_out_free, i + (T - 1))
                project(i, j)
            pairs(pe, T, project1)

            pe.wait_ge(s_diag, 1)
            pe.wait_ge(s_turn, 3 * T)
            for c, (a, n) in enumerate(THIRD):
                mm = pe.matmul(bank[:, 4 + c, 0:n], ones[:, :], work[:, a:a + n], start=True, stop=True)
            mm.then_inc(s_al_row, 1)

            def gather1(i, j):
                if isinstance(i, int) and i < 2:
                    pe.wait_ge(s_out_free, 2 * T)
                    pe.wait_ge(s_al, 1)
                else:
                    pe.wait_ge(s_upd, i + (2 * T - 1))
                pe.wait_ge(s_coef, i + (T + 1))
                for k in range(T):
                    for p, cf in enumerate((coef_h[j], coef_l[j])):
                        pe.matmul(bank[:, 6 + j, 0:1], cf[:, k, :], one16[:, 0:1], start=(k == 0 and p == 0),
                                  stop=(k == T - 1 and p == 1))
                gathered(i, j, None, lambda: turn_before(i, 3 * T))
            pairs(pe, T, gather1)
            turn(T - 1, 3 * T)

            pe.wait_ge(s_turn, 4 * T)
            pe.wait_ge(s_upd, 3 * T)
            pe.wait_ge(s_w, PARTS["L1_ffn_w1"])

            def up1(f):
                for c in range(3):
                    if not isinstance(f, int):
                        pe.wait_ge(s_hid_l, f * 3 + (c - 2))
                    up_unit(f, c, 3 * K, lambda k, a: half_a[a][:, k, ds(f * P, P)], lambda k, b, cols: xT[b][:, k, cols], K)
            singles(pe, F // P, up1)
            pe.wait_ge(s_router1, 1)

            def route1(t):
                product(bank[:, 7, ds(t * 8, 8)], lambda k, a: xT[a][:, k, ds(t * P, P)], lambda k, b: router[b][:, k, :],
                        0, K, K).then_inc(s_logit, 1)
            singles(pe, T, route1)
            pe.wait_ge(s_w, PARTS["L1_ffn_w2"])
            pe.wait_ge(s_up_free, 3 * K + 3 * F // P)
            pe.wait_ge(s_hid_l, 3 * F // P)

            def out1(i, j):
                if not isinstance(i, int) or i >= 2:
                    pe.wait_ge(s_upd, i + (3 * T - 1))
                tile_row(j, lambda k, a: fT[a][:, k, ds(i * P, P)], lambda k, b: half_b[b][:, k, :], F // P, None,
                         lambda: turn_before(i, 4 * T))
            pairs(pe, T, out1)
            turn(T - 1, 4 * T)

            pe.wait_ge(s_wscale, 1)
            pe.matmul(bank[:, 7, 0:F], ones[:, :], work[:, 0:F], start=True, stop=True).then_inc(s_row2, 1)
            pe.wait_ge(s_w, PARTS["L2_gnn_W_b"])
            pe.wait_ge(s_turn, 5 * T)

            def project2(i, j):
                if isinstance(i, int) and i < 2:
                    pe.wait_ge(s_upd, 4 * T)
                else:
                    pe.wait_ge(s_out_free, i + (2 * T - 1))
                project(i, j)
            pairs(pe, T, project2)

            def gather2(i, j):
                if isinstance(i, int) and i < 2:
                    pe.wait_ge(s_out_free, 3 * T)
                else:
                    pe.wait_ge(s_upd, i + (4 * T - 1))
                pe.wait_ge(s_coef, i + (2 * T + 1))
                gathered(i, j, None, lambda: turn_before(i, 5 * T))
            pairs(pe, T, gather2)
            turn(T - 1, 5 * T)

            pe.wait_ge(s_w, PARTS["L2_ffn_W_in"])
            pe.wait_ge(s_q_l, K)
            pe.wait_ge(s_upd, 5 * T)
            singles(pe, F // P, lambda f: [up_unit(f, c, 3 * K + 3 * F // P, lambda k, a: half_a[0][:, k, ds(f * P, P)],
                                                   lambda k, b, cols: hT[b][:, k, cols], K, ((0, 0), (0, 1))) for c in range(3)])
            pe.wait_ge(s_w, PARTS["L2_ffn_W_out"])
            pe.wait_ge(s_up_free, 3 * K + 6 * F // P)
            pe.wait_ge(s_hq_l, F // P)

            def out2(i, j):
                if not isinstance(i, int) or i >= 2:
                    pe.wait_ge(s_upd, i + (5 * T - 1))
                tile_row(j, lambda k, a: fT[a][:, k, ds(i * P, P)], lambda k, b: half_b[0][:, k, :], F // P, None,
                         lambda: turn_before(i, 6 * T), ((0, 0), (1, 0)))
            pairs(pe, T, out2)
            turn(T - 1, 6 * T)

            pe.wait_ge(s_w, PARTS["L3_gnn_W_down"])
            pe.wait_ge(s_turn, 7 * T)
            pe.wait_ge(s_upd, 6 * T)
            for f in range(2):
                for c in range(3):
                    up_unit(f, c, 3 * K + 6 * F // P, lambda k, a: down[a][:, k, ds(f * P, P)], lambda k, b, cols: xT[b][:, k, cols], K)
            pe.wait_ge(s_w, PARTS["L3_gnn_Wr"])
            pe.wait_ge(s_up_free, 3 * K + 6 * F // P + 6)

            def project3(i, j):
                if not isinstance(i, int) or i >= 2:
                    pe.wait_ge(s_lr, i - 1)
                product(ps_out[j][:, 0:HALF], lambda k, a: xdT[a][:, k, ds(i * P, P)], lambda k, b: wlr[b][:, k, :], 0, 2, 2).then_inc(s_out, 1)
            pairs(pe, T, project3)
            pe.wait_ge(s_lr, T)
            pe.wait_ge(s_xr, 1)
            pe.wait_ge(s_aux, 1)
            for credit in (s_dt, s_pick, s_scat):
                pe.sem_inc(credit, 2)

            def nothing_more(*_):
                pass

            def pick_xr(w, c, ch, cm):
                for b in range(2):
                    pe.wait_ge(s_dt, ch * 2 + (b + 3))
                    pe.wait_ge(s_got_free, ch * 2 + (b + 1))
                    for q in range(2):
                        for n, part in enumerate((xr_h, xr_l)):
                            last = pe.matmul(bank[0:EP, 4 + b, q * HID:(q + 1) * HID], by_dst[b][:, q * EP:(q + 1) * EP], part[:, ds(w), :],
                                             start=n == 0, stop=n == 1)
                    last.then_inc(s_pick, 1)

            def turn_max(w, ch, cm, cs):
                pe.wait_ge(s_win, w * 8 + 4)
                for h in range(4):
                    last = pe.transpose(bank[:, 6, h * EP:(h + 1) * EP], run_max[0:EP, 0, h * P:(h + 1) * P], ident[0:EP, 0:EP])
                last.then_inc(s_acct, 1)
                pe.wait_ge(s_mk, w * 2 + 2)
                pe.wait_ge(s_win, w * 8 + 1)
                pe.matmul(bank[:, 0, 0:HID + 4], none16[0:EP, 0:P], none16[0:EP, :], start=True, stop=False)

            def scatter(w, c, ch, cs):
                for b in range(2):
                    pe.wait_ge(s_dt, ch * 2 + (b + 3))
                    pe.wait_ge(s_got_free, ch * 2 + (b + 1))
                    for q in range(2):
                        for n, part in enumerate((m_h, m_l)):
                            last = pe.matmul(bank[0:EP, 4 + b, q * 5:(q + 1) * 5], by_dst[b][:, q * EP:(q + 1) * EP], part,
                                             start=n == 0, stop=n == 1)
                    last.then_inc(s_pick, 1)
                for b in range(2):
                    pe.wait_ge(s_pl, cs * 2 + (b + 1))
                    for q in range(2):
                        for part in (wx_h, wx_l):
                            last = pe.matmul(bank[:, 0, 0:HID + 4], to_dst[b][0:EP, q, :], part[b][0:EP, q, :], start=False, stop=False)
                    last.then_inc(s_scat, 1)

            def close(w, ch, cm, cs):
                pe.matmul(bank[:, 0, 0:HID + 4], none16[0:EP, 0:P], none16[0:EP, :], start=False, stop=True).then_inc(s_agg, 1)
            over_windows(pe, nothing_more, pick_xr, turn_max, scatter, close)

            pe.wait_ge(s_win, 8 * T + 2)
            for k in range(2):
                for t in range(T):
                    at = k * T + t
                    last = pe.transpose(bank[:, at // 4, (at % 4) * P:(at % 4 + 1) * P], sums[:, t, k * P:(k + 1) * P], ident[:, :])
            last.then_inc(s_aggt, 1)
            pe.wait_ge(s_w, PARTS["L3_gnn_W_up"])
            pe.wait_ge(s_aggl, 1)

            def out3(i, j):
                if not isinstance(i, int) or i >= 2:
                    pe.wait_ge(s_upd, i + (6 * T - 1))
                tile_row(j, lambda k, a: aggT[a][:, k, ds(i * P, P)], lambda k, b: w_upp[b][:, k, :], 2, None,
                         lambda: turn_before(i, 7 * T))
            pairs(pe, T, out3)
            turn(T - 1, 7 * T)

            pe.wait_ge(s_turn, 8 * T)
            pe.wait_ge(s_upd, 7 * T)
            pe.wait_ge(s_router1, 2)

            def route3(t):
                product(bank[:, 3, ds(t * 8, 8)], lambda k, a: xT[a][:, k, ds(t * P, P)], lambda k, b: router[b][:, k, :],
                        0, K, K).then_inc(s_logit, 1)
            singles(pe, T, route3)

            def hidden3(x3, j):
                pe.wait_ge(s_w, x3 * 12 + (PARTS["L3_gnn_W_up"] + K))
                for unit3 in range(U3):
                    f, c = unit3 // 3, unit3 % 3
                    a, n = THIRD[c]
                    if not isinstance(x3, int) or x3 or unit3 >= 2:
                        pe.wait_ge(s_h3, x3 * U3 + (unit3 - 1))
                    for to, at in ((4, 0), (6, HID)):
                        mm = product(bank[:, to + unit3 % 2, 0:n], lambda k, p: gu[j][p][:, k, at + f * P:at + (f + 1) * P],
                                     lambda k, p: xT[p][:, k, a:a + n], 0, K, K)
                    mm.then_inc(s_gu, 1)

            def out3x(x3, j):
                pe.wait_ge(s_w, x3 * 12 + (PARTS["L3_gnn_W_up"] + 12))
                pe.wait_ge(s_h3l, x3 * U3 + U3)
                pe.sem_inc(s_met, 1)

                def tile(i, b):
                    pe.wait_ge(s_upd, x3 * T + i + (7 * T - 1))
                    tile_row(b, lambda k, p: h3[j][p][:, k, ds(i * P, P)], lambda k, p: dn[j][p][:, k, :], 2)
                pairs(pe, T, tile, 0)
            hidden3(0, 0)
            hidden3(1, 1)
            pe.wait_ge(s_gates3, 1)
            out3x(0, 0)
            with pe.Fori(1, E3 // 2) as h:
                for j in range(2):
                    hidden3(h * 2 + j, j)
                    out3x(h * 2 + (j - 1), 1 - j)
            hidden3(E3, 0)
            out3x(E3 - 1, 1)
            out3x(E3, 0)



_INS = ['x', 'src', 'dst', 'dst_chunks', 'L0_gnn_W', 'L0_gnn_b', 'L0_ffn_Wm', 'L0_ffn_bm', 'L0_ffn_expert_emb', 'L0_ffn_W1', 'L0_ffn_b1',
        'L0_ffn_W2', 'L0_ffn_b2', 'L0_ffn_Wo', 'L0_ffn_bo', 'L1_gnn_W', 'L1_gnn_a', 'L1_ffn_router_w', 'L1_ffn_w1', 'L1_ffn_b1',
        'L1_ffn_w2', 'L1_ffn_b2', 'L2_ffn_b_in', 'L2_gnn_WT', 'L2_gnn_b', 'L2_ffn_W_in', 'L2_ffn_W_inT', 'L2_ffn_W_out', 'L2_ffn_b_out',
        'dst_row', 'L3_gnn_rms_w', 'L3_gnn_W_down', 'L3_gnn_Wl', 'L3_gnn_Wr', 'L3_gnn_att', 'L3_gnn_W_up', 'L3_gu', 'L3_down',
        'L3_ffn_router_wT', 'L3_ffn_routing_bias']


def kernel(**inputs):
    import numpy as _np
    import concourse.bacc as _bacc
    from concourse import mybir as _mybir
    from concourse.bass_utils import run_bass_kernel_spmd as _run

    laid = {k: _np.ascontiguousarray(v) for k, v in inputs.items()}
    laid["dst_row"] = laid["dst"].reshape(1, EDGES)
    laid["L3_gnn_att"] = laid["L3_gnn_att"].reshape(1, HID)
    laid["dst_chunks"] = laid["dst"].reshape(NC, EDGES // NC)
    for name in ("src", "dst"):
        laid[name] = _np.ascontiguousarray(laid[name].reshape(ET, EP).T)
    laid["L0_ffn_W1"] = _np.ascontiguousarray(laid["L0_ffn_W1"].transpose(1, 0, 2).reshape(P, DIM))
    laid["L0_ffn_W2"] = laid["L0_ffn_W2"].reshape(DIM, P)
    laid["L2_gnn_WT"] = _np.ascontiguousarray(laid["L2_gnn_W"].T)
    laid["L2_ffn_W_inT"] = _np.ascontiguousarray(laid["L2_ffn_W_in"].T)
    gate = _np.concatenate([laid["L3_ffn_wg"], laid["L3_ffn_sg_w"][None]]).transpose(0, 2, 1)
    up = _np.concatenate([laid["L3_ffn_wu"], laid["L3_ffn_su_w"][None]]).transpose(0, 2, 1)
    laid["L3_gu"] = _np.ascontiguousarray(_np.concatenate([gate, up], axis=2).reshape(-1, 2 * HID))
    down = _np.concatenate([laid["L3_ffn_wd"], laid["L3_ffn_sd_w"][None]]).transpose(0, 2, 1)
    laid["L3_down"] = _np.ascontiguousarray(down.reshape(-1, DIM))
    laid["L3_ffn_router_wT"] = _np.ascontiguousarray(laid["L3_ffn_router_w"].T)
    for name in ("L0_ffn_bm", "L0_ffn_b1", "L1_ffn_b1", "L2_ffn_b_in", "L3_gnn_rms_w"):
        laid[name] = _np.ascontiguousarray(laid[name].reshape(-1, P).T)
    nc = _bacc.Bacc("TRN2", target_bir_lowering=False, num_devices=1)
    arrays, args = {}, {}
    for name in _INS:
        a = laid[name]
        arrays[f"in_{name}_dram"] = a
        args[name] = nc.dram_tensor(f"in_{name}_dram", a.shape, _mybir.dt.from_np(a.dtype), kind="ExternalInput").ap()
    out = nc.dram_tensor("out_0_dram", (NODES, DIM), _mybir.dt.float32, kind="ExternalOutput").ap()
    program(nc, args, out)
    r = _run(nc, [arrays], core_ids=[0])
    return r.results[0]["out_0_dram"]
```

```python
from contextlib import ExitStack

import concourse.bass as bass
from concourse import mybir

F32 = mybir.dt.float32
F16 = mybir.dt.float16
BF16 = mybir.dt.bfloat16
U16 = mybir.dt.uint16
I32 = mybir.dt.int32
ALU = mybir.AluOpType
ACT = mybir.ActivationFunctionType
AX_X = mybir.AxisListType.X
RMAX = bass.bass_isa.ReduceOp.max

P = 128
SIZE = {F32: 4, I32: 4, F16: 2, BF16: 2, U16: 2}

NODES = 1250
F = 512
DIM = 1024
E3 = 8
HID = 256
EDGES = 40000
T = -(-NODES // P)
NP = T * P
K = DIM // P
LAST = NODES - (T - 1) * P
EP = 125
ET = EDGES // EP
CHUNK = 4
NC = ET // CHUNK
HALF = 512
THIRD = [(0, 427), (427, 427), (854, 426)]
LN_EPS = 1e-5
RMS_EPS = 1e-6
BIG = 3.0e38
ROUND = 1.5 * 2.0 ** 23


def ds(i, n=1):
    return bass.ds(i, n)


def wait(e, sem, value):
    if isinstance(value, int) and value <= 0:
        return
    e.wait_ge(sem, value)


def pairs(e, n, body, first=2, last=0):
    for i in range(first):
        body(i, i % 2)
    if n - last > first:
        with e.Fori(first // 2, (n - last) // 2) as h:
            for j in range(2):
                body(h * 2 + j, j)
    for i in range(n - last, n):
        body(i, i % 2)


def singles(e, n, body, first=1, last=0):
    for i in range(first):
        body(i)
    if n - last > first:
        with e.Fori(first, n - last) as i:
            body(i)
    for i in range(n - last, n):
        body(i)


def program(nc, A, out):
    xl_table = nc.dram_tensor("xl_table", (NP, HID), F32).ap()
    ctx = ExitStack()
    with ctx:
        def sb(name, shape, dt):
            return ctx.enter_context(nc.sbuf_tensor(name, shape, dt))

        def sem(name):
            return ctx.enter_context(nc.semaphore(name))

        def view(region, start, shape, dt):
            n = 1
            for s in shape:
                n *= s
            words = -(-n * SIZE[dt] // 4)
            ap = region[:, start // 4:start // 4 + words]
            if dt is not F32:
                ap = ap.bitcast(dt)[:, 0:n]
            if len(shape) == 2:
                ap = ap.rearrange("p (a b) -> p a b", a=shape[0])
            return ap

        x = sb("x", [P, T, DIM], F32)
        adj = sb("adj", [P, T, NP], U16)
        turned = sb("turned", [P, K * NP], F32)
        hidden = sb("hidden", [P, T * DIM], F32)
        weights = sb("weights", [P, K * DIM], F32)
        stage = sb("stage", [P, 2, HALF], F32)
        coef = sb("coef", [P, 2 * NP], F32)
        xhat = sb("xhat", [P, DIM], F32)
        work = sb("work", [P, NP], F32)
        bias = sb("bias", [P, NP], F32)
        cols = sb("cols", [P, 3 * K + 4], F32)

        xT_h = view(turned, 0, [K, NP], F16)
        xT_l = view(turned, K * NP * 2, [K, NP], BF16)
        h_h = view(hidden, 0, [T, DIM], F16)
        h_l = view(hidden, T * DIM * 2, [T, DIM], BF16)
        w_h = view(weights, 0, [K, DIM], F16)
        w_l = view(weights, K * DIM * 2, [K, DIM], BF16)
        coef_h = [view(coef, b * NP * 4, [T, P], F16) for b in range(2)]
        coef_l = [view(coef, b * NP * 4 + NP * 2, [T, P], BF16) for b in range(2)]
        row_h = view(work, 0, [NP], F16)
        row_l = view(work, NP * 2, [NP], BF16)
        z = view(work, 0, [T, P], F32)
        hT_h = view(hidden, 0, [K, NP], F16)
        hT_l = view(hidden, K * NP * 2, [K, NP], BF16)
        fT = (view(hidden, 0, [F // P, NP], F16), view(hidden, F // P * NP * 2, [F // P, NP], BF16))
        half_a = (view(weights, 0, [K, F], F16), view(weights, K * DIM * 2, [K, F], BF16))
        half_b = (view(weights, K * F * 2, [F // P, DIM], F16), view(weights, K * DIM * 2 + K * F * 2, [F // P, DIM], BF16))
        w1 = (view(coef, 0, [DIM], F16), view(coef, 2048, [DIM], BF16))
        w2 = (view(coef, 4096, [K, P], F16), view(coef, 6144, [K, P], BF16))
        b2_f = view(coef, 8192, [P], F32)
        b2 = (view(coef, 8704, [P], F16), view(coef, 8960, [P], BF16))
        emb_f = view(coef, 9216, [16], F32)
        emb = (view(coef, 9280, [16], F16), view(coef, 9312, [16], BF16))
        pick = view(xhat, 0, [K, P], F16)
        N3 = THIRD[0][1]
        hid = [(view(turned, b * K * N3 * 4, [K, N3], F16), view(turned, b * K * N3 * 4 + K * N3 * 2, [K, N3], BF16))
               for b in range(2)]
        at = 2 * K * N3 * 4
        gm = [(view(turned, at + b * 1712, [N3], F16), view(turned, at + b * 1712 + 856, [N3], BF16)) for b in range(3)]
        gT = (view(turned, 7 * NP * 4, [NP], F16), view(turned, 7 * NP * 4 + NP * 2, [NP], BF16))
        up_buf = [view(work, a * 4, [n], F32) for a, n in THIRD]
        unit = [view(work, b * 1712, [N3], F32) for b in range(2)] + [view(turned, at + 3 * 1712, [N3], F32)]
        GROUPS = T * K
        lg = view(work, 0, [GROUPS, 16], F32)
        gates_g = view(turned, 0, [GROUPS, 16], F32)
        gates = view(turned, 0, [T, P], F32)
        t_c = view(turned, 5120, [GROUPS, 16], F32)
        t_o = view(turned, 10240, [GROUPS, 16], F32)
        t_m = view(turned, 15360, [GROUPS, 16], F32)
        g_m = view(turned, 20480, [GROUPS], F32)
        g_z = view(turned, 20800, [GROUPS], F32)
        g_c = view(turned, 21120, [GROUPS], F32)
        spare = view(coef, 0, [DIM], F32)
        router_f = view(coef, 0, [K, 8], F32)
        router = (view(coef, 256, [K, 8], F16), view(coef, 384, [K, 8], BF16))
        r_l = view(coef, 512, [T, 8], F32)
        r_e = view(coef, 832, [T, 8], F32)
        r_o = view(coef, 1152, [T, 8], F32)

        edge_i = view(hidden, 0, [2, ET], I32)
        edge_f = view(hidden, 2560, [2, ET], F32)
        span_i = view(hidden, 5120, [EDGES // NC], I32)
        span_f = view(hidden, 7120, [EDGES // NC], F32)
        src_row = view(hidden, 9120, [NP], F16)
        dst_row = view(hidden, 11680, [P], F16)
        src_hot = [view(hidden, 12288 + b * 2560, [NP], F16) for b in range(CHUNK)]
        dst_hot = [view(hidden, 22528 + b * 256, [P], F16) for b in range(CHUNK)]
        nothing = view(hidden, 23552, [HALF], F16)

        ident = sb("ident", [P, P], F32)
        ident16 = sb("ident16", [P, P], F16)
        identb = sb("identb", [P, P], BF16)
        ones = sb("ones", [P, P], F32)
        tiny = sb("tiny", [P, 312], F32)
        used = [0]

        def small(shape, dt):
            n = 1
            for s in shape:
                n *= s
            begin = used[0]
            used[0] += -(-n * SIZE[dt] // 4)
            assert used[0] <= 312
            return view(tiny, begin * 4, shape, dt)

        one16 = small([2], F16)
        win_lo = small([T], F32)
        win_neg = small([T], F32)
        chunk_no = small([1], F32)
        span = small([2], F32)
        hit = small([2 * T], F32)
        hit_all = small([2 * T], F32)
        bounds = small([2 * T], I32)
        deg3 = small([T, 3], F32)
        deg_in = small([T], F32)
        deg_out = small([T], F32)
        deg_part = small([2, T], F32)
        dinv_in = small([T], F32)
        dinv_out = small([T], F32)
        bn = small([2, 6], F32)
        mv = small([2], F32)
        std = small([1], F32)
        rstd = small([1], F32)
        rank = small([16], F32)
        part_i = small([3], I32)
        part_f = small([2], F32)
        eight = small([K], F32)
        head_mask = small([K], F32)
        al = small([T], F32)
        ar = small([T], F32)
        low2 = small([2], F32)
        low2_all = small([2], F32)
        shift = small([3], F32)
        r_s = small([3, T], F32)
        spacer = small([3], F32)
        eps = small([2], F32)
        low_blocks = small([1], I32)

        used_late = [0]

        def late(shape, dt):
            n = 1
            for s in shape:
                n *= s
            begin = used_late[0]
            used_late[0] += -(-n * SIZE[dt] // 4)
            assert used_late[0] <= NP - DIM
            return view(bias, (DIM + begin) * 4, shape, dt)

        w_max = late([16], F32)
        w_amax = late([8], F32)
        w_quant = late([8], F32)
        w_step = late([8], F32)
        magic = late([1], F32)
        x_max = late([2], F32)
        x_max_all = late([1], F32)
        x_quant = late([1], F32)
        x_step = late([1], F32)
        up_scale = late([F // P], F32)
        h_max = late([3 * F // P], F32)
        h_max1 = late([1], F32)
        h_max_all = late([1], F32)
        h_quant = late([1], F32)
        h_scale = late([F // P], F32)
        w_row = view(work, F * 4, [F], F32)
        w_diag = view(work, 0, [F // P, P], F32)
        xT_f = view(turned, 0, [K, NP], F32)
        hid_f = view(turned, 0, [F // P, NP], F32)

        down = (view(weights, 16384, [K, HID], F16), view(weights, 20480, [K, HID], BF16))
        wlr = (view(weights, 24576, [2, 2 * HID], F16), view(weights, 26624, [2, 2 * HID], BF16))
        w_upp = (view(weights, 0, [2, DIM], F16), view(weights, 4096, [2, DIM], BF16))
        xdT = (view(hidden, 0, [2, NP], F16), view(hidden, 5120, [2, NP], BF16))
        lr = view(hidden, 10240, [T, 2 * HID], F32)
        xr_h = view(hidden, 30720, [T, HID], F16)
        xr_l = view(hidden, 35840, [T, HID], BF16)
        aggT = xdT
        adj_words = adj[:, :, :].rearrange("p a b -> p (a b)").bitcast(F32)
        region = {"turned": (turned, 0, K * NP * 4), "adj": (adj, 0, T * NP * 2)}

        def area(which, shape, dt):
            base, begin, end = region[which]
            n = 1
            for s in shape:
                n *= s
            region[which] = (base, begin + -(-n * SIZE[dt] // 4) * 4, end)
            assert region[which][1] <= end
            if which == "adj":
                base = adj_words
            return view(base, begin, shape, dt)
        xl_got = [area("turned", [2, HID], F32) for b in range(2)]
        z3 = [area("turned", [2, HID + 4], F32) for b in range(2)]
        zT = [area("turned", [2 * 2 * EP], F32) for b in range(2)]
        zTb = [area("turned", [2 * 2 * EP], BF16) for b in range(2)]
        away = [area("turned", [2 * EP], F32) for b in range(2)]
        masked = area("turned", [4, 2 * EP], F32)
        att_cols = area("adj", [2, 4], F32)
        att_wide = area("turned", [4, P], BF16)
        to_dst = [area("turned", [2, P], F32) for b in range(2)]
        by_dst = [area("turned", [2 * EP], F16) for b in range(2)]
        dst_in = [area("turned", [2 * EP], I32) for b in range(2)]
        dst_no = area("adj", [P], F32)
        none16 = area("adj", [HID + 4], F16)
        e_all = area("adj", [CHUNK + ET, 4], F32)
        src_i = area("adj", [ET], I32)
        dst_i = area("adj", [ET], I32)
        dst_f = area("adj", [ET], F32)
        sums = area("adj", [T, HID], F32)
        s_now = [area("adj", [2, 4], F32) for b in range(2)]
        idx_now = [area("adj", [2], I32) for b in range(2)]
        e_self = area("adj", [T, 4], F32)
        part_no = area("adj", [1], F32)
        m_now = area("adj", [4], F32)
        m_tile = area("adj", [2, 4], F32)
        m_b = area("adj", [5], BF16)
        att_col = area("adj", [2], F32)
        p_self = area("adj", [4], F32)
        den = area("adj", [4], F32)
        own = area("adj", [HID], F32)
        att = bias[:, 0:HID]

        sets = ((weights, 8192), (adj_words, 0))
        gu = [(view(r, at, [K, 2 * HID], F16), view(r, at + 8192, [K, 2 * HID], BF16)) for r, at in sets]
        dn = [(view(r, at + 16384, [2, DIM], F16), view(r, at + 20480, [2, DIM], BF16)) for r, at in sets]
        h3 = [(view(hidden, 10240 * (b + 1), [2, NP], F16), view(hidden, 10240 * (b + 1) + 5120, [2, NP], BF16)) for b in range(2)]
        route_bias = late([8], F32)
        gates3 = late([T, E3 + 1], F32)

        bank = ctx.enter_context(nc.psum_tensor("bank", [P, 8, HALF], F32))
        ps_out = [bank[:, 2 * b:2 * b + 2, :].rearrange("p a b -> p (a b)") for b in range(2)]
        ps_turn = bank[:, 4:6, :].rearrange("p a (b c) -> p (a b) c", c=P)

        s_x = sem("x_loaded")
        s_pad = sem("pad_cleared")
        s_edges = sem("edges_loaded")
        s_const = sem("constants_made")
        s_pool = sem("pool_step")
        s_v = sem("vector_step")
        s_span = sem("hits_known")
        s_hits = sem("hits_spread")
        s_bounds = sem("bounds_known")
        s_hot = sem("onehots_made")
        s_hot_free = sem("onehots_free")
        s_adj = sem("adj_window_summed")
        s_adj_free = sem("adj_window_stored")
        s_deg = sem("degrees_known")
        s_most = sem("largest_degree")
        s_most_all = sem("largest_degree_spread")
        s_lowb = sem("low_blocks_known")
        s_sq = sem("degree_roots")
        s_dinv = sem("degree_factors")
        s_out = sem("product_ready")
        s_out_free = sem("product_free")
        s_hh = sem("high_part_kept")
        s_upd = sem("residual_updated")
        s_bn = sem("stats_done")
        s_mv = sem("moments_done")
        s_std = sem("std_done")
        s_rstd = sem("rstd_done")
        s_xhat = sem("xhat_done")
        s_turned = sem("tile_turned")
        s_turn_h = sem("turned_high_kept")
        s_turn = sem("turned_split")
        s_stage = [sem(f"stage{b}_loaded") for b in range(2)]
        s_wh = sem("weight_high_kept")
        s_w = sem("weight_split")
        s_row_h = sem("row_high_kept")
        s_row = sem("row_split")
        s_cnt = sem("outs_counted")
        s_sum = sem("sum_scaled")
        s_rowt = sem("row_turned")
        s_coef_h = sem("coef_high_kept")
        s_coef = sem("coef_ready")
        s_bias = sem("bias_loaded")
        s_cols = sem("columns_loaded")
        s_small = sem("small_weights_loaded")
        s_up = sem("up_unit_ready")
        s_up_free = sem("up_unit_free")
        s_up_h = sem("up_high_kept")
        s_emb = sem("embedding_split")
        s_b2 = sem("b2_split")
        s_logit = sem("logits_ready")
        s_lg = sem("logits_shifted")
        s_ex = sem("logits_exponentiated")
        s_gate = sem("gates_ready")
        s_gate_t = sem("gates_turned")
        s_gth = sem("turned_gates_high_kept")
        s_gt = sem("turned_gates_split")
        s_gm = sem("head_gates_masked")
        s_unit = sem("expert_unit_ready")
        s_gelu = sem("expert_gelu_done")
        s_spread = sem("gate_spread_ready")
        s_gated = sem("expert_gated")
        s_hid_h = sem("expert_high_kept")
        s_hid = sem("expert_hidden_split")
        s_comb_mm = sem("expert_sum_ready")
        s_comb_h = sem("expert_sum_high_kept")
        s_comb = sem("expert_sum_split")
        s_diag = sem("al_on_diagonals")
        s_al_row = sem("al_row_ready")
        s_al = sem("al_row_kept")
        s_mins = sem("score_minima")
        s_mins_all = sem("score_minima_spread")
        s_shift = sem("shift_known")
        s_epsr = sem("eps_scaled")
        s_z = sem("scores_leaky")
        s_ez = sem("scores_exponentiated")
        s_cz = sem("scores_counted")
        s_zs = sem("scores_added")
        s_step1 = sem("layer1_update_step")
        s_neg = sem("negative_part_ready")
        s_eneg = sem("negative_part_exponentiated")
        s_hid_l = sem("hidden_split")
        s_router1 = sem("router_split")
        s_wscale = sem("weight_scales")
        s_wq = sem("weight_quantise_step")
        s_row2 = sem("scale_row_ready")
        s_row2k = sem("scale_row_kept")
        s_xm = sem("x_maximum_step")
        s_max1 = sem("x_maximum")
        s_max1_all = sem("x_maximum_spread")
        s_q = sem("x_scaled")
        s_q_h = sem("x_high_kept")
        s_q_l = sem("x_quantised")
        s_max2 = sem("hidden_maximum")
        s_max2_all = sem("hidden_maximum_spread")
        s_xb = sem("bias_added")
        s_hq = sem("hidden_scaled")
        s_hq_h = sem("hidden_high_kept")
        s_hq_l = sem("hidden_quantised")
        s_rms = sem("rms_weight_multiplied")
        s_idx = sem("edges_reloaded")
        s_aux = sem("layer3_constants")
        s_lr = sem("xl_xr_kept")
        s_xrh = sem("xr_high_kept")
        s_xr = sem("xr_split")
        s_table = sem("xl_table_stored")
        s_row_in = [sem(f"dst_row{b}_loaded") for b in range(2)]
        s_dt = sem("dst_onehots_made")
        s_pick = sem("dst_values_picked")
        s_idx_now = sem("indices_copied")
        s_got = [[sem(f"xl_rows{b}_{q}_gathered") for q in range(2)] for b in range(2)]
        s_tile_free = sem("first_xl_rows_free")
        s_got_free = sem("xl_rows_free")
        s_score = sem("score_step")
        s_win = sem("window_step")
        s_att = sem("att_laid")
        s_clear = sem("window_maxima_cleared")
        s_mk = sem("window_maxima_rounded")
        s_fifth = sem("sums_times_slope")
        s_lkb = sem("leaky_sums_rounded")
        s_spread3 = sem("scores_spread")
        s_maxd = sem("scores_compared")
        s_selfp = sem("self_weight_ready")
        s_sub = sem("score_masked")
        s_s = sem("score_shifted")
        s_p = sem("weight_exponentiated")
        s_scat = sem("half_scattered")
        s_agg = sem("window_summed")
        s_aggt = sem("sums_turned")
        s_aggh = sem("sums_high_kept")
        s_aggl = sem("sums_split")
        s_gates3 = sem("gates3_ready")
        s_gu = sem("gate_up_ready")
        s_silu = sem("silu_done")
        s_h3 = sem("hidden3_made")
        s_h3h = sem("hidden3_high_kept")
        s_h3l = sem("hidden3_split")
        s_met = sem("waits_met")
        s_store = sem("x_stored")

        LOADS = [
            ("L0_gnn_W", A["L0_gnn_W"], w_h, w_l, K, DIM, []),
            ("L0_ffn_Wm", A["L0_ffn_Wm"], w_h, w_l, K, DIM, [(s_out, T)]),
            ("L0_ffn_W1", A["L0_ffn_W1"], w1[0].rearrange("p (a n) -> p a n", a=1), w1[1].rearrange("p (a n) -> p a n", a=1),
             1, DIM, [(s_out, 2 * T), (s_cnt, 3 * T)]),
            ("L0_ffn_W2", A["L0_ffn_W2"], w2[0], w2[1], K, P, []),
            ("L0_ffn_Wo", A["L0_ffn_Wo"], w_h, w_l, K, DIM, [(s_up, 3 * K)]),
            ("L1_gnn_W", A["L1_gnn_W"], w_h, w_l, K, DIM, [(s_out, 3 * T)]),
            ("L1_ffn_w1", A["L1_ffn_w1"], half_a[0], half_a[1], K, F, [(s_out, 4 * T)]),
            ("L1_ffn_w2", A["L1_ffn_w2"], half_b[0], half_b[1], F // P, DIM, []),
            ("maxima_in", A["L2_ffn_W_inT"], w_max[:, 0:8], "max", F // P, DIM, [(s_upd, 3 * T)]),
            ("maxima_out", A["L2_ffn_W_out"], w_max[:, 8:16], "max", F // P, DIM, []),
            ("L2_gnn_W_a", A["L2_gnn_WT"][0:HALF, :], w_h[:, 0:K // 2, :], w_l[:, 0:K // 2, :], K // 2, DIM, [(s_up, 3 * K + 3 * F // P)]),
            ("L2_gnn_W_b", A["L2_gnn_WT"][HALF:DIM, :], w_h[:, K // 2:K, :], w_l[:, K // 2:K, :], K // 2, DIM, [(s_out, 6 * T)]),
            ("L2_ffn_W_in", A["L2_ffn_W_in"], half_a[0], "row", K, F, [(s_out, 7 * T), (s_row2k, 1)]),
            ("L2_ffn_W_out", A["L2_ffn_W_out"], half_b[0], "col", F // P, DIM, []),
            ("L3_gnn_W_down", A["L3_gnn_W_down"], down[0], down[1], K, HID, [(s_cols, 80)]),
            ("L3_gnn_Wl", A["L3_gnn_Wl"], wlr[0][:, :, 0:HID], wlr[1][:, :, 0:HID], 2, HID, []),
            ("L3_gnn_Wr", A["L3_gnn_Wr"], wlr[0][:, :, HID:2 * HID], wlr[1][:, :, HID:2 * HID], 2, HID, []),
            ("L3_gnn_W_up", A["L3_gnn_W_up"], w_upp[0], w_upp[1], 2, DIM, [(s_up, 3 * K + 6 * F // P)]),
        ]
        PARTS = {}
        n = 0
        for name, _, _, _, blocks, columns, _ in LOADS:
            n += blocks * max(1, columns // HALF)
            PARTS[name] = n

        SPLIT = n - sum(l[4] * max(1, l[5] // HALF) for l in LOADS if isinstance(l[3], str))

        def load_weights(e, store, first, end):
            names = [load[0] for load in LOADS]
            begin = names.index(first)
            n = PARTS[names[begin - 1]] if begin else 0
            if store:
                wait(e, s_w, n)
            for name, dram, high, low, blocks, columns, free in LOADS[begin:names.index(end) if end else None]:
                if store:
                    for what, value in free:
                        e.wait_ge(what, value)
                src = dram.rearrange("(k p) n -> p k n", p=P)
                width = min(columns, HALF)
                per = columns // width

                skipped = n - sum(l[4] * max(1, l[5] // HALF) for l in LOADS[:names.index(name)] if isinstance(l[3], str))

                def body(h, name=name, n=n, skipped=skipped, high=high, low=low, src=src, width=width, per=per):
                    for b in range(2):
                        k, c = (h, b * width) if per == 2 else (h * 2 + b, 0)
                        m = n + h * 2 + b
                        part = (slice(None), ds(k, 1), slice(c, c + width))
                        flat = stage[:, b, 0:width]
                        if store:
                            e.wait_ge(s_stage[b], (h + n // 2 + 1) * 16)
                        if store and isinstance(low, str) and low == "max":
                            e.tensor_reduce(high[:, h * 2 + b:h * 2 + b + 1], flat, AX_X, ALU.max,
                                            apply_absolute_value=True).then_inc(s_w, 1)
                        elif store and isinstance(low, str):
                            q = h * 6 + b * 3 + (0 if low == "row" else 3 * K)
                            scale = w_row if low == "row" else w_quant[:, ds(F // P + k)].broadcast_to([P, width])
                            e.tensor_tensor(flat, flat, scale, ALU.mult).then_inc(s_wq, 1)
                            e.wait_ge(s_wq, q + 1)
                            e.tensor_tensor(flat, flat, magic[:, 0:1].broadcast_to([P, width]), ALU.add).then_inc(s_wq, 1)
                            e.wait_ge(s_wq, q + 2)
                            e.tensor_tensor(high[part], flat, magic[:, 0:1].broadcast_to([P, width]), ALU.subtract).then_inc(s_wq, 1)
                            e.wait_ge(s_wq, q + 3)
                            e.sem_inc(s_w, 1)
                        elif store:
                            if name == "L3_gnn_W_down":
                                e.tensor_tensor(flat, flat, cols[:, k:k + 1].broadcast_to([P, width]), ALU.mult).then_inc(s_rms, 1)
                                e.wait_ge(s_rms, k + 1)
                            e.tensor_copy(high[part], flat).then_inc(s_wh, 1)
                            e.wait_ge(s_wh, h * 2 + (b + 1 + skipped))
                            e.tensor_tensor(low[part], flat, high[part], ALU.subtract).then_inc(s_w, 1)
                        else:
                            wait(e, s_w, m - 1)
                            e.dma_start(flat, src[part]).then_inc(s_stage[b], 16)

                steps = blocks * per // 2
                singles(e, steps, body, first=steps if name in ("maxima_in", "maxima_out", "L2_ffn_W_out", "L3_gnn_W_down") else 1)
                n += blocks * per

        def wait_own(e, what, value):
            e.wait_ge(what, value)
            if not isinstance(value, int):
                e.wait_ge(s_const, 1)

        def window_bounds(e, w):
            return (e.value_load(bounds[0:1, ds(w)], min_val=0, max_val=NC - 1),
                    e.value_load(bounds[0:1, ds(w + T)], min_val=1, max_val=NC))

        U3 = 6

        def load_experts(e, store):
            n = PARTS["L3_gnn_W_up"]

            def expert(x3, j):
                for name, (high, low), blocks in (("L3_gu", gu[j], K), ("L3_down", dn[j], 2)):
                    src = A[name].rearrange("(k p) n -> p k n", p=P)
                    if store:
                        if name == "L3_gu":
                            if isinstance(x3, int) and x3 < 2:
                                e.wait_ge(s_aggl if j else s_out, 1 if j else 10 * T)
                            else:
                                e.wait_ge(s_gu, x3 * U3 - U3)
                        else:
                            if isinstance(x3, int) and x3 < 2:
                                pass
                            else:
                                e.wait_ge(s_out, x3 * T + 10 * T)
                    for part in range(blocks if name == "L3_gu" else 2 * blocks):
                        at = part + (0 if name == "L3_gu" else K)
                        k, c = (part, 0) if name == "L3_gu" else (part // 2, part % 2 * HALF)
                        b = at % 2
                        flat = stage[:, b, :]
                        if store:
                            e.wait_ge(s_stage[b], (x3 * 6 + (at // 2 + n // 2 + 1)) * 16)
                            e.sem_inc(s_met, 1)
                            e.tensor_copy(high[:, k, c:c + HALF], flat).then_inc(s_wh, 1)
                            e.wait_ge(s_wh, x3 * 12 + (at + 1 + SPLIT))
                            e.tensor_tensor(low[:, k, c:c + HALF], flat, high[:, k, c:c + HALF], ALU.subtract).then_inc(s_w, 1)
                        else:
                            e.wait_ge(s_w, x3 * 12 + (n + at - 1))
                            e.dma_start(flat, src[:, ds(x3 * blocks + k), c:c + HALF]).then_inc(s_stage[b], 16)
            pairs(e, E3 + 1, expert, 2, 1)

        def over_windows(e, begin, chunk_max, between, chunk_sum, end):
            ch, cm, cs = (e.alloc_register(f"layer3_{n}_chunks") for n in ("all", "max", "sum"))
            for r in (ch, cm, cs):
                e.reg_mov(r, 0)
            with e.Fori(0, T) as w:
                first, last = window_bounds(e, w)
                begin(w, e.snap(ch), e.snap(cm), e.snap(cs))
                with e.Fori(first, last) as c:
                    chunk_max(w, c, e.snap(ch), e.snap(cm))
                    e.reg_add(ch, ch, 1)
                    e.reg_add(cm, cm, 1)
                between(w, e.snap(ch), e.snap(cm), e.snap(cs), last)
                with e.Fori(first, last) as c:
                    chunk_sum(w, c, e.snap(ch), e.snap(cs))
                    e.reg_add(ch, ch, 1)
                    e.reg_add(cs, cs, 1)
                end(w, e.snap(ch), e.snap(cm), e.snap(cs))

        block = ctx.enter_context(nc.Block())

        @block.sync
        def _(sp):
            sp.dma_start(edge_i[0:EP, 0, :], A["src"]).then_inc(s_edges, 16)
            sp.dma_start(edge_i[0:EP, 1, :], A["dst"]).then_inc(s_edges, 16)
            sp.dma_start(span_i[0:NC, :], A["dst_chunks"]).then_inc(s_edges, 16)
            sp.wait_ge(s_pad, 1)
            sp.dma_start(x[:, 0:T - 1, :], A["x"][0:(T - 1) * P, :].rearrange("(t p) n -> p t n", p=P)).then_inc(s_x, 16)
            sp.dma_start(x[0:LAST, T - 1, :], A["x"][(T - 1) * P:NODES, :]).then_inc(s_x, 16)
            load_weights(sp, False, "L0_gnn_W", None)
            sp.wait_ge(s_coef, 3 * T)
            sp.dma_start(src_i[0:EP, :], A["src"]).then_inc(s_idx, 16)
            sp.dma_start(dst_i[0:EP, :], A["dst"]).then_inc(s_idx, 16)

            def store_xl(i):
                sp.wait_ge(s_lr, i + 1)
                sp.dma_start(xl_table[ds(i * P, P), :], lr[:, ds(i), 0:HID].rearrange("p a n -> p (a n)")).then_inc(s_table, 16)
            singles(sp, T, store_xl)

            def nothing_more(*_):
                pass

            def load_dst(w, c, ch, _):
                for b in range(2):
                    sp.wait_ge(s_dt, ch * 2 + (b + 1))
                    sp.dma_start(dst_in[b], A["dst_row"][:, ds(c * (CHUNK * EP) + b * 2 * EP, 2 * EP)].partition_broadcast(P)).then_inc(s_row_in[b], 16)
            over_windows(sp, nothing_more, load_dst, nothing_more, load_dst, nothing_more)
            load_experts(sp, False)
            with sp.Fori(0, T - 1) as i:
                sp.wait_ge(s_upd, i + ((7 + E3) * T + 1))
                sp.dma_start(out[ds(i * P, P), :], x[:, ds(i), :].rearrange("p a n -> p (a n)")).then_inc(s_store, 16)
            sp.wait_ge(s_upd, (7 + E3 + 1) * T)
            sp.dma_start(out[(T - 1) * P:NODES, :], x[0:LAST, T - 1, :]).then_inc(s_store, 16)
            sp.wait_ge(s_store, 16 * T)

        @block.gpsimd
        def _(pool):
            pool.memset(x[:, T - 1, :], 0.0).then_inc(s_pad, 1)
            pool.memset(ident[:, :], 0.0)
            pool.memset(ones[:, :], 1.0)
            pool.memset(one16[:, :], 1.0)
            pool.memset(eps[:, 0:1], LN_EPS)
            pool.memset(eps[:, 1:2], LN_EPS * RMS_EPS)
            pool.memset(nothing, 0.0)

            def count(to, pattern, base=0, channel_multiplier=0):
                return pool.iota(to, pattern, base=base, channel_multiplier=channel_multiplier,
                                 allow_small_or_imprecise_dtypes=True)
            count(win_lo[:, :], [[P, T]])
            count(win_neg[:, :], [[-P, T]])
            count(chunk_no[:, :], [[0, 1]], channel_multiplier=1)
            count(rank[:, :], [[-1, 16]], base=16)
            count(eight[:, :], [[1, K]])
            count(part_i[:, 0:1], [[0, 1]], channel_multiplier=1)
            count(src_row, [[1, NP]])
            count(dst_row, [[1, P]]).then_inc(s_pool, 1)
            pool.wait_ge(s_pool, 1)
            pool.affine_select(out=ident[:, :], in_=ident[:, :], compare_op=ALU.not_equal, fill=1.0, base=0,
                               pattern=[[-1, P]], channel_multiplier=1).then_inc(s_pool, 1)
            pool.wait_ge(s_pool, 2)
            pool.tensor_copy(identb[:, :], ident[:, :])
            pool.tensor_copy(ident16[:, :], ident[:, :]).then_inc(s_const, 1)
            pool.wait_ge(s_span, 1)
            pool.partition_all_reduce(hit_all[0:NC, :], hit[0:NC, :], NC, RMAX).then_inc(s_hits, 1)
            load_weights(pool, True, "L0_gnn_W", "L0_ffn_Wm")
            pool.wait_ge(s_most, 1)
            pool.partition_all_reduce(hit_all[:, 0:1], span[:, 0:1], P, RMAX).then_inc(s_most_all, 1)
            load_weights(pool, True, "L0_ffn_Wm", "L1_ffn_w1")
            pool.wait_ge(s_mins, 1)
            pool.partition_all_reduce(low2_all[:, :], low2[:, :], P, RMAX).then_inc(s_mins_all, 1)
            load_weights(pool, True, "L1_ffn_w1", "maxima_in")
            load_weights(pool, True, "L2_gnn_W_a", "L2_ffn_W_in")
            pool.memset(magic[:, :], ROUND).then_inc(s_pool, 1)
            pool.wait_ge(s_pool, 3)
            load_weights(pool, True, "L2_ffn_W_in", "L3_gnn_W_up")
            pool.wait_ge(s_max1, 1)
            pool.partition_all_reduce(x_max_all[:, :], x_max[:, 0:1], P, RMAX).then_inc(s_max1_all, 1)
            load_weights(pool, True, "L3_gnn_W_up", None)
            pool.wait_ge(s_max2, 1)
            pool.partition_all_reduce(h_max_all[:, :], h_max1[:, :], P, RMAX).then_inc(s_max2_all, 1)

            pool.wait_ge(s_coef, 3 * T)
            pool.memset(none16, 0.0)
            count(dst_no, [[1, P]])
            count(part_no, [[0, 1]], channel_multiplier=1)
            pool.memset(m_b, 1.0)
            pool.memset(att_cols, 0.0).then_inc(s_aux, 1)
            pool.wait_ge(s_idx, 32)
            pool.wait_ge(s_table, 16 * T)

            def nothing_more(*_):
                pass

            def rows_free(w, ch, cm, cs):
                pool.wait_ge(s_got_free, ch * 2 + 2)
                pool.sem_inc(s_met, 1)

            def gather(w, c, ch, _, free=s_got_free):
                for b in range(2):
                    for q in range(2):
                        pool.wait_ge(free if q else s_tile_free, ch * 2 + (b + 1))
                        pool.sem_inc(s_idx_now, 1)
                        pool.tensor_copy(idx_now[b][0:EP, q:q + 1], src_i[0:EP, ds(c * CHUNK + 2 * b + q)]).then_inc(s_idx_now, 1)
                        pool.wait_ge(s_idx_now, ch * 12 + (6 * b + 3 * q + 2))
                        pool.sem_inc(s_idx_now, 1)
                        pool.indirect_dma_start(xl_got[b][0:EP, q, :], None, xl_table[:, :],
                                                bass.IndirectOffsetOnAxis(ap=idx_now[b][0:EP, q:q + 1], axis=0),
                                                bounds_check=NP - 1).then_inc(s_got[b][q], 16)
            over_windows(pool, rows_free, lambda *at: gather(*at, free=s_pick), nothing_more, gather, nothing_more)
            load_experts(pool, True)
        @block.scalar
        def _(act):
            def store_window(w):
                wait_own(act, s_adj, w + 1)
                for c, (a, n) in enumerate(THIRD):
                    last = act.activation(adj[:, ds(w, 1), a:a + n], bank[:, c, 0:n], ACT.Copy,
                                          accum_out=deg3[:, ds(w, 1), c])
                last.then_inc(s_adj_free, 1)

            def std_of(i, base):
                wait_own(act, s_mv, base + i + 1)
                act.activation(std[:, :], mv[:, 1:2], ACT.Sqrt, bias=eps[:, 0:1]).then_inc(s_std, 1)

            def std3_of(i, base):
                wait_own(act, s_mv, base + i + 1)
                act.activation(std[:, :], mv[:, 1:2], ACT.Sqrt, scale=1.0 + RMS_EPS, bias=eps[:, 1:2]).then_inc(s_std, 1)

            def keep_turned_high(i, base):
                wait_own(act, s_turned, base + i + 1)
                act.activation(xT_h[:, :, ds(i * P, P)], ps_turn, ACT.Copy).then_inc(s_turn_h, 1)

            def project_scaled(i, j, idx, scale):
                wait_own(act, s_out, idx * T + i + 1)
                act.activation(h_h[:, ds(i), :], ps_out[j], ACT.Copy, scale=scale[:, ds(i)]).then_inc(s_hh, 1)

            for name, at, n in (("L0_ffn_bm", 0, K), ("L0_ffn_b1", K, K), ("L1_ffn_b1", 2 * K, F // P),
                                ("L2_ffn_b_in", 2 * K + F // P, F // P)):
                act.dma_start(cols[:, at:at + n], A[name]).then_inc(s_cols, 16)
            wait_own(act, s_const, 1)
            act.sem_inc(s_adj_free, 1)
            singles(act, T, store_window, first=0)
            wait_own(act, s_deg, 1)
            act.activation(dinv_in[:, :], deg_in[:, :], ACT.Sqrt, bias=ones[:, 0:1]).then_inc(s_sq, 1)

            std_of(0, 0)
            keep_turned_high(0, 0)

            def norm_project(i, j, more=True):
                if more:
                    std_of(i + 1, 0)
                    keep_turned_high(i + 1, 0)
                project_scaled(i, j, 0, dinv_in)
            pairs(act, T - 2, norm_project, first=0)
            norm_project(T - 2, 0)
            norm_project(T - 1, 1, False)

            def row_high(w):
                if not (isinstance(w, int) and w == 0):
                    wait_own(act, s_rowt, 2 * w)
                act.activation(row_h, adj[:, ds(w), :], ACT.Copy).then_inc(s_row_h, 1)

            def coef_high(w, j):
                wait_own(act, s_rowt, 2 * w + 1)
                if not isinstance(w, int) or w >= 2:
                    wait_own(act, s_cnt, 3 * w - 3)
                act.activation(coef_h[j], bank[:, 6:8, :].bitcast(F16)[:, :, 0:5 * P], ACT.Copy).then_inc(s_coef_h, 1)

            def keep_before(i, base):
                if not (isinstance(i, int) and i == 0):
                    keep_turned_high(i - 1, base)

            row_high(0)
            coef_high(0, 0)
            act.dma_start(bias[:, 0:DIM], A["L0_gnn_b"].partition_broadcast(P)).then_inc(s_bias, 16)

            def gather0(i, j, more=True):
                if more:
                    row_high(i + 1)
                    coef_high(i + 1, 1 - j)
                keep_before(i, T)
                std_of(i, T)
            pairs(act, T - 2, gather0)
            gather0(T - 2, 0)
            gather0(T - 1, 1, False)
            keep_turned_high(T - 1, T)

            wait_own(act, s_upd, T)
            act.dma_start(bias[:, 0:DIM], A["L0_ffn_bo"].partition_broadcast(P)).then_inc(s_bias, 16)
            wait_own(act, s_cnt, 3 * T)
            wait_own(act, s_out, 2 * T)
            act.dma_start(emb_f, A["L0_ffn_expert_emb"]).then_inc(s_small, 16)
            for head in range(K):
                act.dma_start(b2_f[head * 16:(head + 1) * 16, :], A["L0_ffn_b2"]).then_inc(s_small, 16)
            wait_own(act, s_cols, 64)

            def up0(f):
                for c, (a, n) in enumerate(THIRD):
                    wait_own(act, s_up, f * 3 + (c + 1))
                    act.activation(hT_h[:, ds(f), a:a + n], bank[:, c, 0:n], ACT.Identity, bias=cols[:, ds(f)]).then_inc(s_up_h, 1)
            singles(act, K, up0)

            wait_own(act, s_lg, 1)
            act.activation(gates_g, lg, ACT.Exp).then_inc(s_ex, 1)
            wait_own(act, s_gate_t, 1)
            act.activation(gT[0], bank[:, 0:3, :].rearrange("p a b -> p (a b)")[:, 0:NP], ACT.Copy).then_inc(s_gth, 1)

            def experts(hp, first=False):
                for jj in range(6):
                    s, b, c = hp * 6 + jj, jj % 2, jj % 3
                    head = hp * 2 + jj // 3
                    a, n = THIRD[c]

                    def gelu(j):
                        u = s * K + j
                        wait_own(act, s_unit, u + 1)
                        if not (first and jj == 0 and j < 3):
                            wait_own(act, s_hid, u - 2)
                        act.activation(unit[(jj * K + j) % 3][:, 0:n], bank[:, j % 2, 0:n], ACT.Gelu, bias=cols[:, K + j:K + j + 1]).then_inc(s_gelu, 1)

                    def high(j):
                        wait_own(act, s_gated, s * K + (j + 1))
                        if j == 0 and not (first and jj < 2):
                            wait_own(act, s_comb_mm, s - 1)
                        act.activation(hid[b][0][:, j, 0:n], unit[(jj * K + j) % 3][:, 0:n], ACT.Copy).then_inc(s_hid_h, 1)

                    gelu(0)
                    for j in range(1, K):
                        gelu(j)
                        high(j - 1)
                    high(K - 1)
                    if not (first and jj == 0):
                        comb_high(s - 1, 1 - b, (jj - 1) % 3, hp * 2 + (jj - 1) // 3)

            def comb_high(s, b, c, head):
                a, n = THIRD[c]
                wait_own(act, s_comb_mm, s + 1)
                act.activation(hT_h[:, ds(head), a:a + n], bank[:, 6 + b, 0:n], ACT.Copy).then_inc(s_comb_h, 1)
            experts(0, True)
            with act.Fori(1, K // 2) as hp:
                experts(hp)
            comb_high(3 * K - 1, 1, 2, K - 1)

            def out0(i, j):
                keep_before(i, 2 * T)
                std_of(i, 2 * T)
            pairs(act, T, out0)
            keep_turned_high(T - 1, 2 * T)

            wait_own(act, s_upd, 2 * T)
            act.dma_start(cols[:, 0:K], A["L3_gnn_rms_w"]).then_inc(s_cols, 16)
            act.dma_start(bias[:, 0:DIM], A["L1_gnn_a"][:, 0:DIM].partition_broadcast(P)).then_inc(s_bias, 16)
            act.dma_start(work[:, 0:DIM], A["L1_gnn_a"][:, DIM:2 * DIM].partition_broadcast(P)).then_inc(s_bias, 16)

            def project1(i, j):
                wait_own(act, s_out, i + (3 * T + 1))
                act.activation(h_h[:, ds(i), :], ps_out[j], ACT.Copy).then_inc(s_hh, 1)
            pairs(act, T, project1)
            wait_own(act, s_al_row, 1)
            for c, (a, n) in enumerate(THIRD):
                last = act.activation(bias[:, a:a + n], bank[:, 4 + c, 0:n], ACT.Copy)
            last.then_inc(s_al, 1)
            wait_own(act, s_shift, 1)
            act.activation(shift[:, 1:2], shift[:, 0:1], ACT.Exp).then_inc(s_epsr, 1)

            def coef1(i):
                wait_own(act, s_z, i + 1)
                act.activation(work[:, :], work[:, :], ACT.Exp, scale=-1.0, bias=shift[:, 0:1]).then_inc(s_ez, 1)

            def coef1_high(i, j):
                wait_own(act, s_cz, i + 1)
                if not isinstance(i, int) or i >= 2:
                    wait_own(act, s_out, i + (4 * T - 1))
                act.activation(coef_h[j], z, ACT.Copy).then_inc(s_coef_h, 1)
            coef1(0)
            coef1_high(0, 0)

            def gather1(i, j, more=True):
                if more:
                    coef1(i + 1)
                    coef1_high(i + 1, 1 - j)
                keep_before(i, 3 * T)
                wait_own(act, s_neg, i + 1)
                act.activation(xhat[:, :], xhat[:, :], ACT.Exp).then_inc(s_eneg, 1)
                std_of(i, 3 * T)
            pairs(act, T - 2, gather1)
            gather1(T - 2, 0)
            gather1(T - 1, 1, False)
            keep_turned_high(T - 1, 3 * T)

            wait_own(act, s_upd, 3 * T)
            act.dma_start(bias[:, 0:DIM], A["L1_ffn_b2"].partition_broadcast(P)).then_inc(s_bias, 16)
            act.dma_start(router_f, A["L1_ffn_router_w"].rearrange("(k p) n -> p k n", p=P)).then_inc(s_small, 16)

            def up1(f):
                for c, (a, n) in enumerate(THIRD):
                    u = f * 3 + c
                    act.wait_ge(s_up, u + (3 * K + 1))
                    act.activation(spacer[:, 2:3], one16[:, 0:1], ACT.Copy)
                    act.activation(up_buf[c][:, 0:n], bank[:, c, 0:n], ACT.Gelu_apprx_tanh, bias=cols[:, ds(f + 2 * K)]).then_inc(s_up_free, 1)
                    wait_own(act, s_up_free, u + (3 * K + 1))
                    act.activation(fT[0][:, ds(f), a:a + n], up_buf[c][:, 0:n], ACT.Copy).then_inc(s_up_h, 1)
            singles(act, F // P, up1)
            wait_own(act, s_lg, 2)
            act.activation(r_e, r_l, ACT.Exp).then_inc(s_ex, 1)

            def out1(i, j):
                keep_before(i, 4 * T)
                std_of(i, 4 * T)
            pairs(act, T, out1)
            keep_turned_high(T - 1, 4 * T)


            wait_own(act, s_upd, 4 * T)
            act.dma_start(bias[:, 0:DIM], A["L2_gnn_b"].partition_broadcast(P)).then_inc(s_bias, 16)
            wait_own(act, s_cnt, 3 * T)
            act.activation(dinv_out[:, :], deg_out[:, :], ACT.Sqrt).then_inc(s_sq, 1)
            wait_own(act, s_row2, 1)
            act.activation(w_row, bank[:, 7, 0:F], ACT.Copy).then_inc(s_row2k, 1)

            def project2(i, j):
                wait_own(act, s_sum, i + (3 * T + 1))
                act.activation(h_h[:, ds(i), :], ps_out[j], ACT.Copy, scale=dinv_out[:, ds(i)]).then_inc(s_hh, 1)
            wait_own(act, s_dinv, 2)
            pairs(act, T, project2)

            def coef2_high(i, j):
                if not isinstance(i, int) or i >= 2:
                    wait_own(act, s_out, i + (7 * T - 1))
                act.activation(coef_h[j], adj[:, :, ds(i * P, P)], ACT.Copy).then_inc(s_coef_h, 1)
            coef2_high(0, 0)

            def keep_turned(i, base):
                wait_own(act, s_turned, base + i + 1)
                act.activation(xT_f[:, :, ds(i * P, P)], ps_turn, ACT.Copy).then_inc(s_turn, 1)

            def gather2(i, j, more=True):
                if more:
                    coef2_high(i + 1, 1 - j)
                if not (isinstance(i, int) and i == 0):
                    keep_turned(i - 1, 5 * T)
                std_of(i, 5 * T)
            pairs(act, T - 2, gather2)
            gather2(T - 2, 0)
            gather2(T - 1, 1, False)
            keep_turned(T - 1, 5 * T)
            act.sem_inc(s_turn_h, T)

            act.dma_start(bias[:, 0:DIM], A["L2_ffn_b_out"].partition_broadcast(P)).then_inc(s_bias, 16)
            for k in range(K):
                wait_own(act, s_q, k + 1)
                act.activation(hT_h[:, k, :], xT_f[:, k, :], ACT.Copy, bias=-ROUND).then_inc(s_q_h, 1)
            wait_own(act, s_q_l, K)

            def up2(f):
                for c, (a, n) in enumerate(THIRD):
                    act.wait_ge(s_up, f * 3 + (c + 3 * K + 3 * F // P + 1))
                    act.wait_ge(s_up_free, f * 3 + (c + 3 * K + 3 * F // P))
                    act.activation(spacer[:, 2:3], one16[:, 0:1], ACT.Copy)
                    act.activation(hid_f[:, ds(f), a:a + n], bank[:, c, 0:n], ACT.Gelu, bias=cols[:, ds(f + 2 * K + F // P)],
                                   scale=up_scale[:, ds(f)]).then_inc(s_up_free, 1)
            singles(act, F // P, up2)
            for f in range(F // P):
                wait_own(act, s_hq, f + 1)
                act.activation(fT[0][:, f, :], hid_f[:, f, :], ACT.Copy).then_inc(s_hq_h, 1)

            def out2(i, j):
                keep_before(i, 6 * T)
                std3_of(i, 6 * T)
            pairs(act, T, out2)
            keep_turned_high(T - 1, 6 * T)

            wait_own(act, s_upd, 6 * T)
            act.dma_start(att, A["L3_gnn_att"].partition_broadcast(P)).then_inc(s_bias, 16)
            act.wait_ge(s_aux, 1)
            act.dma_start(att_col, A["L3_gnn_att_col"]).then_inc(s_bias, 16)

            def up3(f):
                for c, (a, n) in enumerate(THIRD):
                    wait_own(act, s_up, f * 3 + (c + 1 + 3 * K + 6 * F // P))
                    act.activation(xdT[0][:, f, a:a + n], bank[:, c, 0:n], ACT.Copy).then_inc(s_up_h, 1)
            for f in range(2):
                up3(f)

            def project3(i, j):
                wait_own(act, s_out, i + (9 * T + 1))
                act.activation(lr[:, ds(i), :], ps_out[j][:, 0:HALF], ACT.Copy).then_inc(s_lr, 1)
                act.activation(xr_h[:, ds(i), :], ps_out[j][:, HID:2 * HID], ACT.Copy).then_inc(s_xrh, 1)
            pairs(act, T, project3)

            def nothing_more(*_):
                pass

            def self_weight(w, ch, cm, cs, last):
                act.wait_ge(s_win, w * 5 + 4)
                act.activation(p_self, p_self, ACT.Exp).then_inc(s_selfp, 1)

            def round_sums(w, c, ch, cm):
                act.activation(spacer[:, 2:3], one16[:, 0:1], ACT.Copy)
                for b in range(2):
                    act.wait_ge(s_dt, ch * 2 + (b + 3))
                    act.wait_ge(s_maxd, (cm + w) * 2 + (b + 1))
                    act.activation(away[b], by_dst[b], ACT.Copy, scale=BIG, bias=-BIG)
                    act.wait_ge(s_pick, ch * 2 + (b + 3))
                    act.activation(zT[b], bank[:, 4 + b, 0:4 * EP], ACT.Copy, scale=0.2).then_inc(s_fifth, 1)
                for b in range(2):
                    act.wait_ge(s_got_free, ch * 2 + (b + 3))
                    act.activation(zTb[b], zT[b], ACT.Copy).then_inc(s_lkb, 1)

            def edge_weights(w, c, ch, cs):
                for b in range(2):
                    act.wait_ge(s_s, cs * 2 + (b + 1))
                    act.wait_ge(s_scat, (cs + w) * 2 + (b + 1))
                    act.activation(z3[b][0:EP, :, HID:HID + 4], s_now[b][0:EP], ACT.Exp).then_inc(s_p, 1)
            over_windows(act, nothing_more, round_sums, self_weight, edge_weights, nothing_more)

            wait_own(act, s_aggt, 1)
            act.activation(aggT[0], bank[:, 0:5, :].rearrange("p a b -> p (a b)").rearrange("p (a b) -> p a b", a=2), ACT.Copy).then_inc(s_aggh, 1)

            def out3(i, j):
                keep_before(i, 7 * T)
                std_of(i, 7 * T)
            pairs(act, T, out3)
            keep_turned_high(T - 1, 7 * T)

            wait_own(act, s_upd, 7 * T)
            act.dma_start(router_f, A["L3_ffn_router_wT"].rearrange("(k p) n -> p k n", p=P)).then_inc(s_small, 16)
            act.dma_start(route_bias, A["L3_ffn_routing_bias"].partition_broadcast(P)).then_inc(s_small, 16)
            wait_own(act, s_lg, 3)
            act.activation(r_e, r_l, ACT.Sigmoid).then_inc(s_ex, 1)

            def expert3(x3, j):
                for unit3 in range(U3):
                    f, c = unit3 // 3, unit3 % 3
                    a, n = THIRD[c]
                    act.wait_ge(s_gu, x3 * U3 + (unit3 + 1))
                    act.activation(up_buf[c][:, 0:n], bank[:, 4 + unit3 % 2, 0:n], ACT.Silu).then_inc(s_silu, 1)
                    act.wait_ge(s_h3, x3 * U3 + (unit3 + 1))
                    if unit3 == 0:
                        act.wait_ge(s_out, x3 * T + 10 * T)
                    act.activation(h3[j][0][:, f, a:a + n], up_buf[c][:, 0:n], ACT.Copy).then_inc(s_h3h, 1)
            pairs(act, E3 + 1, expert3, 0, 1)
        @block.vector
        def _(dve):
            step = [0]

            def link(ins):
                step[0] += 1
                ins.then_inc(s_v, 1)
                dve.wait_ge(s_v, step[0])

            dve.wait_ge(s_edges, 48)
            dve.tensor_copy(edge_f[0:EP], edge_i[0:EP])
            link(dve.tensor_copy(span_f[0:NC, :], span_i[0:NC, :]))
            dve.tensor_reduce(span[0:NC, 0:1], span_f[0:NC, :], AX_X, ALU.min)
            link(dve.tensor_reduce(span[0:NC, 1:2], span_f[0:NC, :], AX_X, ALU.max))
            dve.wait_ge(s_const, 1)
            dve.tensor_scalar(hit[0:NC, 0:T], win_lo[0:NC, :], span[0:NC, 1:2], None, ALU.is_le)
            link(dve.tensor_scalar(hit[0:NC, T:2 * T], win_lo[0:NC, :], float(P - 1), span[0:NC, 0:1], ALU.add, ALU.is_ge))
            link(dve.tensor_tensor(hit[0:NC, 0:T], hit[0:NC, 0:T], hit[0:NC, T:2 * T], ALU.mult))
            dve.tensor_scalar(span[0:NC, 0:1], chunk_no[0:NC, :], 1.0, None, ALU.add)
            link(dve.tensor_scalar(span[0:NC, 1:2], chunk_no[0:NC, :], -1.0, float(NC), ALU.mult, ALU.add))
            dve.tensor_scalar(hit[0:NC, T:2 * T], hit[0:NC, 0:T], span[0:NC, 0:1], None, ALU.mult)
            link(dve.tensor_scalar(hit_all[0:NC, 0:T], hit[0:NC, 0:T], span[0:NC, 1:2], None, ALU.mult))
            dve.tensor_copy(hit[0:NC, 0:T], hit_all[0:NC, 0:T]).then_inc(s_span, 1)
            dve.wait_ge(s_hits, 1)
            link(dve.tensor_scalar(hit[0:1, 0:T], hit_all[0:1, 0:T], -1.0, float(NC), ALU.mult, ALU.add))
            link(dve.tensor_scalar(hit[0:1, 0:T], hit[0:1, 0:T], float(NC - 1), None, ALU.min))
            link(dve.tensor_scalar(hit[0:1, T:2 * T], hit[0:1, 0:T], 1.0, None, ALU.add))
            link(dve.tensor_tensor(hit[0:1, T:2 * T], hit[0:1, T:2 * T], hit_all[0:1, T:2 * T], ALU.max))
            link(dve.tensor_copy(bounds[0:1, :], hit[0:1, :]))
            dve.sem_inc(s_bounds, 1)

            done = dve.alloc_register("onehots")
            dve.reg_mov(done, 0)
            with dve.Fori(0, T) as w:
                first, end = window_bounds(dve, w)
                with dve.Fori(first, end) as c:
                    m = dve.snap(done)
                    for b in range(CHUNK):
                        dve.wait_ge(s_hot_free, m + (b + 1))
                        dve.tensor_scalar(src_hot[b][0:EP, :], src_row[0:EP, :], edge_f[0:EP, 0, ds(c * CHUNK + b)], None, ALU.is_equal)
                        dve.tensor_scalar(dst_hot[b][0:EP, :], dst_row[0:EP, :], edge_f[0:EP, 1, ds(c * CHUNK + b)],
                                          win_neg[0:EP, ds(w)], ALU.subtract, ALU.is_equal).then_inc(s_hot, 1)
                    dve.reg_add(done, done, CHUNK)
            dve.wait_ge(s_adj_free, T + 1)
            dve.tensor_reduce(deg_in[:, :], deg3[:, :, :], AX_X, ALU.add).then_inc(s_deg, 1)
            link(dve.memset(deg_out[:, :], 1.0))
            dve.wait_ge(s_deg, 1)
            dve.tensor_reduce(span[:, 0:1], deg_in[:, :], AX_X, ALU.max).then_inc(s_most, 1)
            dve.wait_ge(s_most_all, 1)
            link(dve.tensor_scalar(span[:, 1:2], hit_all[:, 0:1], -2048.0, 0.0, ALU.add, ALU.max))
            link(dve.tensor_scalar(span[:, 1:2], span[:, 1:2], float(T), float(T - 1), ALU.mult, ALU.min))
            link(dve.tensor_scalar(span[:, 1:2], span[:, 1:2], 1.0, None, ALU.add))
            dve.tensor_copy(low_blocks[:, :], span[:, 1:2]).then_inc(s_lowb, 1)
            dve.wait_ge(s_sq, 1)
            dve.reciprocal(dinv_in[:, :], dinv_in[:, :]).then_inc(s_dinv, 1)

            def stats(i, base, updated):
                if updated is not None:
                    dve.wait_ge(s_upd, updated)
                    dve.memset(spacer[:, 0:1], 0.0)
                dve.bn_stats(bn[:, 0, :], x[:, ds(i), 0:HALF].rearrange("p a n -> p (a n)"))
                dve.bn_stats(bn[:, 1, :], x[:, ds(i), HALF:DIM].rearrange("p a n -> p (a n)")).then_inc(s_bn, 1)
                dve.wait_ge(s_bn, base + i + 1)
                dve.memset(spacer[:, 1:2], 0.0)
                dve.bn_aggr(mv[:, :], bn[:, :, :]).then_inc(s_mv, 1)

            def normalise(i, base):
                dve.wait_ge(s_std, base + i + 1)
                dve.reciprocal(rstd[:, :], std[:, :]).then_inc(s_rstd, 1)
                dve.wait_ge(s_rstd, base + i + 1)
                wait(dve, s_turned, base + i)
                dve.tensor_scalar(xhat[:, :], x[:, ds(i), :], mv[:, 0:1], rstd[:, :], ALU.subtract, ALU.mult).then_inc(s_xhat, 1)

            def keep_turned_low(i, base):
                dve.wait_ge(s_turn_h, base + i + 1)
                dve.tensor_tensor(xT_l[:, :, ds(i * P, P)], ps_turn, xT_h[:, :, ds(i * P, P)], ALU.subtract).then_inc(s_turn, 1)

            dve.wait_ge(s_x, 32)
            dve.wait_ge(s_dinv, 1)
            stats(0, 0, None)
            normalise(0, 0)
            keep_turned_low(0, 0)

            def norm_project(i, j, more=True):
                if more:
                    stats(i + 1, 0, None)
                    normalise(i + 1, 0)
                    keep_turned_low(i + 1, 0)
                dve.wait_ge(s_hh, i + 1)
                dve.scalar_tensor_tensor(h_l[:, ds(i), :], ps_out[j], dinv_in[:, ds(i)], h_h[:, ds(i), :],
                                         ALU.mult, ALU.subtract).then_inc(s_out_free, 1)
            pairs(dve, T - 2, norm_project, first=0)
            norm_project(T - 2, 0)
            norm_project(T - 1, 1, False)

            def row_low(w):
                dve.wait_ge(s_row_h, w + 1)
                dve.tensor_tensor(row_l, adj[:, ds(w), :], row_h, ALU.subtract).then_inc(s_row, 1)

            def coef_low(w, j):
                dve.wait_ge(s_rowt, 2 * w + 2)
                dve.tensor_copy(coef_l[j], bank[:, 6:8, :].bitcast(BF16)[:, :, 0:5 * P]).then_inc(s_coef, 1)

            def count_out(w, j):
                dve.wait_ge(s_coef, w + 1)
                dve.wait_ge(s_coef_h, w + 1)
                dve.tensor_reduce(deg_part[:, 0, :], coef_h[j], AX_X, ALU.add)
                dve.tensor_reduce(deg_part[:, 1, :], coef_l[j], AX_X, ALU.add).then_inc(s_cnt, 1)
                dve.wait_ge(s_cnt, 3 * w + 1)
                dve.tensor_tensor(deg_out[:, :], deg_out[:, :], deg_part[:, 0, :], ALU.add).then_inc(s_cnt, 1)
                dve.wait_ge(s_cnt, 3 * w + 2)
                dve.tensor_tensor(deg_out[:, :], deg_out[:, :], deg_part[:, 1, :], ALU.add).then_inc(s_cnt, 1)

            def keep_before(i, base):
                if not (isinstance(i, int) and i == 0):
                    keep_turned_low(i - 1, base)

            def next_norm(i, tail):
                stats(i, (tail + 1) * T, i + (tail * T + 1))
                normalise(i, (tail + 1) * T)

            row_low(0)
            coef_low(0, 0)
            dve.wait_ge(s_bias, 16)

            def gather0(i, j, more=True):
                if more:
                    row_low(i + 1)
                    coef_low(i + 1, 1 - j)
                keep_before(i, T)
                count_out(i, j)
                dve.wait_ge(s_out, i + (T + 1))
                dve.scalar_tensor_tensor(ps_out[j], ps_out[j], dinv_in[:, ds(i)], bias[:, 0:DIM], ALU.mult, ALU.add).then_inc(s_sum, 1)
                dve.wait_ge(s_sum, i + 1)
                dve.scalar_tensor_tensor(x[:, ds(i), :], ps_out[j], 0.0, x[:, ds(i), :], ALU.max, ALU.add).then_inc(s_upd, 1)
                next_norm(i, 0)
            pairs(dve, T - 2, gather0)
            gather0(T - 2, 0)
            gather0(T - 1, 1, False)
            keep_turned_low(T - 1, T)

            dve.wait_ge(s_cols, 64)

            def up0(f):
                for c, (a, n) in enumerate(THIRD):
                    dve.wait_ge(s_up_h, f * 3 + (c + 1))
                    dve.scalar_tensor_tensor(hT_l[:, ds(f), a:a + n], bank[:, c, 0:n], cols[:, ds(f)], hT_h[:, ds(f), a:a + n],
                                             ALU.add, ALU.subtract).then_inc(s_up_free, 1)
            singles(dve, K, up0)

            dve.wait_ge(s_small, 16 * (K + 1))
            dve.tensor_copy(emb[0], emb_f)
            link(dve.tensor_copy(b2[0], b2_f))
            dve.tensor_tensor(emb[1], emb_f, emb[0], ALU.subtract).then_inc(s_emb, 1)
            dve.tensor_tensor(b2[1], b2_f, b2[0], ALU.subtract).then_inc(s_b2, 1)
            dve.tensor_scalar(part_i[:, 1:2], part_i[:, 0:1], 15, None, ALU.bitwise_and)
            link(dve.tensor_scalar(part_i[:, 2:3], part_i[:, 0:1], 4, None, ALU.logical_shift_right))
            link(dve.tensor_copy(part_f[:, :], part_i[:, 1:3]))
            dve.tensor_scalar(head_mask[:, :], eight[:, :], part_f[:, 1:2], None, ALU.is_equal)
            for half in range(2):
                for j in range(K):
                    last = dve.tensor_scalar(pick[:, j, half * 64:(half + 1) * 64], ones[:, 0:64], float(2 * j + half), part_f[:, 0:1],
                                             ALU.mult, ALU.is_equal)
            link(last)

            def spread(v, like):
                return v.unsqueeze(2).broadcast_to([P, like.shape[1], like.shape[2]])

            def along(row, like):
                return row[:, 0:like.shape[2]].unsqueeze(1).broadcast_to([P, like.shape[1], like.shape[2]])

            def first_largest(v, top, found, best, scratch):
                link(dve.tensor_tensor(scratch, v, spread(top, v), ALU.is_equal))
                link(dve.tensor_tensor(scratch, scratch, along(rank, v), ALU.mult))
                link(dve.tensor_reduce(best, scratch, AX_X, ALU.max))
                link(dve.tensor_tensor(found, scratch, spread(best, v), ALU.is_equal))

            dve.wait_ge(s_logit, T)
            raw = bank[:, 4:7, :].rearrange("p a b -> p (a b)")[:, 0:GROUPS * 16].rearrange("p (g e) -> p g e", e=16)
            link(dve.tensor_reduce(g_m, raw, AX_X, ALU.max))
            dve.tensor_tensor(lg, raw, spread(g_m, lg), ALU.subtract).then_inc(s_lg, 1)
            dve.wait_ge(s_lg, 1)
            link(dve.memset(g_m, 0.0))
            first_largest(lg, g_m, t_m, g_c, t_c)
            dve.wait_ge(s_ex, 1)
            link(dve.scalar_tensor_tensor(lg, t_m, -BIG, lg, ALU.mult, ALU.add))
            link(dve.tensor_reduce(g_m, lg, AX_X, ALU.max))
            first_largest(lg, g_m, t_o, g_c, t_c)
            link(dve.tensor_tensor(t_m, t_m, t_o, ALU.add))
            link(dve.tensor_reduce(g_z, gates_g, AX_X, ALU.add))
            dve.reciprocal(g_z, g_z)
            link(dve.tensor_tensor(gates_g, gates_g, t_m, ALU.mult))
            dve.tensor_tensor(gates_g, gates_g, spread(g_z, lg), ALU.mult).then_inc(s_gate, 1)
            dve.wait_ge(s_gth, 1)
            dve.tensor_tensor(gT[1], bank[:, 0:3, :].rearrange("p a b -> p (a b)")[:, 0:NP], gT[0], ALU.subtract).then_inc(s_gt, 1)
            dve.wait_ge(s_gt, 1)

            def mask_gates(s, c, head):
                a, n = THIRD[c]
                dve.tensor_scalar(gm[c][0][:, 0:n], gT[0][:, a:a + n], head_mask[:, ds(head)], None, ALU.mult)
                dve.tensor_scalar(gm[c][1][:, 0:n], gT[1][:, a:a + n], head_mask[:, ds(head)], None, ALU.mult).then_inc(s_gm, 1)

            def comb_low(s, b, c, head):
                a, n = THIRD[c]
                dve.wait_ge(s_comb_h, s + 1)
                dve.tensor_tensor(hT_l[:, ds(head), a:a + n], bank[:, 6 + b, 0:n], hT_h[:, ds(head), a:a + n], ALU.subtract).then_inc(s_comb, 1)

            def experts(hp, first=False, last=False):
                for jj in range(6):
                    s, b, c = hp * 6 + jj, jj % 2, jj % 3
                    a, n = THIRD[c]
                    for j in range(K + 1):
                        u = s * K + j
                        if j < K:
                            dve.wait_ge(s_spread, u + 1)
                            dve.wait_ge(s_gelu, u + 1)
                            dve.tensor_tensor(unit[(jj * K + j) % 3][:, 0:n], unit[(jj * K + j) % 3][:, 0:n], bank[:, 2 + j % 2, 0:n], ALU.mult).then_inc(s_gated, 1)
                        if j > 0:
                            dve.wait_ge(s_hid_h, u)
                            dve.tensor_tensor(hid[b][1][:, j - 1, 0:n], unit[(jj * K + j - 1) % 3][:, 0:n], hid[b][0][:, j - 1, 0:n],
                                              ALU.subtract).then_inc(s_hid, 1)
                        if j == 4 and not (last and jj == 5):
                            if not (first and jj < 2):
                                dve.wait_ge(s_comb_mm, s - 1)
                            mask_gates(s + 1, (jj + 1) % 3, hp * 2 + (jj + 1) // 3)
                    if not (first and jj == 0):
                        comb_low(s - 1, 1 - b, (jj - 1) % 3, hp * 2 + (jj - 1) // 3)
            mask_gates(0, 0, 0)
            experts(0, True)
            with dve.Fori(1, K // 2 - 1) as hp:
                experts(hp)
            experts(K // 2 - 1, False, True)
            comb_low(3 * K - 1, 1, 2, K - 1)

            dve.wait_ge(s_bias, 32)

            def out0(i, j):
                keep_before(i, 2 * T)
                dve.wait_ge(s_out, i + (2 * T + 1))
                dve.tensor_tensor(ps_out[j], ps_out[j], bias[:, 0:DIM], ALU.add).then_inc(s_sum, 1)
                dve.wait_ge(s_sum, i + (T + 1))
                dve.tensor_tensor(x[:, ds(i), :], ps_out[j], x[:, ds(i), :], ALU.add).then_inc(s_upd, 1)
                next_norm(i, 1)
            pairs(dve, T, out0)
            keep_turned_low(T - 1, 2 * T)

            dve.wait_ge(s_bias, 64)

            def project1(i, j):
                dve.wait_ge(s_hh, i + (T + 1))
                if not isinstance(i, int) or i >= 1:
                    dve.wait_ge(s_out_free, i + T)
                dve.scalar_tensor_tensor(xhat[:, :], ps_out[j], 1.0, bias[:, 0:DIM], ALU.mult, ALU.mult, accum_out=al[:, ds(i)])
                dve.scalar_tensor_tensor(spare, ps_out[j], 1.0, work[:, 0:DIM], ALU.mult, ALU.mult, accum_out=ar[:, ds(i)])
                dve.tensor_tensor(h_l[:, ds(i), :], ps_out[j], h_h[:, ds(i), :], ALU.subtract).then_inc(s_out_free, 1)
            pairs(dve, T, project1)
            dve.wait_ge(s_out_free, 2 * T)
            dve.tensor_tensor(z, ident[:, :].unsqueeze(1).broadcast_to([P, T, P]), al[:, :].unsqueeze(2).broadcast_to([P, T, P]),
                              ALU.mult).then_inc(s_diag, 1)
            dve.tensor_reduce(low2[:, 0:1], al[:, :], AX_X, ALU.min)
            link(dve.tensor_reduce(low2[:, 1:2], ar[:, :], AX_X, ALU.min))
            dve.tensor_scalar(low2[:, :], low2[:, :], -1.0, None, ALU.mult).then_inc(s_mins, 1)
            dve.wait_ge(s_mins_all, 1)
            link(dve.tensor_tensor(shift[:, 0:1], low2_all[:, 0:1], low2_all[:, 1:2], ALU.add))
            link(dve.tensor_scalar(shift[:, 0:1], shift[:, 0:1], -1.0, None, ALU.mult))
            link(dve.scalar_tensor_tensor(shift[:, 0:1], shift[:, 0:1], 0.1, shift[:, 0:1], ALU.mult, ALU.max))
            dve.tensor_scalar(shift[:, 0:1], shift[:, 0:1], 0.4, 0.0, ALU.add, ALU.min).then_inc(s_shift, 1)
            dve.wait_ge(s_epsr, 1)
            link(dve.tensor_scalar(shift[:, 2:3], shift[:, 1:2], 1e-5, None, ALU.mult))
            dve.wait_ge(s_al, 1)

            def coef1(i, j):
                dve.tensor_tensor(z, bias[:, ds(i * P, P)].unsqueeze(1).broadcast_to([P, T, P]),
                                  ar[:, :].unsqueeze(2).broadcast_to([P, T, P]), ALU.add).then_inc(s_zs, 1)
                dve.wait_ge(s_zs, i + 1)
                dve.scalar_tensor_tensor(z, z, 0.1, z, ALU.mult, ALU.max).then_inc(s_z, 1)
                dve.wait_ge(s_ez, i + 1)
                dve.tensor_tensor(z, z, adj[:, :, ds(i * P, P)], ALU.mult).then_inc(s_cz, 1)

            def coef1_low(i, j):
                dve.wait_ge(s_coef_h, i + (T + 1))
                dve.tensor_tensor(coef_l[j], z, coef_h[j], ALU.subtract).then_inc(s_coef, 1)
            coef1(0, 0)
            coef1_low(0, 0)

            def gather1(i, j, more=True):
                if more:
                    dve.wait_ge(s_coef, i + (T + 1))
                    coef1(i + 1, 1 - j)
                    coef1_low(i + 1, 1 - j)
                keep_before(i, 3 * T)
                dve.wait_ge(s_out, i + (4 * T + 1))
                dve.tensor_scalar(rstd[:, :], bank[:, 6 + j, 0:1], shift[:, 2:3], None, ALU.add).then_inc(s_step1, 1)
                dve.wait_ge(s_step1, 4 * i + 1)
                dve.reciprocal(rstd[:, :], rstd[:, :]).then_inc(s_step1, 1)
                dve.wait_ge(s_step1, 4 * i + 2)
                dve.tensor_scalar(ps_out[j], ps_out[j], rstd[:, :], None, ALU.mult).then_inc(s_step1, 1)
                dve.wait_ge(s_step1, 4 * i + 3)
                dve.tensor_scalar(xhat[:, :], ps_out[j], 0.0, None, ALU.min).then_inc(s_neg, 1)
                dve.wait_ge(s_eneg, i + 1)
                dve.scalar_tensor_tensor(ps_out[j], ps_out[j], 0.0, xhat[:, :], ALU.max, ALU.add).then_inc(s_step1, 1)
                dve.wait_ge(s_step1, 4 * i + 4)
                dve.scalar_tensor_tensor(x[:, ds(i), :], ps_out[j], -1.0, x[:, ds(i), :], ALU.add, ALU.add).then_inc(s_upd, 1)
                next_norm(i, 2)
            pairs(dve, T - 2, gather1)
            gather1(T - 2, 0)
            gather1(T - 1, 1, False)
            keep_turned_low(T - 1, 3 * T)

            def up1(f):
                for c, (a, n) in enumerate(THIRD):
                    dve.wait_ge(s_up_h, f * 3 + (3 * K + c + 1))
                    dve.tensor_tensor(fT[1][:, ds(f), a:a + n], up_buf[c][:, 0:n], fT[0][:, ds(f), a:a + n],
                                      ALU.subtract).then_inc(s_hid_l, 1)
            dve.wait_ge(s_small, 16 * (K + 2))
            link(dve.tensor_copy(router[0], router_f))
            dve.tensor_tensor(router[1], router_f, router[0], ALU.subtract).then_inc(s_router1, 1)
            singles(dve, F // P, up1)
            load_weights(dve, True, "maxima_in", "L2_gnn_W_a")
            dve.wait_ge(s_logit, 2 * T)
            raw1 = bank[:, 7, 0:T * 8].rearrange("p (t e) -> p t e", e=8)
            a_, b_, c_ = r_s[:, 0, :], r_s[:, 1, :], r_s[:, 2, :]
            link(dve.tensor_reduce(a_, raw1, AX_X, ALU.max))
            dve.tensor_tensor(r_l, raw1, spread(a_, r_l), ALU.subtract).then_inc(s_lg, 1)
            dve.wait_ge(s_ex, 2)
            link(dve.tensor_reduce(a_, r_e, AX_X, ALU.add))
            link(dve.reciprocal(a_, a_))
            link(dve.tensor_tensor(r_e, r_e, spread(a_, r_e), ALU.mult))
            link(dve.tensor_reduce(a_, r_e, AX_X, ALU.max))
            first_largest(r_e, a_, r_o, b_, r_l)
            link(dve.tensor_scalar(r_o, r_o, -1.0, 1.0, ALU.mult, ALU.add))
            link(dve.tensor_tensor(r_e, r_e, r_o, ALU.mult))
            link(dve.tensor_reduce(b_, r_e, AX_X, ALU.max))
            link(dve.tensor_tensor(c_, a_, b_, ALU.add))
            link(dve.reciprocal(c_, c_))
            dve.tensor_tensor(a_, a_, c_, ALU.mult)
            link(dve.tensor_tensor(b_, b_, c_, ALU.mult))
            link(dve.tensor_tensor(a_, a_, b_, ALU.add))
            dve.wait_ge(s_bias, 80)

            def out1(i, j):
                keep_before(i, 4 * T)
                dve.wait_ge(s_out, i + (5 * T + 1))
                dve.tensor_tensor(ps_out[j], ps_out[j], bias[:, 0:DIM], ALU.add).then_inc(s_sum, 1)
                dve.wait_ge(s_sum, i + (2 * T + 1))
                dve.scalar_tensor_tensor(x[:, ds(i), :], ps_out[j], r_s[:, 0, ds(i)], x[:, ds(i), :], ALU.mult, ALU.add).then_inc(s_upd, 1)
                next_norm(i, 3)
            pairs(dve, T, out1)
            keep_turned_low(T - 1, 4 * T)

            dve.wait_ge(s_w, PARTS["maxima_out"])
            link(dve.tensor_reduce(w_amax[:, :], w_max.rearrange("p (a b) -> p a b", b=2), AX_X, ALU.max))
            link(dve.tensor_scalar(w_amax[:, :], w_amax[:, :], 1e-8, None, ALU.max))
            dve.tensor_scalar(w_step[:, :], w_amax[:, :], 1.0 / 127.0, None, ALU.mult)
            link(dve.reciprocal(w_quant[:, :], w_amax[:, :]))
            link(dve.tensor_scalar(w_quant[:, :], w_quant[:, :], 127.0, None, ALU.mult))
            dve.tensor_tensor(w_diag, ident[:, :].unsqueeze(1).broadcast_to([P, F // P, P]),
                              w_quant[:, 0:F // P].unsqueeze(2).broadcast_to([P, F // P, P]), ALU.mult).then_inc(s_wscale, 1)
            dve.wait_ge(s_sq, 2)
            dve.reciprocal(dinv_out[:, :], dinv_out[:, :]).then_inc(s_dinv, 1)
            dve.wait_ge(s_dinv, 2)
            dve.wait_ge(s_bias, 96)

            def project2(i, j):
                dve.wait_ge(s_out, i + (6 * T + 1))
                dve.tensor_tensor(ps_out[j], ps_out[j], bias[:, 0:DIM], ALU.add).then_inc(s_sum, 1)
                dve.wait_ge(s_hh, i + (2 * T + 1))
                dve.scalar_tensor_tensor(h_l[:, ds(i), :], ps_out[j], dinv_out[:, ds(i)], h_h[:, ds(i), :],
                                         ALU.mult, ALU.subtract).then_inc(s_out_free, 1)
            pairs(dve, T, project2)

            def coef2_low(i, j):
                dve.wait_ge(s_coef_h, i + (2 * T + 1))
                dve.tensor_tensor(coef_l[j], adj[:, :, ds(i * P, P)], coef_h[j], ALU.subtract).then_inc(s_coef, 1)

            def largest(i, rows=P):
                dve.wait_ge(s_xhat, i + (5 * T + 1))
                dve.tensor_reduce(x_max[0:rows, 1:2], xhat[0:rows, :], AX_X, ALU.max, apply_absolute_value=True).then_inc(s_xm, 1)
                dve.wait_ge(s_xm, i + 2)
                dve.tensor_tensor(x_max[0:rows, 0:1], x_max[0:rows, 0:1], x_max[0:rows, 1:2], ALU.max)

            coef2_low(0, 0)
            dve.memset(x_max[:, :], 0.0).then_inc(s_xm, 1)

            def gather2(i, j, more=True):
                if more:
                    coef2_low(i + 1, 1 - j)
                dve.wait_ge(s_out, i + (7 * T + 1))
                dve.scalar_tensor_tensor(x[:, ds(i), :], ps_out[j], dinv_out[:, ds(i)], x[:, ds(i), :], ALU.mult, ALU.add).then_inc(s_upd, 1)
                next_norm(i, 4)
                if more:
                    largest(i)
            pairs(dve, T - 2, gather2)
            gather2(T - 2, 0)
            gather2(T - 1, 1, False)
            largest(T - 1, LAST)
            dve.memset(spacer[:, 0:1], 0.0).then_inc(s_max1, 1)

            dve.wait_ge(s_max1_all, 1)
            link(dve.tensor_scalar(x_max_all[:, :], x_max_all[:, :], 1e-8, None, ALU.max))
            dve.tensor_scalar(x_step[:, :], x_max_all[:, :], 1.0 / 32767.0, None, ALU.mult)
            link(dve.reciprocal(x_quant[:, :], x_max_all[:, :]))
            link(dve.tensor_scalar(x_quant[:, :], x_quant[:, :], 32767.0, None, ALU.mult))
            dve.tensor_scalar(up_scale[:, :], w_step[:, 0:F // P], x_step[:, :], None, ALU.mult)
            dve.wait_ge(s_turn, 6 * T)

            def quantised_low(k):
                dve.wait_ge(s_q_h, k + 1)
                dve.scalar_tensor_tensor(hT_l[:, k, :], xT_f[:, k, :], -ROUND, hT_h[:, k, :], ALU.add, ALU.subtract).then_inc(s_q_l, 1)

            for k in range(K):
                dve.tensor_scalar(xT_f[:, k, :], xT_f[:, k, :], x_quant[:, :], ROUND, ALU.mult, ALU.add).then_inc(s_q, 1)
                if k:
                    quantised_low(k - 1)
            quantised_low(K - 1)

            dve.wait_ge(s_bias, 112)

            def add_bias(i):
                dve.tensor_tensor(x[:, ds(i), :], x[:, ds(i), :], bias[:, 0:DIM].unsqueeze(1), ALU.add).then_inc(s_xb, 1)
            singles(dve, T, add_bias, first=0)
            dve.wait_ge(s_xb, T)
            for f in range(F // P):
                for c, (a, n) in enumerate(THIRD):
                    u = f * 3 + c
                    dve.wait_ge(s_up_free, 3 * K + 3 * F // P + u + 1)
                    last = dve.tensor_reduce(h_max[:, u:u + 1], hid_f[:, f, a:min(a + n, NODES)], AX_X, ALU.max, apply_absolute_value=True)
            link(last)
            dve.tensor_reduce(h_max1[:, :], h_max[:, :], AX_X, ALU.max).then_inc(s_max2, 1)
            dve.wait_ge(s_max2_all, 1)
            link(dve.tensor_scalar(h_max_all[:, :], h_max_all[:, :], 1e-8, None, ALU.max))
            link(dve.reciprocal(h_quant[:, :], h_max_all[:, :]))
            dve.tensor_scalar(h_max_all[:, :], h_max_all[:, :], 1.0 / 32767.0, None, ALU.mult)
            link(dve.tensor_scalar(h_quant[:, :], h_quant[:, :], 32767.0, None, ALU.mult))
            link(dve.tensor_scalar(h_scale[:, :], w_step[:, F // P:], h_max_all[:, :], None, ALU.mult))
            for f in range(F // P):
                link(dve.tensor_scalar(hid_f[:, f, :], hid_f[:, f, :], h_quant[:, :], ROUND, ALU.mult, ALU.add))
                dve.tensor_scalar(hid_f[:, f, :], hid_f[:, f, :], -ROUND, h_scale[:, f:f + 1], ALU.add, ALU.mult).then_inc(s_hq, 1)
                if f:
                    dve.wait_ge(s_hq_h, f)
                    dve.tensor_tensor(fT[1][:, f - 1, :], hid_f[:, f - 1, :], fT[0][:, f - 1, :], ALU.subtract).then_inc(s_hq_l, 1)
            dve.wait_ge(s_hq_h, F // P)
            dve.tensor_tensor(fT[1][:, F // P - 1, :], hid_f[:, F // P - 1, :], fT[0][:, F // P - 1, :], ALU.subtract).then_inc(s_hq_l, 1)

            def out2(i, j):
                keep_before(i, 6 * T)
                dve.wait_ge(s_out, i + (8 * T + 1))
                dve.tensor_tensor(x[:, ds(i), :], ps_out[j], x[:, ds(i), :], ALU.add).then_inc(s_upd, 1)
                next_norm(i, 5)
            pairs(dve, T, out2)
            keep_turned_low(T - 1, 6 * T)

            for f in range(2):
                for c, (a, n) in enumerate(THIRD):
                    dve.wait_ge(s_up_h, 3 * K + 3 * F // P + f * 3 + c + 1)
                    dve.tensor_tensor(xdT[1][:, f, a:a + n], bank[:, c, 0:n], xdT[0][:, f, a:a + n], ALU.subtract).then_inc(s_up_free, 1)
            dve.sem_inc(s_got_free, 2)
            dve.sem_inc(s_tile_free, 2)
            dve.wait_ge(s_idx, 32)
            dve.tensor_copy(dst_f[0:EP, :], dst_i[0:EP, :])
            dve.wait_ge(s_bias, 144)

            own_z = sums[:, 0:2, :]
            att_2 = att.unsqueeze(1).broadcast_to([P, 2, HID])
            for i in range(0, T, 2):
                two = slice(i, i + 2)
                dve.wait_ge(s_xrh, i + 2)
                dve.tensor_tensor(xr_l[:, two, :], lr[:, two, HID:2 * HID], xr_h[:, two, :], ALU.subtract).then_inc(s_xr, 2)
                link(dve.tensor_tensor(own_z, lr[:, two, 0:HID], lr[:, two, HID:2 * HID], ALU.add))
                link(dve.scalar_tensor_tensor(own_z, own_z, 0.2, own_z, ALU.mult, ALU.max))
                link(dve.tensor_tensor(own_z, own_z, att_2, ALU.mult))
                link(dve.tensor_reduce(e_self[:, two, :], own_z.rearrange("p t (h d) -> p t h d", d=64), AX_X, ALU.add))
            dve.sem_inc(s_score, 1)
            dve.sem_inc(s_win, 1)
            dve.wait_ge(s_aux, 1)

            for f in range(2):
                for half in range(2):
                    rows = slice(half * 64, (half + 1) * 64)
                    last = dve.tensor_copy(att_cols[rows, f, 2 * f + half:2 * f + half + 1], att_col[rows, f:f + 1])
            link(last)
            for h in range(4):
                last = dve.tensor_copy(att_wide[:, h, :], att_cols[:, h // 2, h:h + 1].broadcast_to([P, P]))
            last.then_inc(s_att, 1)

            def dst_onehot(w, ch, b):
                dve.wait_ge(s_row_in[b], ch * 16 + 16)
                dve.wait_ge(s_pick, ch * 2 + (b + 1))
                dve.wait_ge(s_got_free, ch * 2 + (b + 1))
                dve.tensor_scalar(by_dst[b], dst_in[b], win_neg[:, ds(w)], part_no[:, :], ALU.add, ALU.is_equal).then_inc(s_dt, 1)

            def clear_max(w, ch, cm, cs):
                dve.wait_ge(s_win, w * 5 + 1)
                dve.memset(m_now, -BIG).then_inc(s_win, 1)
                for b in range(2):
                    dve.memset(away[b], -BIG)
                dve.wait_ge(s_win, w * 5 + 2)
                dve.memset(spacer[:, 0:1], 0.0).then_inc(s_clear, 1)
                dve.wait_ge(s_clear, w + 1)
                dve.sem_inc(s_met, 1)

            def score_tail(w, at, cm):
                for b in range(2):
                    dve.wait_ge(s_spread3, cm * 2 + (b + 1))
                    dve.tensor_scalar(e_all[0:EP, ds(at * CHUNK + 2 * b, 2), :], bank[0:EP, 6 + b, 0:8].rearrange("p (q h) -> p q h", q=2), 0.0, None, ALU.add)
                    for h in range(4):
                        spread_h = bank[:, 2 * b + h // 2, (h % 2) * 2 * EP:(h % 2 + 1) * 2 * EP]
                        last = dve.tensor_tensor_reduce(masked[:, h, :], spread_h, away[b], 1.0, -BIG, ALU.add, ALU.max, m_tile[:, b, h:h + 1])
                    last.then_inc(s_score, 1)
                    dve.wait_ge(s_score, (cm + w) * 2 + (b + 2))
                    dve.tensor_tensor(m_now, m_now, m_tile[:, b, :], ALU.max).then_inc(s_maxd, 1)

            def chunk_max(w, c, ch, cm):
                for b in range(2):
                    dst_onehot(w, ch, b)
                score_tail(w, c, cm)
                for b in range(2):
                    dve.wait_ge(s_fifth, cm * 2 + (b + 1))
                    dve.tensor_tensor(zT[b], bank[:, 4 + b, 0:4 * EP], zT[b], ALU.max).then_inc(s_got_free, 1)

            def window_max(w, ch, cm, cs, last):
                n = w * 5 + 1
                score_tail(w, last, cm)
                dve.wait_ge(s_maxd, (cm + w) * 2 + 2)
                dve.tensor_tensor(m_now.unsqueeze(1), m_now.unsqueeze(1), e_self[:, ds(w), :], ALU.max).then_inc(s_win, 1)
                dve.wait_ge(s_win, n + 2)
                for b in range(2):
                    dve.memset(to_dst[b], 0.0)
                dve.tensor_copy(m_b[:, 0:4], m_now).then_inc(s_mk, 1)
                dve.wait_ge(s_mk, w + 1)
                dve.tensor_tensor(p_self.unsqueeze(1), e_self[:, ds(w), :], m_b[:, 0:4].unsqueeze(1), ALU.subtract).then_inc(s_win, 1)

            def chunk_sum(w, c, ch, cs):
                def masked_scores(b):
                    picked = bank[0:EP, 4 + b, 0:10].rearrange("p (a b) -> p a b", a=2)
                    dve.wait_ge(s_pick, ch * 2 + (b + 3))
                    dve.tensor_tensor(s_now[b][0:EP], e_all[0:EP, ds(c * CHUNK + (CHUNK + 2 * b), 2), :], picked[:, :, 4:5].broadcast_to([EP, 2, 4]),
                                      ALU.mult).then_inc(s_sub, 1)
                    dve.wait_ge(s_sub, cs * 2 + (b + 1))
                    dve.tensor_tensor(s_now[b][0:EP], s_now[b][0:EP], picked[:, :, 0:4], ALU.subtract).then_inc(s_s, 1)

                def weighted_rows(b):
                    dve.wait_ge(s_scat, (cs + w) * 2 + (b + 1))
                    for q in range(2):
                        dve.tensor_scalar(to_dst[b][0:EP, q, :], dst_no[0:EP, :], dst_f[0:EP, ds(c * CHUNK + 2 * b + q)],
                                          win_neg[0:EP, ds(w)], ALU.subtract, ALU.is_equal)
                    dve.wait_ge(s_p, cs * 2 + (b + 1))
                    for q in range(2):
                        dve.wait_ge(s_got[b][q], ch * 16 + 16)
                        dve.tensor_tensor(z3[b][0:EP, q, 0:HID].rearrange("p (h d) -> p h d", d=64),
                                          xl_got[b][0:EP, q, :].rearrange("p (h d) -> p h d", d=64),
                                          z3[b][0:EP, q, HID:HID + 4].unsqueeze(2).broadcast_to([EP, 4, 64]),
                                          ALU.mult).then_inc(s_got_free if q else s_tile_free, 1)
                dst_onehot(w, ch, 0)
                masked_scores(0)
                dst_onehot(w, ch, 1)
                weighted_rows(0)
                masked_scores(1)
                weighted_rows(1)

            def window_sum(w, ch, cm, cs):
                n = w * 5 + 1
                dve.wait_ge(s_selfp, w + 1)
                dve.tensor_tensor(own.rearrange("p (h d) -> p h d", d=64), lr[:, ds(w), 0:HID].rearrange("p a (h d) -> p (a h) d", d=64),
                                  p_self.unsqueeze(2).broadcast_to([P, 4, 64]), ALU.mult)
                dve.wait_ge(s_agg, w + 1)
                dve.scalar_tensor_tensor(den, bank[:, 0, HID:HID + 4], 1e-16, p_self, ALU.add, ALU.add).then_inc(s_win, 1)
                dve.wait_ge(s_win, n + 4)
                dve.reciprocal(den, den)
                dve.tensor_tensor(own, own, bank[:, 0, 0:HID], ALU.add).then_inc(s_win, 1)
                dve.wait_ge(s_win, n + 5)
                dve.tensor_tensor(sums[:, ds(w), :].rearrange("p a (h d) -> p (a h) d", d=64), own.rearrange("p (h d) -> p h d", d=64),
                                  den.unsqueeze(2).broadcast_to([P, 4, 64]), ALU.mult)
            link(dve.memset(z3[0], 0.0))
            link(dve.memset(z3[1], 0.0))
            over_windows(dve, clear_max, chunk_max, window_max, chunk_sum, window_sum)
            dve.memset(spacer[:, 0:1], 0.0).then_inc(s_win, 1)

            dve.wait_ge(s_aggh, 1)
            dve.tensor_tensor(aggT[1], bank[:, 0:5, :].rearrange("p a b -> p (a b)").rearrange("p (a b) -> p a b", a=2), aggT[0], ALU.subtract).then_inc(s_aggl, 1)

            def out3(i, j):
                keep_before(i, 7 * T)
                dve.wait_ge(s_out, i + (10 * T + 1))
                dve.tensor_tensor(x[:, ds(i), :], ps_out[j], x[:, ds(i), :], ALU.add).then_inc(s_upd, 1)
                next_norm(i, 6)
            pairs(dve, T, out3)
            keep_turned_low(T - 1, 7 * T)

            dve.wait_ge(s_small, 16 * (K + 4))
            link(dve.tensor_copy(router[0], router_f))
            dve.tensor_tensor(router[1], router_f, router[0], ALU.subtract).then_inc(s_router1, 1)
            dve.wait_ge(s_logit, 3 * T)
            raw3 = bank[:, 3, 0:T * 8].rearrange("p (t e) -> p t e", e=8)
            dve.tensor_tensor(r_l, raw3, route_bias.unsqueeze(1).broadcast_to([P, T, 8]), ALU.add).then_inc(s_lg, 1)
            dve.wait_ge(s_ex, 3)
            link(dve.tensor_reduce(a_, r_e, AX_X, ALU.max))
            first_largest(r_e, a_, r_o, b_, r_l)
            link(dve.scalar_tensor_tensor(r_l, r_o, -2.0, r_e, ALU.mult, ALU.add))
            link(dve.tensor_reduce(b_, r_l, AX_X, ALU.max))
            link(dve.tensor_tensor(c_, a_, b_, ALU.add))
            dve.reciprocal(c_, c_)
            r_2 = gates3[:, :, 0:8]
            link(dve.tensor_copy(gates3[:, :, 0:8], r_o))
            first_largest(r_l, b_, r_o, a_, r_l)
            link(dve.tensor_tensor(r_o, r_o, r_2, ALU.add))
            link(dve.tensor_tensor(r_o, r_o, r_e, ALU.mult))
            dve.tensor_tensor(gates3[:, :, 0:8], r_o, spread(c_, r_o), ALU.mult)
            link(dve.memset(gates3[:, :, 8:9], 1.0))
            dve.sem_inc(s_gates3, 1)

            def hidden3(x3, j):
                for unit3 in range(U3):
                    f, c = unit3 // 3, unit3 % 3
                    a, n = THIRD[c]
                    dve.wait_ge(s_silu, x3 * U3 + (unit3 + 1))
                    dve.tensor_tensor(up_buf[c][:, 0:n], up_buf[c][:, 0:n], bank[:, 6 + unit3 % 2, 0:n], ALU.mult).then_inc(s_h3, 1)
                    dve.wait_ge(s_h3h, x3 * U3 + (unit3 + 1))
                    dve.tensor_tensor(h3[j][1][:, f, a:a + n], up_buf[c][:, 0:n], h3[j][0][:, f, a:a + n], ALU.subtract).then_inc(s_h3l, 1)

            def add3(x3):
                def tile(i, j):
                    dve.wait_ge(s_out, x3 * T + i + (11 * T + 1))
                    dve.wait_ge(s_upd, x3 * T + i + (6 * T + 1))
                    dve.scalar_tensor_tensor(x[:, ds(i), :], ps_out[j], gates3[:, ds(i), ds(x3)], x[:, ds(i), :], ALU.mult, ALU.add).then_inc(s_upd, 1)
                pairs(dve, T, tile, 0)

            def expert3(x3, j):
                hidden3(x3, j)
                add3(x3 - 1)
            hidden3(0, 0)
            expert3(1, 1)
            with dve.Fori(1, E3 // 2) as h:
                for j in range(2):
                    expert3(h * 2 + j, j)
            expert3(E3, 0)
            add3(E3)
        @block.tensor
        def _(pe):
            pe.wait_ge(s_const, 1)
            pe.sem_inc(s_hot_free, CHUNK)

            done = pe.alloc_register("onehots")
            pe.reg_mov(done, 0)
            pe.wait_ge(s_bounds, 1)
            with pe.Fori(0, T) as w:
                first, end = window_bounds(pe, w)
                pe.wait_ge(s_adj_free, w + 1)
                for c, (a, n) in enumerate(THIRD):
                    pe.matmul(bank[:, c, 0:n], nothing[0:EP, 0:P], nothing[0:EP, 0:n], start=True, stop=False)
                with pe.Fori(first, end):
                    m = pe.snap(done)
                    for b in range(CHUNK):
                        pe.wait_ge(s_hot, m + (b + 1))
                        for c, (a, n) in enumerate(THIRD):
                            last = pe.matmul(bank[:, c, 0:n], dst_hot[b][0:EP, :], src_hot[b][0:EP, a:a + n], start=False, stop=False)
                        last.then_inc(s_hot_free, 1)
                    pe.reg_add(done, done, CHUNK)
                for c, (a, n) in enumerate(THIRD):
                    last = pe.matmul(bank[:, c, 0:n], nothing[0:EP, 0:P], nothing[0:EP, 0:n], start=False, stop=True)
                last.then_inc(s_adj, 1)

            def turn(i, base):
                pe.wait_ge(s_xhat, base + i + 1)
                wait(pe, s_turn, base + i)
                for k in range(K):
                    last = pe.transpose(ps_turn[:, k, :], xhat[:, k * P:(k + 1) * P], ident[:, :])
                last.then_inc(s_turned, 1)

            def product(to, lhs, rhs, first, last, blocks, terms=((0, 0), (1, 0), (0, 1))):
                mm = None
                for k in range(first, last):
                    for n, (a, b) in enumerate(terms):
                        mm = pe.matmul(to, lhs(k, a), rhs(k, b), start=(k == 0 and n == 0),
                                       stop=(k == blocks - 1 and n == len(terms) - 1))
                return mm

            def tile_row(j, lhs, rhs, blocks, between=None, late=None, terms=((0, 0), (1, 0), (0, 1))):
                product(bank[:, 2 * j, :], lhs, lambda k, b: rhs(k, b)[:, 0:HALF], 0, blocks, blocks, terms)
                if between:
                    between()
                right = (bank[:, 2 * j + 1, :], lhs, lambda k, b: rhs(k, b)[:, HALF:DIM])
                product(*right, 0, blocks // 2, blocks, terms)
                if late:
                    late()
                product(*right, blocks // 2, blocks, blocks, terms).then_inc(s_out, 1)

            xT = (xT_h, xT_l)
            hT = (hT_h, hT_l)
            wt = (w_h, w_l)
            hv = (h_h, h_l)

            def project(i, j, between=None):
                tile_row(j, lambda k, a: xT[a][:, k, ds(i * P, P)], lambda k, b: wt[b][:, k, :], K, between)

            def project_two(parts):
                for k in range(K):
                    pe.wait_ge(s_w, parts - 2 * (K - 1 - k))
                    for i in range(2):
                        for half in range(2):
                            for n, (a, b) in enumerate(((0, 0), (1, 0), (0, 1))):
                                mm = pe.matmul(bank[:, 2 * i + half, :], xT[a][:, k, i * P:(i + 1) * P], wt[b][:, k, half * HALF:(half + 1) * HALF],
                                               start=(k == 0 and n == 0), stop=(k == K - 1 and n == 2))
                        if k == K - 1:
                            mm.then_inc(s_out, 1)

            turn(0, 0)

            def norm_project(i, j, more=True):
                if isinstance(i, int) and i == 0:
                    pe.wait_ge(s_w, PARTS["L0_gnn_W"])
                    pe.wait_ge(s_adj_free, T + 1)
                if not isinstance(i, int) or i >= 2:
                    pe.wait_ge(s_out_free, i - 1)
                pe.wait_ge(s_turn, i + 1)
                project(i, j, (lambda: turn(i + 1, 0)) if more else None)
            pairs(pe, T - 2, norm_project)
            norm_project(T - 2, 0)
            norm_project(T - 1, 1, False)

            def turn_row(w, low):
                if low:
                    pe.wait_ge(s_row, w + 1)
                    pe.wait_ge(s_coef_h, w + 1)
                else:
                    pe.wait_ge(s_row_h, w + 1)
                    wait(pe, s_coef, w)
                row, dt, idt = (row_l, BF16, identb) if low else (row_h, F16, ident16)
                for s in range(T):
                    to = bank[:, 6 + s // 5, :].bitcast(dt)[:, (s % 5) * P:(s % 5 + 1) * P]
                    last = pe.transpose(to, row[:, s * P:(s + 1) * P], idt[:, :])
                last.then_inc(s_rowt, 1)

            def gathered(i, j, between, late):
                cf = (coef_h[j], coef_l[j])
                tile_row(j, lambda k, a: cf[a][:, k, :], lambda k, b: hv[b][:, k, :], T, between, late)

            def gathered_counts(i, j, n_low, between, late):
                for half in range(2):
                    to, at = bank[:, 2 * j + half, :], slice(half * HALF, (half + 1) * HALF)
                    for k in range(T):
                        if half and k == T // 2 and late:
                            late()
                        pe.matmul(to, coef_h[j][:, k, :], h_h[:, k, at], start=k == 0, stop=False)
                        if k < T - 1:
                            pe.matmul(to, coef_h[j][:, k, :], h_l[:, k, at], start=False, stop=False)
                    for part in hv:
                        pe.matmul(to, ident16[:, :], part[:, ds(i), at], start=False, stop=False)
                    with pe.Fori(0, n_low) as k:
                        pe.matmul(to, coef_l[j][:, ds(k), :], h_h[:, ds(k), at], start=False, stop=False)
                    last = pe.matmul(to, coef_h[j][:, T - 1, :], h_l[:, T - 1, at], start=False, stop=True)
                    if not half and between:
                        between()
                last.then_inc(s_out, 1)

            def turn_before(i, base):
                if not (isinstance(i, int) and i == 0):
                    turn(i - 1, base)

            turn_row(0, False)
            turn_row(0, True)

            def gather0(i, j, more=True):
                if isinstance(i, int) and i < 2:
                    pe.wait_ge(s_out_free, T)
                else:
                    pe.wait_ge(s_upd, i - 1)
                pe.wait_ge(s_coef, i + 1)

                def late():
                    if more:
                        turn_row(i + 1, True)
                    turn_before(i, T)
                gathered_counts(i, j, n_low, (lambda: turn_row(i + 1, False)) if more else None, late)
            pe.wait_ge(s_lowb, 1)
            n_low = pe.value_load(low_blocks[0:1, 0:1], min_val=1, max_val=T)
            pairs(pe, T - 2, gather0)
            gather0(T - 2, 0)
            gather0(T - 1, 1, False)
            turn(T - 1, T)

            def up_unit(f, c, base, lhs, rhs, blocks, terms=((0, 0), (1, 0), (0, 1))):
                a, n = THIRD[c]
                if isinstance(f, int) and f == 0:
                    if base:
                        pe.wait_ge(s_up_free, base)
                else:
                    pe.wait_ge(s_up_free, f * 3 + (base + c - 2))
                product(bank[:, c, 0:n], lhs, lambda k, b: rhs(k, b, slice(a, a + n)), 0, blocks, blocks, terms).then_inc(s_up, 1)

            pe.wait_ge(s_turn, 2 * T)
            pe.wait_ge(s_upd, T)
            pe.wait_ge(s_w, PARTS["L0_ffn_Wm"])
            singles(pe, K, lambda f: [up_unit(f, c, 0, lambda k, a: wt[a][:, k, ds(f * P, P)],
                                              lambda k, b, cols: xT[b][:, k, cols], K) for c in range(3)])

            pe.wait_ge(s_up_free, 3 * K)
            pe.wait_ge(s_emb, 1)
            logits = bank[:, 4:7, :].rearrange("p a b -> p (a b)")

            def route(t):
                for head in range(K):
                    mm = product(logits[:, ds(t * P + head * 16, 16)], lambda k, a: hT[a][:, head, ds(t * P, P)],
                                 lambda k, b: emb[b][:, :], 0, 1, 1)
                mm.then_inc(s_logit, 1)
            singles(pe, T, route)

            pe.wait_ge(s_gate, 1)
            for t in range(T):
                mm = pe.transpose(bank[:, t // 4, (t % 4) * P:(t % 4 + 1) * P], gates[:, t, :], ident[:, :])
            mm.then_inc(s_gate_t, 1)

            def expert_out(s, b, j, third):
                n = THIRD[third][1]
                if j == 0:
                    wait(pe, s_comb, s - 1)
                pe.wait_ge(s_hid, s * K + (j + 1))
                product(bank[:, 6 + b, 0:n], lambda k, a: w2[a][:, k, :], lambda k, c: hid[b][c][:, k, 0:n], j, j + 1, K + 1)
                if j == K - 1:
                    product(bank[:, 6 + b, 0:n], lambda k, a: b2[a][:, :], lambda k, c: gm[third][c][:, 0:n], K, K + 1, K + 1).then_inc(s_comb_mm, 1)

            pe.wait_ge(s_w, PARTS["L0_ffn_W2"])
            pe.wait_ge(s_b2, 1)
            pe.wait_ge(s_gt, 1)

            def experts(hp, first=False):
                for jj in range(6):
                    s, b, c = hp * 6 + jj, jj % 2, jj % 3
                    head = hp * 2 + jj // 3
                    a, n = THIRD[c]
                    for j in range(K):
                        u = s * K + j
                        if not (first and jj == 0 and j < 2):
                            pe.wait_ge(s_gelu, u - 1)
                        product(bank[:, j % 2, 0:n], lambda k, p: w1[p][:, j * P:(j + 1) * P],
                                lambda k, p: hT[p][:, ds(head), a:a + n].rearrange("p a n -> p (a n)"), 0, 1, 1).then_inc(s_unit, 1)
                        if j == 0:
                            pe.wait_ge(s_gm, s + 1)
                        if not (first and jj == 0 and j < 2):
                            pe.wait_ge(s_gated, u - 1)
                        product(bank[:, 2 + j % 2, 0:n], lambda k, p: pick[:, j, :], lambda k, p: gm[c][p][:, 0:n],
                                0, 1, 1, ((0, 0), (0, 1))).then_inc(s_spread, 1)
                        if not (first and jj == 0):
                            expert_out(s - 1, 1 - b, j, (jj - 1) % 3)
            experts(0, True)
            with pe.Fori(1, K // 2) as hp:
                experts(hp)
            for j in range(K):
                expert_out(3 * K - 1, 1, j, 2)

            pe.wait_ge(s_w, PARTS["L0_ffn_Wo"])
            pe.wait_ge(s_comb, 3 * K)
            pe.wait_ge(s_gelu, 3 * K * K)
            pe.wait_ge(s_gated, 3 * K * K)

            def out0(i, j):
                if not isinstance(i, int) or i >= 2:
                    pe.wait_ge(s_upd, i + (T - 1))
                tile_row(j, lambda k, a: hT[a][:, k, ds(i * P, P)], lambda k, b: wt[b][:, k, :], K, None,
                         lambda: turn_before(i, 2 * T))
            pairs(pe, T, out0)
            turn(T - 1, 2 * T)

            pe.wait_ge(s_turn, 2 * T + 2)
            pe.wait_ge(s_upd, 2 * T)
            project_two(PARTS["L1_gnn_W"])
            pe.wait_ge(s_turn, 3 * T)

            def project1(i, j):
                pe.wait_ge(s_out_free, i + (T - 1))
                project(i, j)
            with pe.Fori(1, T // 2) as h:
                for j in range(2):
                    project1(h * 2 + j, j)

            pe.wait_ge(s_diag, 1)
            pe.wait_ge(s_turn, 3 * T)
            for c, (a, n) in enumerate(THIRD):
                mm = pe.matmul(bank[:, 4 + c, 0:n], ones[:, :], work[:, a:a + n], start=True, stop=True)
            mm.then_inc(s_al_row, 1)

            def gather1(i, j):
                if isinstance(i, int) and i < 2:
                    pe.wait_ge(s_out_free, 2 * T)
                    pe.wait_ge(s_al, 1)
                else:
                    pe.wait_ge(s_upd, i + (2 * T - 1))
                pe.wait_ge(s_coef, i + (T + 1))
                for k in range(T):
                    for p, cf in enumerate((coef_h[j], coef_l[j])):
                        pe.matmul(bank[:, 6 + j, 0:1], cf[:, k, :], one16[:, 0:1], start=(k == 0 and p == 0),
                                  stop=(k == T - 1 and p == 1))
                gathered(i, j, None, lambda: turn_before(i, 3 * T))
            pairs(pe, T, gather1)
            turn(T - 1, 3 * T)

            pe.wait_ge(s_turn, 4 * T)
            pe.wait_ge(s_upd, 3 * T)
            pe.wait_ge(s_w, PARTS["L1_ffn_w1"])

            def up1(f):
                for c in range(3):
                    if not isinstance(f, int):
                        pe.wait_ge(s_hid_l, f * 3 + (c - 2))
                    up_unit(f, c, 3 * K, lambda k, a: half_a[a][:, k, ds(f * P, P)], lambda k, b, cols: xT[b][:, k, cols], K)
            singles(pe, F // P, up1)
            pe.wait_ge(s_router1, 1)

            def route1(t):
                product(bank[:, 7, ds(t * 8, 8)], lambda k, a: xT[a][:, k, ds(t * P, P)], lambda k, b: router[b][:, k, :],
                        0, K, K).then_inc(s_logit, 1)
            singles(pe, T, route1)
            pe.wait_ge(s_w, PARTS["L1_ffn_w2"])
            pe.wait_ge(s_up_free, 3 * K + 3 * F // P)
            pe.wait_ge(s_hid_l, 3 * F // P)

            def out1(i, j):
                if not isinstance(i, int) or i >= 2:
                    pe.wait_ge(s_upd, i + (3 * T - 1))
                tile_row(j, lambda k, a: fT[a][:, k, ds(i * P, P)], lambda k, b: half_b[b][:, k, :], F // P, None,
                         lambda: turn_before(i, 4 * T))
            pairs(pe, T, out1)
            turn(T - 1, 4 * T)

            pe.wait_ge(s_wscale, 1)
            pe.matmul(bank[:, 7, 0:F], ones[:, :], work[:, 0:F], start=True, stop=True).then_inc(s_row2, 1)
            pe.wait_ge(s_turn, 4 * T + 2)
            pe.wait_ge(s_upd, 4 * T)
            project_two(PARTS["L2_gnn_W_b"])
            pe.wait_ge(s_turn, 5 * T)

            def project2(i, j):
                pe.wait_ge(s_out_free, i + (2 * T - 1))
                project(i, j)
            with pe.Fori(1, T // 2) as h:
                for j in range(2):
                    project2(h * 2 + j, j)

            def gather2(i, j):
                if isinstance(i, int) and i < 2:
                    pe.wait_ge(s_out_free, 3 * T)
                else:
                    pe.wait_ge(s_upd, i + (4 * T - 1))
                pe.wait_ge(s_coef, i + (2 * T + 1))
                gathered_counts(i, j, n_low, None, lambda: turn_before(i, 5 * T))
            pairs(pe, T, gather2)
            turn(T - 1, 5 * T)

            pe.wait_ge(s_w, PARTS["L2_ffn_W_in"])
            pe.wait_ge(s_upd, 5 * T)
            pe.wait_ge(s_up_free, 3 * K + 3 * F // P)
            for k in range(K):
                pe.wait_ge(s_q_l, k + 1)
                for c, (a, n) in enumerate(THIRD):
                    for b in range(2):
                        mm = pe.matmul(bank[:, c, 0:n], half_a[0][:, k, 0:P], hT[b][:, k, a:a + n], start=(k == 0 and b == 0),
                                       stop=(k == K - 1 and b == 1))
                    if k == K - 1:
                        mm.then_inc(s_up, 1)
            with pe.Fori(1, F // P) as f:
                for c in range(3):
                    up_unit(f, c, 3 * K + 3 * F // P, lambda k, a: half_a[0][:, k, ds(f * P, P)],
                            lambda k, b, cols: hT[b][:, k, cols], K, ((0, 0), (0, 1)))
            pe.wait_ge(s_w, PARTS["L2_ffn_W_out"])
            pe.wait_ge(s_up_free, 3 * K + 6 * F // P)
            for k in range(F // P):
                pe.wait_ge(s_hq_l, k + 1)
                for i in range(2):
                    for half in range(2):
                        for a in range(2):
                            mm = pe.matmul(bank[:, 2 * i + half, :], fT[a][:, k, i * P:(i + 1) * P], half_b[0][:, k, half * HALF:(half + 1) * HALF],
                                           start=(k == 0 and a == 0), stop=(k == F // P - 1 and a == 1))
                    if k == F // P - 1:
                        mm.then_inc(s_out, 1)

            def out2(i, j):
                pe.wait_ge(s_upd, i + (5 * T - 1))
                tile_row(j, lambda k, a: fT[a][:, k, ds(i * P, P)], lambda k, b: half_b[0][:, k, :], F // P, None,
                         lambda: turn(i - 1, 6 * T), ((0, 0), (1, 0)))
            pe.wait_ge(s_upd, 5 * T + 1)
            turn(0, 6 * T)
            with pe.Fori(1, T // 2) as h:
                for j in range(2):
                    out2(h * 2 + j, j)
            turn(T - 1, 6 * T)

            pe.wait_ge(s_w, PARTS["L3_gnn_W_down"])
            pe.wait_ge(s_turn, 7 * T)
            pe.wait_ge(s_upd, 6 * T)
            for f in range(2):
                for c in range(3):
                    up_unit(f, c, 3 * K + 6 * F // P, lambda k, a: down[a][:, k, ds(f * P, P)], lambda k, b, cols: xT[b][:, k, cols], K)
            pe.wait_ge(s_w, PARTS["L3_gnn_Wr"])
            pe.wait_ge(s_up_free, 3 * K + 6 * F // P + 6)

            def project3(i, j):
                if not isinstance(i, int) or i >= 2:
                    pe.wait_ge(s_xrh, i - 1)
                product(ps_out[j][:, 0:HALF], lambda k, a: xdT[a][:, k, ds(i * P, P)], lambda k, b: wlr[b][:, k, :], 0, 2, 2).then_inc(s_out, 1)
            pairs(pe, T, project3)
            pe.wait_ge(s_xr, T)
            pe.wait_ge(s_aux, 1)
            for credit in (s_dt, s_pick, s_spread3):
                pe.sem_inc(credit, 2)
            pe.wait_ge(s_att, 1)

            def nothing_more(*_):
                pass

            def scores(w, c, ch, cm):
                for b in range(2):
                    pe.wait_ge(s_dt, ch * 2 + (b + 3))
                    pe.wait_ge(s_got_free, ch * 2 + (b + 1))
                    for q in range(2):
                        pe.wait_ge(s_got[b][q], ch * 16 + 16)
                        for f in range(2):
                            to = bank[:, 4 + b, (2 * f + q) * EP:(2 * f + q + 1) * EP]
                            edges = by_dst[b][:, q * EP:(q + 1) * EP]
                            pe.matmul(to, xr_h[:, ds(w), f * P:(f + 1) * P], edges, start=True, stop=False)
                            pe.matmul(to, xr_l[:, ds(w), f * P:(f + 1) * P], edges, start=False, stop=False)
                            last = pe.matmul(to, xl_got[b][0:EP, q, f * P:(f + 1) * P], ident[0:EP, 0:EP], start=False, stop=True)
                        last.then_inc(s_pick if q else s_tile_free, 1)
                for b in range(2):
                    pe.wait_ge(s_got_free, ch * 2 + (b + 3))
                    pe.wait_ge(s_maxd, (cm + w) * 2 + (b + 1))
                    for q in range(2):
                        for f in range(2):
                            pe.matmul(bank[0:EP, 6 + b, 4 * q:4 * q + 4], zT[b][:, (2 * f + q) * EP:(2 * f + q + 1) * EP], att_cols[:, f, :],
                                      start=f == 0, stop=f == 1)
                    pe.wait_ge(s_lkb, cm * 2 + (b + 1))
                    for h in range(4):
                        last = pe.matmul(bank[:, 2 * b + h // 2, (h % 2) * 2 * EP:(h % 2 + 1) * 2 * EP], att_wide[:, h, :],
                                         zTb[b][:, h // 2 * 2 * EP:(h // 2 + 1) * 2 * EP], start=True, stop=True)
                    last.then_inc(s_spread3, 1)

            def open_sums(w, ch, cm, cs, last):
                pe.wait_ge(s_mk, w + 1)
                pe.matmul(bank[:, 0, 0:HID + 4], none16[0:EP, 0:P], none16[0:EP, :], start=True, stop=False)

            def scatter(w, c, ch, cs):
                for b in range(2):
                    pe.wait_ge(s_dt, ch * 2 + (b + 3))
                    pe.wait_ge(s_got_free, ch * 2 + (b + 1))
                    for q in range(2):
                        last = pe.matmul(bank[0:EP, 4 + b, q * 5:(q + 1) * 5], by_dst[b][:, q * EP:(q + 1) * EP], m_b, start=True, stop=True)
                    last.then_inc(s_pick, 1)
                    scatter_before(ch, b)

            def scatter_before(ch, b):
                pe.wait_ge(s_got_free, ch * 2 + (b + 1))
                for q in range(2):
                    last = pe.matmul(bank[:, 0, 0:HID + 4], to_dst[b][0:EP, q, :], z3[b][0:EP, q, :], start=False, stop=False)
                last.then_inc(s_scat, 1)

            def close(w, ch, cm, cs):
                for b in range(2):
                    scatter_before(ch, b)
                pe.matmul(bank[:, 0, 0:HID + 4], none16[0:EP, 0:P], none16[0:EP, :], start=False, stop=True).then_inc(s_agg, 1)
            over_windows(pe, nothing_more, scores, open_sums, scatter, close)

            pe.wait_ge(s_win, 5 * T + 2)
            for k in range(2):
                for t in range(T):
                    at = k * T + t
                    last = pe.transpose(bank[:, at // 4, (at % 4) * P:(at % 4 + 1) * P], sums[:, t, k * P:(k + 1) * P], ident[:, :])
            last.then_inc(s_aggt, 1)
            pe.wait_ge(s_w, PARTS["L3_gnn_W_up"])
            pe.wait_ge(s_aggl, 1)

            def out3(i, j):
                if not isinstance(i, int) or i >= 2:
                    pe.wait_ge(s_upd, i + (6 * T - 1))
                tile_row(j, lambda k, a: aggT[a][:, k, ds(i * P, P)], lambda k, b: w_upp[b][:, k, :], 2, None,
                         lambda: turn_before(i, 7 * T))
            pairs(pe, T, out3)
            turn(T - 1, 7 * T)

            pe.wait_ge(s_turn, 8 * T)
            pe.wait_ge(s_upd, 7 * T)
            pe.wait_ge(s_router1, 2)

            def route3(t):
                product(bank[:, 3, ds(t * 8, 8)], lambda k, a: xT[a][:, k, ds(t * P, P)], lambda k, b: router[b][:, k, :],
                        0, K, K).then_inc(s_logit, 1)
            singles(pe, T, route3)

            def hidden3(x3, j):
                pe.wait_ge(s_w, x3 * 12 + (PARTS["L3_gnn_W_up"] + K))
                for unit3 in range(U3):
                    f, c = unit3 // 3, unit3 % 3
                    a, n = THIRD[c]
                    if not isinstance(x3, int) or x3 or unit3 >= 2:
                        pe.wait_ge(s_h3, x3 * U3 + (unit3 - 1))
                    for to, at in ((4, 0), (6, HID)):
                        mm = product(bank[:, to + unit3 % 2, 0:n], lambda k, p: gu[j][p][:, k, at + f * P:at + (f + 1) * P],
                                     lambda k, p: xT[p][:, k, a:a + n], 0, K, K)
                    mm.then_inc(s_gu, 1)

            def out3x(x3, j):
                pe.wait_ge(s_w, x3 * 12 + (PARTS["L3_gnn_W_up"] + 12))
                pe.wait_ge(s_h3l, x3 * U3 + U3)
                pe.sem_inc(s_met, 1)

                def tile(i, b):
                    pe.wait_ge(s_upd, x3 * T + i + (7 * T - 1))
                    tile_row(b, lambda k, p: h3[j][p][:, k, ds(i * P, P)], lambda k, p: dn[j][p][:, k, :], 2)
                pairs(pe, T, tile, 0)
            hidden3(0, 0)
            hidden3(1, 1)
            pe.wait_ge(s_gates3, 1)
            out3x(0, 0)
            with pe.Fori(1, E3 // 2) as h:
                for j in range(2):
                    hidden3(h * 2 + j, j)
                    out3x(h * 2 + (j - 1), 1 - j)
            hidden3(E3, 0)
            out3x(E3 - 1, 1)
            out3x(E3, 0)



_INS = ['x', 'src', 'dst', 'dst_chunks', 'L0_gnn_W', 'L0_gnn_b', 'L0_ffn_Wm', 'L0_ffn_bm', 'L0_ffn_expert_emb', 'L0_ffn_W1', 'L0_ffn_b1',
        'L0_ffn_W2', 'L0_ffn_b2', 'L0_ffn_Wo', 'L0_ffn_bo', 'L1_gnn_W', 'L1_gnn_a', 'L1_ffn_router_w', 'L1_ffn_w1', 'L1_ffn_b1',
        'L1_ffn_w2', 'L1_ffn_b2', 'L2_ffn_b_in', 'L2_gnn_WT', 'L2_gnn_b', 'L2_ffn_W_in', 'L2_ffn_W_inT', 'L2_ffn_W_out', 'L2_ffn_b_out',
        'dst_row', 'L3_gnn_rms_w', 'L3_gnn_W_down', 'L3_gnn_Wl', 'L3_gnn_Wr', 'L3_gnn_att', 'L3_gnn_att_col', 'L3_gnn_W_up', 'L3_gu', 'L3_down',
        'L3_ffn_router_wT', 'L3_ffn_routing_bias']


def kernel(**inputs):
    import numpy as _np
    import concourse.bacc as _bacc
    from concourse import mybir as _mybir
    from concourse.bass_utils import run_bass_kernel_spmd as _run

    laid = {k: _np.ascontiguousarray(v) for k, v in inputs.items()}
    laid["dst_row"] = laid["dst"].reshape(1, EDGES)
    laid["L3_gnn_att_col"] = _np.ascontiguousarray(laid["L3_gnn_att"].reshape(2, P).T)
    laid["L3_gnn_att"] = laid["L3_gnn_att"].reshape(1, HID)
    laid["dst_chunks"] = laid["dst"].reshape(NC, EDGES // NC)
    for name in ("src", "dst"):
        laid[name] = _np.ascontiguousarray(laid[name].reshape(ET, EP).T)
    laid["L0_ffn_W1"] = _np.ascontiguousarray(laid["L0_ffn_W1"].transpose(1, 0, 2).reshape(P, DIM))
    laid["L0_ffn_W2"] = laid["L0_ffn_W2"].reshape(DIM, P)
    laid["L2_gnn_WT"] = _np.ascontiguousarray(laid["L2_gnn_W"].T)
    laid["L2_ffn_W_inT"] = _np.ascontiguousarray(laid["L2_ffn_W_in"].T)
    gate = _np.concatenate([laid["L3_ffn_wg"], laid["L3_ffn_sg_w"][None]]).transpose(0, 2, 1)
    up = _np.concatenate([laid["L3_ffn_wu"], laid["L3_ffn_su_w"][None]]).transpose(0, 2, 1)
    laid["L3_gu"] = _np.ascontiguousarray(_np.concatenate([gate, up], axis=2).reshape(-1, 2 * HID))
    down = _np.concatenate([laid["L3_ffn_wd"], laid["L3_ffn_sd_w"][None]]).transpose(0, 2, 1)
    laid["L3_down"] = _np.ascontiguousarray(down.reshape(-1, DIM))
    laid["L3_ffn_router_wT"] = _np.ascontiguousarray(laid["L3_ffn_router_w"].T)
    for name in ("L0_ffn_bm", "L0_ffn_b1", "L1_ffn_b1", "L2_ffn_b_in", "L3_gnn_rms_w"):
        laid[name] = _np.ascontiguousarray(laid[name].reshape(-1, P).T)
    nc = _bacc.Bacc("TRN2", target_bir_lowering=False, num_devices=1)
    arrays, args = {}, {}
    for name in _INS:
        a = laid[name]
        arrays[f"in_{name}_dram"] = a
        args[name] = nc.dram_tensor(f"in_{name}_dram", a.shape, _mybir.dt.from_np(a.dtype), kind="ExternalInput").ap()
    out = nc.dram_tensor("out_0_dram", (NODES, DIM), _mybir.dt.float32, kind="ExternalOutput").ap()
    program(nc, args, out)
    r = _run(nc, [arrays], core_ids=[0])
    return r.results[0]["out_0_dram"]
```
